# Optimizing a Trainium2 kernel written in Bass

```python
import numpy as np
import jax
import jax.numpy as jnp

def _softmax(x, axis=-1):
    return jax.nn.softmax(x, axis=axis)

def _gelu(x):
    return jax.nn.gelu(x, approximate=True)

def _silu(x):
    return jax.nn.silu(x)

def _sigmoid(x):
    return jax.nn.sigmoid(x)

def _layernorm(x, axis=-1, eps=1e-05):
    m = jnp.mean(x, axis=axis, keepdims=True)
    v = jnp.var(x, axis=axis, keepdims=True)
    return (x - m) / jnp.sqrt(v + eps)

def _scatter_add(tgt, idx, src, axis=0):
    return tgt.at[idx].add(src)

def _segment_sum(src, seg, n):
    return jax.ops.segment_sum(src, seg, n)
kernel_name = 'mk_prb_d4_jaxref_r8_068145'

def setup_inputs(seed: int=0):
    np.random.seed(seed)
    _w = jnp.asarray

    def _L0_attn_setup():
        import jax, jax.numpy as jnp
        import numpy as np
        import math
        D_MODEL = 128
        N_HEADS = 16
        SPARSITY = 0.3
        key = jax.random.key(seed)
        ks = jax.random.split(key, 12)
        B, S, D = (4, 256, D_MODEL)
        Dh = D // 2
        sc = 0.02
        inp = {'x': jax.random.normal(ks[0], (B, S, D), dtype=jnp.float32), 'wq': jax.random.normal(ks[1], (D, D), dtype=jnp.float32) * sc, 'bq': jnp.zeros((D,), jnp.float32), 'wk': jax.random.normal(ks[2], (D, D), dtype=jnp.float32) * sc, 'bk': jnp.zeros((D,), jnp.float32), 'wv': jax.random.normal(ks[3], (D, D), dtype=jnp.float32) * sc, 'bv': jnp.zeros((D,), jnp.float32), 'wo': jax.random.normal(ks[4], (D, D), dtype=jnp.float32) * sc, 'bo': jnp.zeros((D,), jnp.float32), 'wi1': jax.random.normal(ks[5], (Dh, D), dtype=jnp.float32) * sc, 'bi1': jnp.zeros((Dh,), jnp.float32), 'wi2': jax.random.normal(ks[6], (1, Dh), dtype=jnp.float32) * sc, 'bi2': jnp.zeros((1,), jnp.float32)}
        return inp
    _L0_attn_in = _L0_attn_setup()

    def _L0_ffn_setup():
        import jax, jax.numpy as jnp
        import numpy as np
        NUM_EXPERTS = 8
        CAPACITY = 512
        key = jax.random.key(seed)
        ks = jax.random.split(key, 5)
        dim, hidden = (128, 256)
        x = jax.random.normal(ks[0], (4, 512, dim), dtype=jnp.float32)
        wg = jax.random.normal(ks[1], (dim, NUM_EXPERTS), dtype=jnp.float32) * 0.02
        w1 = jax.random.normal(ks[2], (NUM_EXPERTS, dim, hidden), dtype=jnp.float32) * 0.02
        w3 = jax.random.normal(ks[3], (NUM_EXPERTS, dim, hidden), dtype=jnp.float32) * 0.02
        w2 = jax.random.normal(ks[4], (NUM_EXPERTS, hidden, dim), dtype=jnp.float32) * 0.02
        return {'x': x, 'wg': wg, 'w1': w1, 'w3': w3, 'w2': w2}
    _L0_ffn_in = _L0_ffn_setup()

    def _L1_attn_setup():
        import jax, jax.numpy as jnp
        import numpy as np
        import math
        DIM = 128
        HEADS = 16
        HEAD_DIM = 64
        WINDOW = 32
        GLOBAL = 64
        B, S = (1, 512)

        def _sparse_mask(seq_len, window, global_tokens):
            i = jnp.arange(seq_len)[:, None]
            j = jnp.arange(seq_len)[None, :]
            half = window // 2
            local = (j >= i - half) & (j <= i + half)
            glob = (j < global_tokens) | (i < global_tokens)
            causal = j <= i
            return ((local | glob) & causal)[None, None, :, :]
        key = jax.random.key(seed)
        k1, k2, k3 = jax.random.split(key, 3)
        x = jax.random.normal(k1, (B, S, DIM), dtype=jnp.float32)
        w_qkv = jax.random.normal(k2, (DIM, 3 * HEADS * HEAD_DIM), dtype=jnp.float32) * (1.0 / math.sqrt(DIM))
        w_out = jax.random.normal(k3, (HEADS * HEAD_DIM, DIM), dtype=jnp.float32) * (1.0 / math.sqrt(HEADS * HEAD_DIM))
        return {'x': x, 'w_qkv': w_qkv, 'w_out': w_out}
    _L1_attn_in = _L1_attn_setup()

    def _L1_ffn_setup():
        import jax, jax.numpy as jnp
        import numpy as np
        DIM = 128
        NUM_EXPERTS = 8
        TOP_K = 2
        HIDDEN = 4 * DIM // TOP_K
        BS, SLEN = (1, 256)

        def _moe(x, gate_w, w_up, w_down, expert_bias):
            bs, slen, dim = x.shape
            xf = x.reshape(-1, dim)
            scores = jax.nn.sigmoid(xf @ gate_w.T)
            biased = scores + expert_bias
            _, sel = jax.lax.top_k(biased, TOP_K)
            top_scores = jnp.take_along_axis(scores, sel, axis=-1)

            def body(acc, ew):
                e, wu, wd = ew
                w_t = jnp.sum(jnp.where(sel == e, top_scores, 0.0), axis=-1)
                xe = xf * w_t[:, None]
                h = jnp.square(jax.nn.relu(xe @ wu.T))
                return (acc + h @ wd.T, None)
            out0 = jnp.zeros_like(xf)
            out, _ = jax.lax.scan(body, out0, (jnp.arange(NUM_EXPERTS), w_up, w_down))
            return out.reshape(bs, slen, dim)
        key = jax.random.key(seed)
        k0, k1, k2, k3 = jax.random.split(key, 4)
        x = jax.random.normal(k0, (BS, SLEN, DIM), dtype=jnp.float32)
        gate_w = jax.random.normal(k1, (NUM_EXPERTS, DIM), dtype=jnp.float32) * 0.02
        w_up = jax.random.normal(k2, (NUM_EXPERTS, HIDDEN, DIM), dtype=jnp.float32) * 0.02
        w_down = jax.random.normal(k3, (NUM_EXPERTS, DIM, HIDDEN), dtype=jnp.float32) * 0.02
        expert_bias = jnp.zeros((NUM_EXPERTS,), dtype=jnp.float32)
        return {'x': x, 'gate_w': gate_w, 'w_up': w_up, 'w_down': w_down, 'expert_bias': expert_bias}
    _L1_ffn_in = _L1_ffn_setup()

    def _L2_attn_setup():
        import jax, jax.numpy as jnp
        import numpy as np
        B, L, D = (8, 256, 128)
        LEARNED = 32
        WINDOWS = (32.0, 64.0, 128.0, 256.0)

        def _forward(x, Wq, Wk, Wv, Wqkv, bqkv, Wop, W2, b2):
            dt = x.dtype
            Bs, Ls, Ds = x.shape
            windows = jnp.asarray(WINDOWS, dt)
            G = windows.shape[0]
            dh = Ds // G
            BIG = jnp.asarray(1e+18, dt)
            q_in = x @ Wq.T
            _k_unused = x @ Wk.T
            _v_unused = x @ Wv.T
            qkv = (q_in @ Wqkv.T + bqkv).reshape(Bs, Ls, 3, Ds)
            q = qkv[:, :, 0].reshape(Bs, Ls, G, dh)
            k = qkv[:, :, 1].reshape(Bs, Ls, G, dh)
            v = qkv[:, :, 2].reshape(Bs, Ls, G, dh)
            scale = jnp.asarray(1.0 / np.sqrt(Ls), dt)
            scores = jnp.einsum('blgd,bmgd->bglm', q, k) * scale
            h = jax.nn.relu(q_in) @ Wop.T
            dx = jax.nn.sigmoid(h @ W2.T + b2) * Ls
            dx_g = dx[:, None, :, :] + windows[None, :, None, None]
            idx = jnp.arange(Ls)
            dist = jnp.abs(idx[:, None] - idx[None, :]).astype(dt)
            win_mask = jnp.where(idx[None, :] < idx[:, None], BIG, dist)
            masked = jnp.where(win_mask[None, None] > dx_g, -BIG, scores)
            s2 = masked + scores
            attn = jax.nn.softmax(s2, axis=-1)
            out = jnp.einsum('bglm,bmgd->blgd', attn, v).reshape(Bs, Ls, Ds)
            return out
        key = jax.random.key(seed)
        ks = jax.random.split(key, 9)
        s = 0.02
        return {'x': jax.random.normal(ks[0], (B, L, D), jnp.float32), 'Wq': jax.random.normal(ks[1], (D, D), jnp.float32) * s, 'Wk': jax.random.normal(ks[2], (D, D), jnp.float32) * s, 'Wv': jax.random.normal(ks[3], (D, D), jnp.float32) * s, 'Wqkv': jax.random.normal(ks[4], (3 * D, D), jnp.float32) * s, 'bqkv': jnp.zeros((3 * D,), jnp.float32), 'Wop': jax.random.normal(ks[5], (LEARNED, D), jnp.float32) * s, 'W2': jax.random.normal(ks[6], (1, LEARNED), jnp.float32) * s, 'b2': jnp.zeros((1,), jnp.float32)}
    _L2_attn_in = _L2_attn_setup()

    def _L2_ffn_setup():
        import jax, jax.numpy as jnp
        import numpy as np
        D_IN, D_HID = (128, 512)

        def _ternary(key, shape):
            return jax.random.randint(key, shape, -1, 2).astype(jnp.float32)

        def _tlin(x, w, s):
            return jnp.einsum('bsi,oi->bso', x, w) * s
        key = jax.random.key(seed)
        ks = jax.random.split(key, 12)
        inv = lambda fan: 1.0 / np.sqrt(fan).astype(np.float32)
        return {'x': jax.random.normal(ks[0], (4, 256, D_IN), dtype=jnp.float32), 'w1_w': _ternary(ks[1], (D_HID, D_IN)), 'w1_s': jax.random.uniform(ks[2], (D_HID,), dtype=jnp.float32) * inv(D_IN), 'w2_w': _ternary(ks[3], (D_HID, D_IN)), 'w2_s': jax.random.uniform(ks[4], (D_HID,), dtype=jnp.float32) * inv(D_IN), 'h1_w': _ternary(ks[5], (D_HID, D_HID)), 'h1_s': jax.random.uniform(ks[6], (D_HID,), dtype=jnp.float32) * inv(D_HID), 'h2_w': _ternary(ks[7], (D_HID, D_HID)), 'h2_s': jax.random.uniform(ks[8], (D_HID,), dtype=jnp.float32) * inv(D_HID), 'w3_w': _ternary(ks[9], (D_IN, D_HID)), 'w3_s': jax.random.uniform(ks[10], (D_IN,), dtype=jnp.float32) * inv(D_HID)}
    _L2_ffn_in = _L2_ffn_setup()

    def _L3_attn_setup():
        import jax, jax.numpy as jnp
        import numpy as np
        DIM = 128
        HEADS = 16
        HEAD_DIM = 64
        key = jax.random.key(seed)
        ks = jax.random.split(key, 6)
        inner = HEADS * HEAD_DIM
        s = 0.02
        return {'x': jax.random.normal(ks[0], (2, 256, DIM), dtype=jnp.float32), 'Wq': jax.random.normal(ks[1], (DIM, inner), dtype=jnp.float32) * s, 'Wk': jax.random.normal(ks[2], (DIM, inner), dtype=jnp.float32) * s, 'Wv': jax.random.normal(ks[3], (DIM, inner), dtype=jnp.float32) * s, 'Wo': jax.random.normal(ks[4], (inner, DIM), dtype=jnp.float32) * s, 'bo': jax.random.normal(ks[5], (DIM,), dtype=jnp.float32) * s}
    _L3_attn_in = _L3_attn_setup()

    def _L3_ffn_setup():
        import jax, jax.numpy as jnp
        import numpy as np
        INT4_QMAX = 7.0

        def simulate_quantize_int4(w):
            scale = jnp.max(jnp.abs(w)) / INT4_QMAX
            q = jnp.clip(jnp.round(w / scale), -8.0, 7.0)
            return q * scale
        key = jax.random.key(seed)
        k_x, k_w, k_bias, k_a, k_b = jax.random.split(key, 5)
        d_in, features, rank = (128, 128, 16)
        x = jax.random.normal(k_x, (4, 1024, d_in), dtype=jnp.float32)
        kernel = jax.random.normal(k_w, (d_in, features), dtype=jnp.float32)
        bias = jax.random.normal(k_bias, (features,), dtype=jnp.float32)
        a = jax.random.normal(k_a, (d_in, rank), dtype=jnp.float32) * (1.0 / np.sqrt(d_in))
        b = jax.random.normal(k_b, (rank, features), dtype=jnp.float32) * 0.01
        return {'x': x, 'kernel': kernel, 'bias': bias, 'a': a, 'b': b}
    _L3_ffn_in = _L3_ffn_setup()
    _d = {'L0_attn_x': _L0_attn_in['x'], 'L0_attn_wq': _L0_attn_in['wq'], 'L0_attn_bq': _L0_attn_in['bq'], 'L0_attn_wk': _L0_attn_in['wk'], 'L0_attn_bk': _L0_attn_in['bk'], 'L0_attn_wv': _L0_attn_in['wv'], 'L0_attn_bv': _L0_attn_in['bv'], 'L0_attn_wo': _L0_attn_in['wo'], 'L0_attn_bo': _L0_attn_in['bo'], 'L0_attn_wi1': _L0_attn_in['wi1'], 'L0_attn_bi1': _L0_attn_in['bi1'], 'L0_attn_wi2': _L0_attn_in['wi2'], 'L0_attn_bi2': _L0_attn_in['bi2'], 'L0_ffn_wg': _L0_ffn_in['wg'], 'L0_ffn_w1': _L0_ffn_in['w1'], 'L0_ffn_w3': _L0_ffn_in['w3'], 'L0_ffn_w2': _L0_ffn_in['w2'], 'L1_attn_w_qkv': _L1_attn_in['w_qkv'], 'L1_attn_w_out': _L1_attn_in['w_out'], 'L1_ffn_gate_w': _L1_ffn_in['gate_w'], 'L1_ffn_w_up': _L1_ffn_in['w_up'], 'L1_ffn_w_down': _L1_ffn_in['w_down'], 'L1_ffn_expert_bias': _L1_ffn_in['expert_bias'], 'L2_attn_Wq': _L2_attn_in['Wq'], 'L2_attn_Wk': _L2_attn_in['Wk'], 'L2_attn_Wv': _L2_attn_in['Wv'], 'L2_attn_Wqkv': _L2_attn_in['Wqkv'], 'L2_attn_bqkv': _L2_attn_in['bqkv'], 'L2_attn_Wop': _L2_attn_in['Wop'], 'L2_attn_W2': _L2_attn_in['W2'], 'L2_attn_b2': _L2_attn_in['b2'], 'L2_ffn_w1_w': _L2_ffn_in['w1_w'], 'L2_ffn_w1_s': _L2_ffn_in['w1_s'], 'L2_ffn_w2_w': _L2_ffn_in['w2_w'], 'L2_ffn_w2_s': _L2_ffn_in['w2_s'], 'L2_ffn_h1_w': _L2_ffn_in['h1_w'], 'L2_ffn_h1_s': _L2_ffn_in['h1_s'], 'L2_ffn_h2_w': _L2_ffn_in['h2_w'], 'L2_ffn_h2_s': _L2_ffn_in['h2_s'], 'L2_ffn_w3_w': _L2_ffn_in['w3_w'], 'L2_ffn_w3_s': _L2_ffn_in['w3_s'], 'L3_attn_Wq': _L3_attn_in['Wq'], 'L3_attn_Wk': _L3_attn_in['Wk'], 'L3_attn_Wv': _L3_attn_in['Wv'], 'L3_attn_Wo': _L3_attn_in['Wo'], 'L3_attn_bo': _L3_attn_in['bo'], 'L3_ffn_kernel': _L3_ffn_in['kernel'], 'L3_ffn_bias': _L3_ffn_in['bias'], 'L3_ffn_a': _L3_ffn_in['a'], 'L3_ffn_b': _L3_ffn_in['b']}
    _x0 = _d['L0_attn_x']
    _d['L0_attn_x'] = jax.random.normal(jax.random.fold_in(jax.random.key(seed), 1), (16, 256, 128), dtype=_x0.dtype)
    del _x0
    return _d

def reference(L0_attn_x, L0_attn_wq, L0_attn_bq, L0_attn_wk, L0_attn_bk, L0_attn_wv, L0_attn_bv, L0_attn_wo, L0_attn_bo, L0_attn_wi1, L0_attn_bi1, L0_attn_wi2, L0_attn_bi2, L0_ffn_wg, L0_ffn_w1, L0_ffn_w3, L0_ffn_w2, L1_attn_w_qkv, L1_attn_w_out, L1_ffn_gate_w, L1_ffn_w_up, L1_ffn_w_down, L1_ffn_expert_bias, L2_attn_Wq, L2_attn_Wk, L2_attn_Wv, L2_attn_Wqkv, L2_attn_bqkv, L2_attn_Wop, L2_attn_W2, L2_attn_b2, L2_ffn_w1_w, L2_ffn_w1_s, L2_ffn_w2_w, L2_ffn_w2_s, L2_ffn_h1_w, L2_ffn_h1_s, L2_ffn_h2_w, L2_ffn_h2_s, L2_ffn_w3_w, L2_ffn_w3_s, L3_attn_Wq, L3_attn_Wk, L3_attn_Wv, L3_attn_Wo, L3_attn_bo, L3_ffn_kernel, L3_ffn_bias, L3_ffn_a, L3_ffn_b):

    def _L0_attn_ref(x, wq, bq, wk, bk, wv, bv, wo, bo, wi1, bi1, wi2, bi2):
        import jax, jax.numpy as jnp
        import numpy as np
        import math
        D_MODEL = 128
        N_HEADS = 16
        SPARSITY = 0.3
        B, S, D = x.shape
        H = N_HEADS
        hd = D // H
        k = max(1, int(S * SPARSITY))
        Q = (x @ wq.T + bq).reshape(B, S, H, hd).transpose(0, 2, 1, 3)
        K = (x @ wk.T + bk).reshape(B, S, H, hd).transpose(0, 2, 1, 3)
        V = (x @ wv.T + bv).reshape(B, S, H, hd).transpose(0, 2, 1, 3)
        h = jnp.maximum(x @ wi1.T + bi1, 0.0)
        importance = (h @ wi2.T + bi2)[..., 0]
        _, top_idx = jax.lax.top_k(importance, k)
        sparse_mask = jnp.zeros((B, S), dtype=x.dtype).at[jnp.arange(B)[:, None], top_idx].set(1.0)
        scores = jnp.einsum('bhqd,bhkd->bhqk', Q, K) / math.sqrt(hd)
        scores = jnp.where(sparse_mask[:, None, None, :] == 0, -jnp.inf, scores)
        attn = jax.nn.softmax(scores, axis=-1)
        out = jnp.einsum('bhqk,bhkd->bhqd', attn, V)
        out = out.transpose(0, 2, 1, 3).reshape(B, S, D)
        return out @ wo.T + bo

    def _L0_ffn_ref(x, wg, w1, w3, w2):
        import jax, jax.numpy as jnp
        import numpy as np
        NUM_EXPERTS = 8
        CAPACITY = 512
        bz, slen, dim = x.shape
        xt = x.reshape(bz * slen, dim)
        scores = jax.nn.softmax(xt @ wg, axis=-1)
        top_scores, sel = jax.lax.top_k(scores.T, CAPACITY)
        token_idx = sel.reshape(-1)
        routed = xt[token_idx] * top_scores.reshape(-1, 1)
        routed = routed.reshape(NUM_EXPERTS, CAPACITY, dim)
        h = jax.nn.silu(jnp.einsum('ecd,edh->ech', routed, w1)) * jnp.einsum('ecd,edh->ech', routed, w3)
        routed_out = jnp.einsum('ech,ehd->ecd', h, w2).reshape(-1, dim)
        out = jnp.zeros_like(xt).at[token_idx].add(routed_out)
        return out.reshape(bz, slen, dim)

    def _L1_attn_ref(x, w_qkv, w_out):
        import jax, jax.numpy as jnp
        import numpy as np
        import math
        DIM = 128
        HEADS = 16
        HEAD_DIM = 64
        WINDOW = 32
        GLOBAL = 64
        B, S = (1, 512)

        def _sparse_mask(seq_len, window, global_tokens):
            i = jnp.arange(seq_len)[:, None]
            j = jnp.arange(seq_len)[None, :]
            half = window // 2
            local = (j >= i - half) & (j <= i + half)
            glob = (j < global_tokens) | (i < global_tokens)
            causal = j <= i
            return ((local | glob) & causal)[None, None, :, :]
        b, s, _ = x.shape
        scale = 1.0 / math.sqrt(HEAD_DIM)
        qkv = x @ w_qkv
        qkv = qkv.reshape(b, s, 3, HEADS, HEAD_DIM)
        q, k, v = jnp.transpose(qkv, (2, 0, 3, 1, 4))
        mask = _sparse_mask(s, WINDOW, GLOBAL)
        scores = jnp.einsum('bhid,bhjd->bhij', q, k) * scale
        scores = jnp.where(mask, scores, -jnp.inf)
        attn = jax.nn.softmax(scores, axis=-1)
        out = jnp.einsum('bhij,bhjd->bhid', attn, v)
        out = jnp.transpose(out, (0, 2, 1, 3)).reshape(b, s, HEADS * HEAD_DIM)
        return out @ w_out

    def _L1_ffn_ref(x, gate_w, w_up, w_down, expert_bias):
        import jax, jax.numpy as jnp
        import numpy as np
        DIM = 128
        NUM_EXPERTS = 8
        TOP_K = 2
        HIDDEN = 4 * DIM // TOP_K
        BS, SLEN = (1, 256)

        def _moe(x, gate_w, w_up, w_down, expert_bias):
            bs, slen, dim = x.shape
            xf = x.reshape(-1, dim)
            scores = jax.nn.sigmoid(xf @ gate_w.T)
            biased = scores + expert_bias
            _, sel = jax.lax.top_k(biased, TOP_K)
            top_scores = jnp.take_along_axis(scores, sel, axis=-1)

            def body(acc, ew):
                e, wu, wd = ew
                w_t = jnp.sum(jnp.where(sel == e, top_scores, 0.0), axis=-1)
                xe = xf * w_t[:, None]
                h = jnp.square(jax.nn.relu(xe @ wu.T))
                return (acc + h @ wd.T, None)
            out0 = jnp.zeros_like(xf)
            out, _ = jax.lax.scan(body, out0, (jnp.arange(NUM_EXPERTS), w_up, w_down))
            return out.reshape(bs, slen, dim)
        return _moe(x, gate_w, w_up, w_down, expert_bias)

    def _L2_attn_ref(x, Wq, Wk, Wv, Wqkv, bqkv, Wop, W2, b2):
        import jax, jax.numpy as jnp
        import numpy as np
        B, L, D = (8, 256, 128)
        LEARNED = 32
        WINDOWS = (32.0, 64.0, 128.0, 256.0)

        def _forward(x, Wq, Wk, Wv, Wqkv, bqkv, Wop, W2, b2):
            dt = x.dtype
            Bs, Ls, Ds = x.shape
            windows = jnp.asarray(WINDOWS, dt)
            G = windows.shape[0]
            dh = Ds // G
            BIG = jnp.asarray(1e+18, dt)
            q_in = x @ Wq.T
            _k_unused = x @ Wk.T
            _v_unused = x @ Wv.T
            qkv = (q_in @ Wqkv.T + bqkv).reshape(Bs, Ls, 3, Ds)
            q = qkv[:, :, 0].reshape(Bs, Ls, G, dh)
            k = qkv[:, :, 1].reshape(Bs, Ls, G, dh)
            v = qkv[:, :, 2].reshape(Bs, Ls, G, dh)
            scale = jnp.asarray(1.0 / np.sqrt(Ls), dt)
            scores = jnp.einsum('blgd,bmgd->bglm', q, k) * scale
            h = jax.nn.relu(q_in) @ Wop.T
            dx = jax.nn.sigmoid(h @ W2.T + b2) * Ls
            dx_g = dx[:, None, :, :] + windows[None, :, None, None]
            idx = jnp.arange(Ls)
            dist = jnp.abs(idx[:, None] - idx[None, :]).astype(dt)
            win_mask = jnp.where(idx[None, :] < idx[:, None], BIG, dist)
            masked = jnp.where(win_mask[None, None] > dx_g, -BIG, scores)
            s2 = masked + scores
            attn = jax.nn.softmax(s2, axis=-1)
            out = jnp.einsum('bglm,bmgd->blgd', attn, v).reshape(Bs, Ls, Ds)
            return out
        return _forward(x, Wq, Wk, Wv, Wqkv, bqkv, Wop, W2, b2)

    def _L2_ffn_ref(x, w1_w, w1_s, w2_w, w2_s, h1_w, h1_s, h2_w, h2_s, w3_w, w3_s):
        import jax, jax.numpy as jnp
        import numpy as np
        D_IN, D_HID = (128, 512)

        def _ternary(key, shape):
            return jax.random.randint(key, shape, -1, 2).astype(jnp.float32)

        def _tlin(x, w, s):
            return jnp.einsum('bsi,oi->bso', x, w) * s
        h = jax.nn.silu(_tlin(x, w1_w, w1_s)) * _tlin(x, w2_w, w2_s)
        h = jax.nn.gelu(_tlin(h, h1_w, h1_s), approximate=False)
        h = jax.nn.gelu(_tlin(h, h2_w, h2_s), approximate=False)
        return _tlin(h, w3_w, w3_s)

    def _L3_attn_ref(x, Wq, Wk, Wv, Wo, bo):
        import jax, jax.numpy as jnp
        import numpy as np
        DIM = 128
        HEADS = 16
        HEAD_DIM = 64
        N, S, _ = x.shape
        scale = 1.0 / np.sqrt(HEAD_DIM).astype(np.float32)
        q = (x @ Wq).reshape(N, S, HEADS, HEAD_DIM).transpose(0, 2, 1, 3)
        k = (x @ Wk).reshape(N, S, HEADS, HEAD_DIM).transpose(0, 2, 1, 3)
        v = (x @ Wv).reshape(N, S, HEADS, HEAD_DIM).transpose(0, 2, 1, 3)
        logits = jnp.einsum('nhid,nhjd->nhij', q, k) * scale
        causal = 1000000000.0 * (jnp.tril(jnp.ones((S, S), dtype=logits.dtype)) - 1.0)
        logits = logits + causal[None, None, :, :]
        attn = jax.nn.softmax(logits, axis=-1)
        out = jnp.einsum('nhij,nhjd->nhid', attn, v)
        out = out.transpose(0, 2, 1, 3).reshape(N, S, HEADS * HEAD_DIM)
        return out @ Wo + bo

    def _L3_ffn_ref(x, kernel, bias, a, b):
        import jax, jax.numpy as jnp
        import numpy as np
        INT4_QMAX = 7.0

        def simulate_quantize_int4(w):
            scale = jnp.max(jnp.abs(w)) / INT4_QMAX
            q = jnp.clip(jnp.round(w / scale), -8.0, 7.0)
            return q * scale
        w = simulate_quantize_int4(kernel)
        y = jnp.einsum('bsd,df->bsf', x, w) + bias
        lora = jnp.einsum('bsr,rf->bsf', jnp.einsum('bsd,dr->bsr', x, a), b)
        return y + lora
    x = L0_attn_x
    xn = _layernorm(x, axis=-1)
    x = x + _L0_attn_ref(xn, L0_attn_wq, L0_attn_bq, L0_attn_wk, L0_attn_bk, L0_attn_wv, L0_attn_bv, L0_attn_wo, L0_attn_bo, L0_attn_wi1, L0_attn_bi1, L0_attn_wi2, L0_attn_bi2) + _L0_ffn_ref(xn, L0_ffn_wg, L0_ffn_w1, L0_ffn_w3, L0_ffn_w2)
    xn = _layernorm(x, axis=-1)
    x = x + _L1_attn_ref(xn, L1_attn_w_qkv, L1_attn_w_out) + _L1_ffn_ref(xn, L1_ffn_gate_w, L1_ffn_w_up, L1_ffn_w_down, L1_ffn_expert_bias)
    xn = _layernorm(x, axis=-1)
    x = x + _L2_attn_ref(xn, L2_attn_Wq, L2_attn_Wk, L2_attn_Wv, L2_attn_Wqkv, L2_attn_bqkv, L2_attn_Wop, L2_attn_W2, L2_attn_b2) + _L2_ffn_ref(xn, L2_ffn_w1_w, L2_ffn_w1_s, L2_ffn_w2_w, L2_ffn_w2_s, L2_ffn_h1_w, L2_ffn_h1_s, L2_ffn_h2_w, L2_ffn_h2_s, L2_ffn_w3_w, L2_ffn_w3_s)
    xn = _layernorm(x, axis=-1)
    x = x + _L3_attn_ref(xn, L3_attn_Wq, L3_attn_Wk, L3_attn_Wv, L3_attn_Wo, L3_attn_bo) + _L3_ffn_ref(xn, L3_ffn_kernel, L3_ffn_bias, L3_ffn_a, L3_ffn_b)
    return x

_drawn_inputs = setup_inputs


def setup_inputs(seed=0):
    import zlib

    import numpy as np

    out = dict(_drawn_inputs(seed))
    spreads = {'L0_attn_bq': (0.0, 0.1),
     'L0_attn_bk': (0.0, 0.1),
     'L0_attn_bv': (0.0, 0.1),
     'L0_attn_bo': (0.0, 0.1),
     'L0_attn_bi1': (0.0, 0.1),
     'L1_ffn_expert_bias': (0.0, 0.1),
     'L2_attn_bqkv': (0.0, 0.1)}
    factors = {}
    for name, (base, spread) in spreads.items():
        noise = np.random.default_rng([zlib.crc32(name.encode()), seed]).standard_normal(out[name].shape)
        drawn = base * np.exp(spread * noise) if base else spread * noise
        out[name] = jnp.asarray(drawn.astype(out[name].dtype))
    for name, factor in factors.items():
        out[name] = (out[name] * factor).astype(out[name].dtype)
    return out
```

```python
import numpy as np

import concourse.bass as bass
from concourse import mybir
from contextlib import ExitStack

B, S, D = 16, 256, 128
TILES = B * S // 128
PASSES = B // 2
H0, HD0 = 16, 8
KEEP = int(S * 0.3)
KPAD = 80
HCH = H0 * KPAD // 128
E0, CAP, HID0 = 8, 512, 256
ROW = D + E0
HEADS, HD = 16, 64
E1, HID1 = 8, 256
G2, DH2 = 4, 32
WINDOWS = (32.0, 64.0, 128.0, 256.0)
HID2 = 512
C2 = HID2 // 128
EPS = 1e-5
MASKED = -1e30
FAR = 1e18

PACKS = {
    "const": [("ident", 128), ("blockones", 128), ("lowerblk", 128), ("dist", 256), ("iota", 128),
              ("tileno", 256), ("pidx", 1), ("tri", 512), ("headmask", H0), ("vmask", HCH * 128), ("tri8", 64), ("win", G2)],
    "l0": [("wqT", 128), ("wkT", 128), ("wvT", 128), ("woT", 128), ("wi1T", 64), ("wi2rep", 128),
           ("bq", 1), ("bk", 1), ("bv", 1), ("bi1", 1), ("bi2", 1), ("bo", 128), ("wg", E0)],
    "f0": [("w1", E0 * HID0), ("w3", E0 * HID0), ("w2", E0 * HID0)],
    "l1": [("wv", 1024), ("wout", 1024), ("up", E1 * HID1), ("down", E1 * HID1), ("gw", E1), ("eb", E1)],
    "l2": [("wq", 128), ("wqkv", 384), ("wop", 128), ("w2c", 1), ("b2", 1), ("bq", 1), ("bk", 1), ("bv", 1),
           ("w1", HID2), ("w2", HID2), ("h1", C2 * HID2), ("h2", C2 * HID2), ("w3", HID2),
           ("s1", C2), ("s2", C2), ("hs1", C2), ("hs2", C2), ("s3", 128)],
    "l3": [("wv", 1024), ("wout", 1024), ("kernel", 128), ("bias", 128), ("bo", 128), ("aT", 128), ("b", 128)],
    "qk1": [("wqT", 2048), ("wkT", 2048), ("mask", 384)],
    "qk3": [("wqT", 2048), ("wkT", 2048), ("mask", 384)],
}


def width(pack):
    return sum(n for _, n in PACKS[pack])


class Sig:

    def __init__(self, nc, ctx, name, n, ahead=0):
        self.s, self.n, self.ahead = ctx.enter_context(nc.semaphore(name)), n, ahead

    def at(self, i, k):
        return i * self.n + (self.n + self.ahead + k + 1)

    def before(self, k):
        return self.n + k + 1

    def end(self):
        return self.n + self.ahead + PASSES * self.n


def program(nc, ins, out, upto=9):
    F32, BF16, U32, I32 = mybir.dt.float32, mybir.dt.bfloat16, mybir.dt.uint32, mybir.dt.int32
    ALU, ACT, AX = mybir.AluOpType, mybir.ActivationFunctionType, mybir.AxisListType.X
    ctx = ExitStack()
    with ctx:
        def sb(name, cols, dt=F32):
            return ctx.enter_context(nc.sbuf_tensor(name, [128, cols], dt))

        sigs = []

        def sig(name, n, ahead=0):
            sigs.append(Sig(nc, ctx, name, n, ahead))
            return sigs[-1]

        def sem(name):
            return ctx.enter_context(nc.semaphore(name))

        def views(region, pack):
            got, at = {}, 0
            for name, n in PACKS[pack]:
                got[name] = region[:, at:at + n]
                at += n
            return got

        x_t = sb("x_sb", (TILES + 4) * D)
        x_sb = x_t[:, :].rearrange("p (t d) -> p t d", d=D)
        regions = {p: sb("w_" + p, width(p)) for p in ("const", "l0", "f0", "l1", "l2")}
        regions["l3"] = regions["f0"]
        W = {p: views(regions[p], p) for p in ("const", "l0", "f0", "l1", "l2", "l3")}
        qk_t = sb("qk", 2 * HEADS * 128)
        a1_t, a3_t = qk_t[:, 0:HEADS * 128], qk_t[:, HEADS * 128:]
        mask1, mask3 = sb("mask1", 384, BF16), sb("mask3", 384, BF16)
        ident16 = sb("ident16", 128, BF16)
        half, one = sb("minus_half", 32), sb("one", 1)
        work = sb("work", 17400)
        PS = [ctx.enter_context(nc.psum_tensor(f"bank{j}", [128, 512], F32)) for j in range(8)]
        C = W["const"]
        ident = C["ident"]
        top = [0]

        def carve(*shape):
            n = int(np.prod(shape))
            v = work[:, top[0]:top[0] + n]
            top[0] += n
            assert top[0] <= 17400, top[0]
            if len(shape) == 2:
                v = v.rearrange("p (a b) -> p a b", b=shape[1])
            if len(shape) == 3:
                v = v.rearrange("p (a b c) -> p a b c", b=shape[1], c=shape[2])
            return v

        def spread(ap, *shape):
            return ap.to_broadcast([128, *shape])

        def copy(pool, dst, src):
            return pool.tensor_tensor(dst, src, spread(one[:, :].unsqueeze(2), *src.shape[1:]), ALU.mult)

        x_in, consts_in, w_in = sem("x_in"), sem("consts_in"), {p: sem("in_" + p) for p in PACKS}
        phase_end = sem("phase_end")
        stored = sem("stored")
        rows_d = nc.dram_tensor("normed_rows", (B * S, ROW), F32, kind="Internal").ap()
        res_d = nc.dram_tensor("residual", (B * S, D), F32, kind="Internal").ap()
        rows_v, res_v = (d.rearrange("(t p) c -> p t c", p=128) for d in (rows_d, res_d))
        rows_out = sem("rows_out")
        out_v = out.rearrange("b (i p) d -> p (b i) d", p=128)

        def close(eng, n):
            eng.drain().then_inc(phase_end, 1)
            eng.wait_ge(phase_end, 4 * n)

        pe_prog, act_prog, dve_prog, pool_prog, sp_prog = [], [], [], [], []

        top[0] = 0
        xn_all = carve(TILES + 6, D)
        sc_nat = carve(2, B, E0)
        keep_scores = top[0]
        scT = carve(2, 128)
        keep_work = top[0]
        st_all, mv_all = carve(TILES, 6), carve(TILES, 2)
        ve_all, rstd_all = carve(TILES), carve(TILES)
        xn4, xnT4 = carve(4, D), carve(512)
        lg_all, ex_all = carve(TILES, E0), carve(TILES, E0)
        mx_all, sm_all, rc_all = carve(TILES), carve(TILES), carve(TILES)
        g_set = sem("g_set")
        g_stat, g_var, g_pow = sem("g_stat"), sem("g_var"), sem("g_pow")
        g_xn, g_saved, g_tr = sig("g_xn", 1), sig("g_saved", 1), sig("g_tr", 1)
        g_xnT, g_lg, g_lgs = sig("g_xnT", 1), sig("g_lg", 1), sig("g_lgs", 1)
        g_sm, g_ex, g_sct = sem("g_sm"), sem("g_ex"), sem("g_sct")
        bo0 = W["l0"]["bo"]

        def sp_load(sp):
            for s in sigs:
                sp.sem_inc(s.s, s.n)
            xv = ins["x"].rearrange("b (i p) d -> p (b i) d", p=128)
            for c in range(4):
                sp.dma_start(x_sb[:, 8 * c:8 * c + 8, :], xv[:, 8 * c:8 * c + 8, :]).then_inc(x_in, 16)
            for p in ("const", "l0", "f0", "l1"):
                sp.dma_start(regions[p][:, :], ins[p]).then_inc(w_in[p], 16)

        def sp_rows(sp):
            sp.wait_ge(g_saved.s, g_saved.end())
            sp.dma_start(rows_v[:, :, 0:D], xn_all[:, 0:TILES, :]).then_inc(rows_out, 16)
            sp.wait_ge(g_sm, 6)
            for n in range(2):
                sp.dma_start(rows_v.rearrange("p (b i) c -> p i b c", i=2)[:, n, :, D:ROW], sc_nat[:, n, :, :]).then_inc(rows_out, 16)
            sp.wait_ge(rows_out, 48)

        def pool_gates(pool):
            pool.memset(x_sb[:, TILES:, :], 0.0).then_inc(g_set, 1)
            pool.memset(half[:, :], -0.5).then_inc(g_set, 1)
            pool.memset(one[:, :], 1.0).then_inc(g_set, 1)
            pool.wait_ge(g_set, 3)
            pool.wait_ge(g_var, 1)
            pool.tensor_tensor(rstd_all, ve_all, half[:, :], ALU.pow).then_inc(g_pow, 1)
            pool.wait_ge(w_in["l0"], 16)
            with pool.Fori(0, PASSES) as i:
                pool.wait_ge(g_xn.s, g_xn.at(i, 0))
                pool.tensor_copy(xn_all[:, bass.ds(4 * i, 4), :], xn4)
                pool.tensor_tensor(x_sb[:, bass.ds(4 * i, 4), :], x_sb[:, bass.ds(4 * i, 4), :],
                                   spread(bo0.unsqueeze(1), 4, D), ALU.add).then_inc(g_saved.s, 1)

        def dve_gates(dve):
            dve.wait_ge(x_in, 64)
            with dve.Fori(0, TILES) as t:
                dve.bn_stats(st_all[:, t, :], x_sb[:, t, :]).then_inc(g_stat, 1)
            dve.wait_ge(g_stat, TILES)
            for t in range(TILES):
                dve.bn_aggr(mv_all[:, t, :], st_all[:, t, :]).then_inc(g_stat, 1)
            dve.wait_ge(g_stat, 2 * TILES)
            dve.tensor_scalar(ve_all, mv_all[:, :, 1], EPS, None, ALU.add).then_inc(g_var, 1)
            dve.wait_ge(g_pow, 1)
            with dve.Fori(0, PASSES) as i:
                dve.wait_ge(g_tr.s, g_tr.at(i, -1))
                dve.wait_ge(g_saved.s, g_saved.at(i, -1))
                for k in range(4):
                    last = dve.tensor_scalar(xn4[:, k, :], x_sb[:, 4 * i + k, :], mv_all[:, 4 * i + k, 0:1],
                                             rstd_all[:, bass.ds(4 * i + k, 1)], ALU.subtract, ALU.mult)
                last.then_inc(g_xn.s, 1)
                dve.wait_ge(g_lg.s, g_lg.at(i, 0))
                dve.tensor_copy(lg_all[:, bass.ds(4 * i, 4), :],
                                PS[1][:, 0:4 * E0].rearrange("p (t e) -> p t e", e=E0)).then_inc(g_lgs.s, 1)
            dve.wait_ge(g_lgs.s, g_lgs.end())
            dve.tensor_reduce(mx_all, lg_all, AX, ALU.max).then_inc(g_sm, 1)
            dve.wait_ge(g_sm, 1)
            dve.tensor_tensor(lg_all, lg_all, spread(mx_all.unsqueeze(2), TILES, E0), ALU.subtract).then_inc(g_sm, 1)
            dve.wait_ge(g_ex, 1)
            dve.tensor_reduce(sm_all, ex_all, AX, ALU.add).then_inc(g_sm, 1)
            dve.wait_ge(g_sm, 3)
            dve.reciprocal(rc_all, sm_all).then_inc(g_sm, 1)
            dve.wait_ge(g_sm, 4)
            for n in range(2):
                dve.tensor_tensor(sc_nat[:, n, :, :], ex_all.rearrange("p (b i) e -> p i b e", i=2)[:, n, :, :],
                                  spread(rc_all.rearrange("p (b i) -> p i b", i=2)[:, n, :].unsqueeze(2), B, E0),
                                  ALU.mult).then_inc(g_sm, 1)
            dve.wait_ge(g_sct, 1)
            dve.tensor_copy(scT, PS[0][:, 0:256].rearrange("p (i t) -> p i t", i=2)).then_inc(g_sm, 1)

        def act_gates(act):
            with act.Fori(0, PASSES) as i:
                act.wait_ge(g_tr.s, g_tr.at(i, 0))
                act.activation(xnT4, PS[0][:, :], ACT.Copy).then_inc(g_xnT.s, 1)
            act.wait_ge(g_sm, 2)
            act.activation(ex_all, lg_all, ACT.Exp).then_inc(g_ex, 1)
            act.activation(ident16[:, :], ident, ACT.Copy).then_inc(g_ex, 1)

        def pe_gates(pe):
            pe.wait_ge(w_in["const"], 16)
            pe.wait_ge(w_in["l0"], 16)
            with pe.Fori(0, PASSES) as i:
                pe.wait_ge(g_xn.s, g_xn.at(i, 0))
                pe.wait_ge(g_xnT.s, g_xnT.at(i, -1))
                for k in range(4):
                    last = pe.transpose(PS[0][:, k * 128:(k + 1) * 128], xn4[:, k, :], ident)
                last.then_inc(g_tr.s, 1)
                pe.wait_ge(g_xnT.s, g_xnT.at(i, 0))
                pe.wait_ge(g_lgs.s, g_lgs.at(i, -1))
                for k in range(4):
                    last = pe.matmul(PS[1][:, k * E0:(k + 1) * E0], xnT4[:, k * 128:(k + 1) * 128], W["l0"]["wg"],
                                     start=True, stop=True)
                last.then_inc(g_lg.s, 1)
            pe.wait_ge(g_sm, 6)
            pe.wait_ge(g_xnT.s, g_xnT.end())
            for n in range(2):
                last = pe.transpose(PS[0][:, n * 128:(n + 1) * 128], sc_nat[:, n, :, :].rearrange("p b e -> p (b e)"), ident)
            last.then_inc(g_sct, 1)

        sp_prog.append(sp_load)
        sp_prog.append(sp_rows)
        pe_prog.append(pe_gates)
        act_prog.append(act_gates)
        dve_prog.append(dve_gates)
        pool_prog.append(pool_gates)

        SEARCH = 2
        top[0] = keep_work
        xnc = [carve(2, D) for _ in range(2)]
        xnT = [carve(256) for _ in range(2)]
        qT, hT = [carve(256) for _ in range(2)], [carve(256) for _ in range(2)]
        row = [carve(256) for _ in range(2)]
        junk, junk2 = carve(256), carve(256)
        impc, cnt, rank = carve(2, 2), carve(2, 4), carve(2, 2)
        sel = [carve(2, KEEP) for _ in range(2)]
        xselT, kselT = [carve(KEEP) for _ in range(2)], [carve(KEEP) for _ in range(2)]
        xselR = [carve(H0, KPAD) for _ in range(2)]
        kblk = [carve(H0, KEEP) for _ in range(2)]
        early = regions["l2"]
        vblk = [early[:, p * HCH * 128:(p + 1) * HCH * 128].rearrange("p (c d) -> p c d", d=128) for p in range(2)]
        p0_flat = [qk_t[:, n * H0 * KPAD:(n + 1) * H0 * KPAD].rearrange("p (h k) -> p h k", k=KPAD) for n in range(3)]
        P0 = [[p0_flat[0], p0_flat[1]], [p0_flat[2], carve(H0, KPAD)]]
        PT0 = early[:, 2 * HCH * 128:4 * HCH * 128].rearrange("p (c q) -> p c q", q=256)
        oT0 = [carve(256) for _ in range(2)]
        mx0, sm0, rc0 = carve(4, H0), carve(4, H0), carve(4, H0)
        t_bits, c_bits, bit, kept, cnt_e = carve(1), carve(1), carve(1), carve(1), carve(1)
        u32 = lambda ap: ap.bitcast(U32)
        SEL, SOFT, FIND = 10, 16, 5 * SEARCH
        per = {}

        def batch_sig(name, m):
            s = sig(name, 2 * m)
            per[s] = m
            return s

        def of(s, i, c, k=0):
            return s.s, s.at(i, c * per[s] + k)

        a_xnc, a_tr, a_xnT, a_q, a_qe, a_h, a_he, a_imp, a_row, a_sel, a_xs, a_xse, a_xr, a_ks, a_kse, a_kb, a_vb, a_vbe, a_o, a_oe, a_out, a_x = (
            batch_sig("a_" + n, 1) for n in (
                "rows", "turned", "turned_out", "queries", "queries_out", "hidden", "hidden_out", "importance", "importance_out", "kept", "kept_rows",
                "kept_rows_out", "kept_spread", "keys", "keys_out", "key_blocks", "value_blocks", "value_blocks_out",
                "heads", "heads_out", "output", "added"))
        a_s, a_sub, a_exp, a_rc, a_nm = (batch_sig("a_" + n, 2) for n in ("scores", "shifted", "exps", "sums", "weights"))
        a_pt, a_pte = batch_sig("a_weights_turned", 5), batch_sig("a_weights_turned_out", 5)
        a_dsel, a_dsoft, a_dfind = batch_sig("a_sel_order", SEL), batch_sig("a_softmax_order", SOFT), batch_sig("a_search_order", FIND)
        a_find, a_found = batch_sig("a_find", SEARCH), batch_sig("a_found", SEARCH)
        a_set, a_bits = sem("a_set"), sem("a_bits")
        HGROUPS = ((0, 6), (6, 11), (11, 16))
        VGROUPS = ((0, 4, 7), (4, 8, 6), (8, 10, 4))

        def run_steps(eng, step, tail):
            for p in range(2):
                step(0, p, p > 0)
            with eng.Fori(1, PASSES) as i:
                for p in range(2):
                    step(i, p, True)
            tail(PASSES, -1)

        def pool_attn0(pool):
            for p in range(2):
                pool.memset(xselR[p][:, :, KEEP:], 0.0).then_inc(a_set, 1)
                for q in range(2):
                    pool.memset(P0[p][q][:, :, KEEP:], 0.0).then_inc(a_set, 1)
            pool.memset(xn_all[:, TILES:, :], 0.0).then_inc(a_set, 1)
            pool.wait_ge(a_set, 7)

            def rows_(i, c):
                pool.wait_ge(*of(a_xs, i, c - 2))
                copy(pool, xnc[c % 2], xn_all[:, bass.ds(4 * i + 2 * c, 2), :]).then_inc(a_xnc.s, 1)

            def spread_rows(i, c):
                pool.wait_ge(*of(a_xse, i, c))
                pool.wait_ge(*of(a_vb, i, c - 2))
                copy(pool, xselR[c % 2][:, :, 0:KEEP], spread(xselT[c % 2].unsqueeze(1), H0, KEEP)).then_inc(a_xr.s, 1)

            def key_blocks(i, c):
                pool.wait_ge(*of(a_kse, i, c))
                pool.wait_ge(*of(a_s, i, c - 2, 1))
                pool.tensor_tensor(kblk[c % 2], spread(kselT[c % 2].unsqueeze(1), H0, KEEP),
                                   spread(C["headmask"].unsqueeze(2), H0, KEEP), ALU.mult).then_inc(a_kb.s, 1)

            def weights(i, c, q):
                w = P0[c % 2][q][:, :, 0:KEEP]
                pool.wait_ge(*of(a_rc, i, c, q))
                pool.tensor_tensor(w, w, spread(rc0[:, 2 * q + c % 2, :].unsqueeze(2), H0, KEEP), ALU.mult).then_inc(a_nm.s, 1)

            def step(i, p, back):
                if back:
                    weights(i, p - 1, 1)
                spread_rows(i, p + 1)
                weights(i, p, 0)
                key_blocks(i, p + 1)
                rows_(i, p + 3)

            rows_(0, 0)
            rows_(0, 1)
            spread_rows(0, 0)
            key_blocks(0, 0)
            rows_(0, 2)
            run_steps(pool, step, lambda i, c: weights(i, c, 1))

        def act_attn0(act):
            L = W["l0"]

            def turned_out(i, c):
                act.wait_ge(*of(a_tr, i, c))
                act.wait_ge(*of(a_q, i, c - 2))
                act.activation(xnT[c % 2], PS[6][:, 0:256], ACT.Copy).then_inc(a_xnT.s, 1)

            def hidden_out(i, c):
                act.wait_ge(*of(a_h, i, c))
                act.wait_ge(*of(a_imp, i, c - 2))
                act.activation(hT[c % 2][0:64, :], PS[7][0:64, 256:512], ACT.Relu, bias=L["bi1"][0:64, :]).then_inc(a_he.s, 1)

            def queries_out(i, c):
                act.wait_ge(*of(a_q, i, c))
                act.wait_ge(*of(a_s, i, c - 2, 1))
                act.activation(qT[c % 2], PS[6][:, 256:512], ACT.Identity, bias=L["bq"]).then_inc(a_qe.s, 1)

            def kept_out(i, c):
                act.wait_ge(*of(a_xs, i, c))
                act.wait_ge(*of(a_xr, i, c - 2))
                act.activation(xselT[c % 2], PS[7][:, 0:KEEP], ACT.Copy).then_inc(a_xse.s, 1)

            def keys_out(i, c):
                act.wait_ge(*of(a_ks, i, c))
                act.wait_ge(*of(a_kb, i, c - 2))
                act.activation(kselT[c % 2], PS[7][:, 128:128 + KEEP], ACT.Identity, bias=L["bk"]).then_inc(a_kse.s, 1)

            def exps(i, c, q):
                w = P0[c % 2][q][:, :, 0:KEEP]
                act.wait_ge(*of(a_sub, i, c, q))
                act.activation(w, w, ACT.Exp, scale=float(1 / np.sqrt(HD0))).then_inc(a_exp.s, 1)

            def weights_out(i, c):
                for j in range(5):
                    act.wait_ge(*of(a_pt, i, c, j))
                    if j == 0:
                        act.wait_ge(*of(a_o, i, c - 1))
                    act.activation(PT0[:, 2 * j:2 * j + 2, :].rearrange("p c t -> p (c t)"), PS[3 + j % 2][:, :], ACT.Copy).then_inc(a_pte.s, 1)

            def heads_out(i, c):
                act.wait_ge(*of(a_o, i, c))
                act.wait_ge(*of(a_out, i, c - 2))
                act.activation(oT0[c % 2], PS[5][:, 0:256], ACT.Identity, bias=L["bv"]).then_inc(a_oe.s, 1)

            def step(i, p, back):
                turned_out(i, p + 2)
                kept_out(i, p + 1)
                queries_out(i, p + 1)
                if back:
                    weights_out(i, p - 1)
                hidden_out(i, p + 2)
                exps(i, p, 0)
                keys_out(i, p + 1)
                if back:
                    heads_out(i, p - 1)
                exps(i, p, 1)

            def tail(i, c):
                weights_out(i, c)
                heads_out(i, c)

            turned_out(0, 0)
            hidden_out(0, 0)
            turned_out(0, 1)
            kept_out(0, 0)
            queries_out(0, 0)
            hidden_out(0, 1)
            keys_out(0, 0)
            run_steps(act, step, tail)

        def dve_attn0(dve):
            L = W["l0"]

            def link(s, i, c, k, ins):
                ins.then_inc(s.s, 1)
                dve.wait_ge(*of(s, i, c, k))

            def count(i, c, n):
                lk = lambda k, ins: link(a_dfind, i, c, 5 * n + k, ins)
                lk(0, dve.tensor_tensor(u32(c_bits), u32(t_bits), u32(bit), ALU.bitwise_or))
                lk(1, dve.tensor_scalar(junk2, scT.rearrange("p i t -> p (i t)"), c_bits, 0.0, ALU.is_ge, ALU.add, accum_out=cnt_e))
                dve.sem_inc(a_find.s, 1)

            def decide(i, c, n):
                lk = lambda k, ins: link(a_dfind, i, c, 5 * n + k, ins)
                dve.wait_ge(*of(a_found, i, c, n))
                lk(2, dve.scalar_tensor_tensor(u32(kept), PS[2][:, 511:512], CAP - 0.5, u32(bit), ALU.is_ge, ALU.mult))
                lk(3, dve.tensor_tensor(u32(t_bits), u32(t_bits), u32(kept), ALU.bitwise_or))
                lk(4, dve.tensor_scalar(u32(bit), u32(bit), 1, None, ALU.logical_shift_right))

            def importance_out(i, c):
                dve.wait_ge(*of(a_imp, i, c))
                dve.tensor_scalar(row[c % 2], PS[6][:, 0:256], L["bi2"], None, ALU.add).then_inc(a_row.s, 1)

            def keep(i, c):
                p = c % 2
                dve.wait_ge(*of(a_row, i, c))
                dve.wait_ge(*of(a_xs, i, c - 2))
                for n in range(2):
                    lk = lambda k, ins: link(a_dsel, i, c, 5 * n + k, ins)
                    own = impc[:, p, n:n + 1]
                    lk(0, dve.scalar_tensor_tensor(junk[:, 0:128], row[p][:, n * 128:(n + 1) * 128], 1.0, ident,
                                                   ALU.mult, ALU.mult, accum_out=own))
                    lk(1, dve.tensor_scalar(junk, row[p], own, 0.0, ALU.is_gt, ALU.add, accum_out=cnt[:, p, 2 * n:2 * n + 1]))
                    lk(2, dve.scalar_tensor_tensor(junk, row[p], own, C["tri"][:, n * 256:(n + 1) * 256],
                                                   ALU.is_equal, ALU.mult, accum_out=cnt[:, p, 2 * n + 1:2 * n + 2]))
                    lk(3, dve.tensor_tensor(rank[:, p, n:n + 1], cnt[:, p, 2 * n:2 * n + 1], cnt[:, p, 2 * n + 1:2 * n + 2], ALU.add))
                    lk(4, dve.tensor_scalar(sel[p][:, n, :], C["iota"][:, 0:KEEP], rank[:, p, n:n + 1], None, ALU.is_equal))
                dve.sem_inc(a_sel.s, 1)

            def value_blocks_out(i, c):
                dve.wait_ge(*of(a_vb, i, c))
                dve.wait_ge(*of(a_o, i, c - 2))
                for c0, c1, bk in VGROUPS:
                    last = dve.tensor_tensor(vblk[c % 2][:, c0:c1, :].rearrange("p c d -> p (c d)"),
                                             PS[bk][:, 0:(c1 - c0) * 128], C["vmask"][:, c0 * 128:c1 * 128], ALU.mult)
                last.then_inc(a_vbe.s, 1)

            def shifted(i, c, q):
                m = 2 * q + c % 2
                lk = lambda k, ins: link(a_dsoft, i, c, 8 * q + k, ins)
                dve.wait_ge(*of(a_s, i, c, q))
                dve.wait_ge(*of(a_pt, i, c - 2, 4))
                scores = [PS[j][:, 0:(h1 - h0) * KEEP].rearrange("p (h k) -> p h k", k=KEEP) for j, (h0, h1) in enumerate(HGROUPS)]
                for j, (h0, h1) in enumerate(HGROUPS):
                    dve.tensor_reduce(mx0[:, m, h0:h1], scores[j], AX, ALU.max).then_inc(a_dsoft.s, 1)
                for j, (h0, h1) in enumerate(HGROUPS):
                    dve.wait_ge(*of(a_dsoft, i, c, 8 * q + j))
                    last = dve.tensor_tensor(P0[c % 2][q][:, h0:h1, 0:KEEP], scores[j], spread(mx0[:, m, h0:h1].unsqueeze(2), h1 - h0, KEEP), ALU.subtract)
                    if j < 2:
                        last.then_inc(a_dsoft.s, 1)
                last.then_inc(a_sub.s, 1)
                dve.sem_inc(a_dsoft.s, 1)

            def sums(i, c, q):
                m = 2 * q + c % 2
                dve.wait_ge(*of(a_exp, i, c, q))
                link(a_dsoft, i, c, 8 * q + 6, dve.tensor_reduce(sm0[:, m, :], P0[c % 2][q][:, :, 0:KEEP], AX, ALU.add))
                dve.reciprocal(rc0[:, m, :], sm0[:, m, :]).then_inc(a_rc.s, 1)
                dve.sem_inc(a_dsoft.s, 1)

            def added(i, c):
                tt = bass.ds(4 * i + 2 * c, 2)
                dve.wait_ge(*of(a_out, i, c))
                dve.tensor_tensor(x_sb[:, tt, :], x_sb[:, tt, :], PS[5][:, 256:512].rearrange("p (t d) -> p t d", d=D), ALU.add).then_inc(a_x.s, 1)

            def step(i, p, back):
                if back:
                    sums(i, p - 1, 1)
                shifted(i, p, 0)
                count(i, p, 0)
                sums(i, p, 0)
                decide(i, p, 0)
                importance_out(i, p + 2)
                shifted(i, p, 1)
                count(i, p, 1)
                keep(i, p + 2)
                value_blocks_out(i, p + 1)
                decide(i, p, 1)
                if back:
                    added(i, p - 1)

            def tail(i, c):
                sums(i, c, 1)
                added(i, c)

            dve.wait_ge(g_sm, 7)
            dve.memset(u32(t_bits), 0).then_inc(a_bits, 1)
            dve.memset(u32(bit), 1 << 29).then_inc(a_bits, 1)
            dve.wait_ge(a_bits, 2)
            for c in range(2):
                importance_out(0, c)
                keep(0, c)
            value_blocks_out(0, 0)
            run_steps(dve, step, tail)

        def pe_attn0(pe):
            L = W["l0"]

            def search(i, c, n):
                pe.wait_ge(*of(a_find, i, c, n))
                pe.wait_ge(*of(a_sub, i, c, n))
                pe.matmul(PS[2][:, 511:512], C["blockones"], cnt_e, start=True, stop=True).then_inc(a_found.s, 1)

            def turn(i, c):
                pe.wait_ge(*of(a_xnc, i, c))
                pe.wait_ge(*of(a_vbe, i, c - 2))
                pe.wait_ge(*of(a_row, i, c - 1))
                for n in range(2):
                    last = pe.transpose(PS[6][:, n * 128:(n + 1) * 128], xnc[c % 2][:, n, :], ident)
                last.then_inc(a_tr.s, 1)

            def hidden(i, c):
                pe.wait_ge(*of(a_xnT, i, c))
                pe.wait_ge(*of(a_xse, i, c - 1))
                pe.matmul(PS[7][0:64, 256:512], L["wi1T"], xnT[c % 2], start=True, stop=True).then_inc(a_h.s, 1)

            def importance(i, c):
                pe.wait_ge(*of(a_he, i, c))
                pe.wait_ge(*of(a_qe, i, c - 1))
                pe.matmul(PS[6][:, 0:256], L["wi2rep"][0:64, :], hT[c % 2][0:64, :], start=True, stop=True).then_inc(a_imp.s, 1)

            def queries(i, c):
                pe.wait_ge(*of(a_xnT, i, c))
                pe.wait_ge(*of(a_xnT, i, c + 1))
                pe.matmul(PS[6][:, 256:512], L["wqT"], xnT[c % 2], start=True, stop=True).then_inc(a_q.s, 1)

            def kept_rows(i, c):
                pe.wait_ge(*of(a_sel, i, c))
                pe.wait_ge(*of(a_vbe, i, c - 1))
                for n in range(2):
                    last = pe.matmul(PS[7][:, 0:KEEP], xnc[c % 2][:, n, :], sel[c % 2][:, n, :], start=(n == 0), stop=(n == 1))
                last.then_inc(a_xs.s, 1)

            def keys(i, c):
                pe.wait_ge(*of(a_xse, i, c))
                pe.wait_ge(*of(a_he, i, c + 1))
                pe.matmul(PS[7][:, 128:128 + KEEP], L["wkT"], xselT[c % 2], start=True, stop=True).then_inc(a_ks.s, 1)

            def value_blocks(i, c):
                pe.wait_ge(*of(a_xr, i, c))
                pe.wait_ge(*of(a_kse, i, c))
                pe.wait_ge(*of(a_qe, i, c))
                pe.wait_ge(*of(a_he, i, c + 1))
                pe.wait_ge(*of(a_row, i, c + 1))
                pe.wait_ge(*of(a_pte, i, c - 2, 4))
                for c0, c1, bk in VGROUPS:
                    for j in range(c0, c1):
                        last = pe.matmul(PS[bk][:, (j - c0) * 128:(j - c0 + 1) * 128],
                                         xselR[c % 2].rearrange("p h k -> p (h k)")[:, j * 128:(j + 1) * 128], L["wvT"], start=True, stop=True)
                last.then_inc(a_vb.s, 1)

            def scores(i, c, q):
                if q == 0:
                    pe.wait_ge(*of(a_kb, i, c))
                    pe.wait_ge(*of(a_qe, i, c))
                    pe.wait_ge(*of(a_sub, i, c - 1, 1))
                    pe.wait_ge(*of(a_dfind, i, c - 1, FIND - 1))
                else:
                    pe.wait_ge(*of(a_sub, i, c, 0))
                    pe.wait_ge(*of(a_dfind, i, c, FIND // 2 - 1))
                for j, (h0, h1) in enumerate(HGROUPS):
                    last = pe.matmul(PS[j][:, 0:(h1 - h0) * KEEP], qT[c % 2][:, q * 128:(q + 1) * 128],
                                     kblk[c % 2][:, h0:h1, :].rearrange("p h k -> p (h k)"), start=True, stop=True)
                last.then_inc(a_s.s, 1)

            def weights_turned(i, c):
                for q in range(2):
                    pe.wait_ge(*of(a_nm, i, c, q))
                pe.wait_ge(*of(a_vbe, i, c + 1))
                for j in range(5):
                    pe.wait_ge(*of(a_pte, i, c, j - 2))
                    for k in range(2):
                        for q in range(2):
                            last = pe.transpose(PS[3 + j % 2][:, k * 256 + q * 128:k * 256 + (q + 1) * 128],
                                                P0[c % 2][q].rearrange("p h k -> p (h k)")[:, (2 * j + k) * 128:(2 * j + k + 1) * 128], ident)
                    last.then_inc(a_pt.s, 1)

            def heads(i, c):
                pe.wait_ge(*of(a_pte, i, c, 4))
                pe.wait_ge(*of(a_vbe, i, c))
                pe.wait_ge(*of(a_x, i, c - 1))
                for j in range(HCH):
                    last = pe.matmul(PS[5][:, 0:256], vblk[c % 2][:, j, :], PT0[:, j, :], start=(j == 0), stop=(j == HCH - 1))
                last.then_inc(a_o.s, 1)

            def output(i, c):
                pe.wait_ge(*of(a_oe, i, c))
                for n in range(2):
                    last = pe.matmul(PS[5][:, 256 + n * 128:256 + (n + 1) * 128], oT0[c % 2][:, n * 128:(n + 1) * 128], L["woT"], start=True, stop=True)
                last.then_inc(a_out.s, 1)

            def step(i, p, back):
                scores(i, p, 0)
                turn(i, p + 2)
                kept_rows(i, p + 1)
                queries(i, p + 1)
                if back:
                    weights_turned(i, p - 1)
                hidden(i, p + 2)
                keys(i, p + 1)
                search(i, p, 0)
                if back:
                    heads(i, p - 1)
                importance(i, p + 2)
                scores(i, p, 1)
                value_blocks(i, p + 1)
                search(i, p, 1)
                if back:
                    output(i, p - 1)

            def tail(i, c):
                weights_turned(i, c)
                heads(i, c)
                output(i, c)

            pe.wait_ge(a_set, 7)
            turn(0, 0)
            hidden(0, 0)
            importance(0, 0)
            turn(0, 1)
            kept_rows(0, 0)
            queries(0, 0)
            hidden(0, 1)
            keys(0, 0)
            importance(0, 1)
            value_blocks(0, 0)
            run_steps(pe, step, tail)

        if upto >= 2:
            pe_prog.append(pe_attn0)
            act_prog.append(act_attn0)
            dve_prog.append(dve_attn0)
            pool_prog.append(pool_attn0)
        else:
            for prog in (pe_prog, act_prog, dve_prog, pool_prog):
                prog.append(lambda eng: None)

        top[0] = 0
        CT = CAP // 128
        xg = carve(E0 * CT, ROW)
        assert top[0] <= keep_scores, top[0]
        top[0] = keep_work
        ones256, eq, gt, cum = carve(256), carve(256), carve(256), carve(256)
        eqn, allow, offs, ngt, total, first = (carve(1) for _ in range(6))
        pos, hi = carve(256), carve(256)
        eq4 = carve(256, CT)
        lo16 = carve(128).bitcast(BF16).rearrange("p (i b e) -> p i b e", b=B, e=E0)
        lists16 = carve(128 * CT * 2).bitcast(BF16).rearrange("p (j k w) -> p j k w", k=CT, w=2)
        lists_rhs = lists16.rearrange("p (i b e) k w -> p i b e (k w)", b=B, e=E0)
        iota16, zero16 = carve(64).bitcast(BF16), carve(64).bitcast(BF16)
        oh = [carve(E0 * 64).bitcast(BF16).rearrange("p (e s) -> p e s", s=128) for _ in range(2)]
        idx = carve(E0 * CT).bitcast(U32)
        xs = [carve(CT, D) for _ in range(2)]
        xeT = [carve(512) for _ in range(2)]
        sa = [carve(512) for _ in range(2)]
        hh = [carve(2, 512) for _ in range(2)]
        y = [carve(CT, D) for _ in range(2)]
        b_set, b_dv, b_cnt, b_selT, b_idx = sem("b_set"), sem("b_dv"), sem("b_cnt"), sem("b_selT"), sem("b_idx")
        b_oh, b_ohu = sig("b_onehot", 2), sig("b_onehot_used", 2)
        b_got = [sem(f"b_got{e}") for e in range(3)]
        b_acc, b_added, x_back = sem("b_acc"), sem("b_added"), sem("x_back")
        b_xs, b_tr, b_xe, b_up, b_sa, b_g, b_dn, b_y = (sem("b_" + n) for n in ("scaled", "turned", "turned_out", "up", "silu", "gated", "down", "y"))
        scT_f = scT.rearrange("p i t -> p (i t)")

        def dve_ffn0(dve):
            k = [0]

            def link(ins):
                k[0] += 1
                ins.then_inc(b_dv, 1)
                dve.wait_ge(b_dv, k[0])

            link(dve.memset(ones256, 1.0))
            link(dve.memset(zero16, 0.0))
            link(dve.tensor_copy(iota16, C["iota"]))
            link(dve.tensor_scalar(gt, scT_f, t_bits, 0.0, ALU.is_gt, ALU.add, accum_out=ngt))
            link(dve.tensor_scalar(eq, scT_f, t_bits, None, ALU.is_equal))
            link(dve.tensor_tensor_scan(cum, ones256, eq, 0.0, ALU.mult, ALU.add))
            link(dve.tensor_copy(eqn, cum[:, 255:256]))
            dve.sem_inc(b_set, 1)
            dve.wait_ge(b_cnt, 2)
            link(dve.tensor_scalar(allow, PS[0][:, 0:1], -1.0, float(CAP), ALU.mult, ALU.add))
            link(dve.tensor_tensor(offs, allow, PS[1][:, 0:1], ALU.subtract))
            link(dve.scalar_tensor_tensor(eq, cum, offs, eq, ALU.is_le, ALU.mult))
            link(dve.tensor_tensor(gt, gt, eq, ALU.add))
            link(dve.tensor_tensor_scan(cum, ones256, gt, 0.0, ALU.mult, ALU.add))
            link(dve.tensor_copy(total, cum[:, 255:256]))
            dve.sem_inc(b_set, 1)
            dve.wait_ge(b_cnt, 3)
            link(dve.tensor_copy(first, PS[2][:, 0:1]))
            link(dve.scalar_tensor_tensor(cum, cum, first, gt, ALU.add, ALU.mult))
            link(dve.tensor_scalar(cum, cum, -1.0, None, ALU.add))
            dve.sem_inc(b_set, 1)
            dve.wait_ge(b_selT, 1)
            link(dve.tensor_copy(pos, PS[0][:, 0:256]))
            link(dve.tensor_scalar(hi, pos, 128.0, None, ALU.is_ge))
            for c in range(2, CT):
                link(dve.scalar_tensor_tensor(hi, pos, 128.0 * c, hi, ALU.is_ge, ALU.add))
            link(dve.scalar_tensor_tensor(lo16.rearrange("p i b e -> p (i b e)"), hi, -128.0, pos, ALU.mult, ALU.add))
            link(dve.tensor_tensor(eq4, spread(hi.unsqueeze(2), 256, CT), spread(C["iota"][:, 0:CT].unsqueeze(1), 256, CT), ALU.is_equal))
            link(dve.tensor_tensor(lists16[:, :, :, 0], eq4, spread(C["tileno"].unsqueeze(2), 256, CT), ALU.mult))
            link(dve.tensor_scalar(lists16[:, :, :, 1], eq4, C["pidx"], None, ALU.mult))
            dve.sem_inc(b_set, 1)
            with dve.Fori(0, B) as b:
                for n in range(2):
                    dve.wait_ge(b_ohu.s, b_ohu.at(b, n - 2))
                    dve.tensor_tensor(oh[n], spread(lo16[:, n, b, :].unsqueeze(2), E0, 128), spread(iota16.unsqueeze(1), E0, 128),
                                      ALU.is_equal).then_inc(b_oh.s, 1)
            dve.wait_ge(b_ohu.s, 2 * B + 2)
            dve.wait_ge(b_cnt, 4)
            sums = PS[2][:, 0:E0 * CT * 2].rearrange("p (j w) -> p j w", w=2)
            link(dve.tensor_copy(pos[:, 0:E0 * CT], sums[:, :, 0]))
            dve.scalar_tensor_tensor(idx, pos[:, 0:E0 * CT], 128.0, sums[:, :, 1], ALU.mult, ALU.add).then_inc(b_idx, 1)

            def scaled(e):
                dve.wait_ge(b_got[e % 3], 16 * CT * (e // 3 + 1))
                if e >= 2:
                    dve.wait_ge(b_tr, e - 1)
                for t in range(CT):
                    r = xg[:, CT * e + t, :]
                    last = dve.tensor_scalar(xs[e % 2][:, t, :], r[:, 0:D], r[:, D + e:D + e + 1], None, ALU.mult)
                last.then_inc(b_xs, 1)

            def out_(e):
                dve.wait_ge(b_dn, e + 1)
                if e >= 2:
                    dve.wait_ge(b_added, 16 * CT * (e - 1))
                dve.tensor_copy(y[e % 2].rearrange("p t d -> p (t d)"), PS[6 + e % 2][:, :]).then_inc(b_y, 1)

            scaled(0)
            for e in range(E0):
                if e + 1 < E0:
                    scaled(e + 1)
                for c in range(2):
                    u = 2 * e + c
                    dve.wait_ge(b_sa, u + 1)
                    dve.wait_ge(b_up, u + 1)
                    if e >= 2:
                        dve.wait_ge(b_dn, e - 1)
                    dve.tensor_tensor(hh[e % 2][:, c, :], sa[c], PS[4 + c][:, :], ALU.mult).then_inc(b_g, 1)
                if e >= 1:
                    out_(e - 1)
            out_(E0 - 1)
            dve.wait_ge(x_back, 64)

        def pool_ffn0(pool):
            pool.wait_ge(b_idx, 1)
            pool.wait_ge(rows_out, 48)
            slot = lambda e, t: bass.IndirectOffsetOnAxis(ap=idx[:, CT * e + t:CT * e + t + 1], axis=0)
            for e in range(E0):
                if e >= 3:
                    pool.wait_ge(b_got[e % 3], 16 * CT * (e // 3))
                for t in range(CT):
                    pool.indirect_dma_start(xg[:, CT * e + t, :], None, rows_d, slot(e, t)).then_inc(b_got[e % 3], 16)
            pool.wait_ge(b_acc, 16)
            for e in range(E0):
                pool.wait_ge(b_y, e + 1)
                if e:
                    pool.wait_ge(b_added, 16 * CT * e)
                for t in range(CT):
                    pool.indirect_dma_start(res_d, slot(e, t), y[e % 2][:, t, :], None, compute_op=ALU.add).then_inc(b_added, 16)

        def sp_ffn0(sp):
            sp.wait_ge(phase_end, 4 * 2)
            sp.dma_start(res_v, x_sb[:, 0:TILES, :]).then_inc(b_acc, 16)
            sp.wait_ge(b_added, 16 * CT * E0)
            for c in range(4):
                sp.dma_start(x_sb[:, 8 * c:8 * c + 8, :], res_v[:, 8 * c:8 * c + 8, :]).then_inc(x_back, 16)

        def act_ffn0(act):
            def evac(e):
                act.wait_ge(b_tr, e + 1)
                if e >= 2:
                    act.wait_ge(b_up, 2 * e - 2)
                act.activation(xeT[e % 2], PS[e % 2][:, :], ACT.Copy).then_inc(b_xe, 1)

            evac(0)
            for e in range(E0):
                if e + 1 < E0:
                    evac(e + 1)
                for c in range(2):
                    u = 2 * e + c
                    act.wait_ge(b_up, u + 1)
                    if u >= 2:
                        act.wait_ge(b_g, u - 1)
                    act.activation(sa[c], PS[2 + c][:, :], ACT.Silu).then_inc(b_sa, 1)

        def pe_ffn0(pe):
            F = W["f0"]
            pe.wait_ge(w_in["f0"], 16)
            pe.wait_ge(b_set, 1)
            pe.matmul(PS[0][:, 0:1], C["blockones"], ngt, start=True, stop=True).then_inc(b_cnt, 1)
            pe.matmul(PS[1][:, 0:1], C["lowerblk"], eqn, start=True, stop=True).then_inc(b_cnt, 1)
            pe.wait_ge(b_set, 2)
            pe.matmul(PS[2][:, 0:1], C["lowerblk"], total, start=True, stop=True).then_inc(b_cnt, 1)
            pe.wait_ge(b_set, 3)
            for n in range(2):
                last = pe.transpose(PS[0][:, n * 128:(n + 1) * 128], cum[:, n * 128:(n + 1) * 128], ident)
            last.then_inc(b_selT, 1)
            pe.wait_ge(b_set, 4)
            pe.matmul(PS[2][:, 0:E0 * CT * 2], zero16, zero16[:, 0:E0 * CT * 2], start=True, stop=False, skip_group_check=True)
            with pe.Fori(0, B) as b:
                for n in range(2):
                    pe.wait_ge(b_oh.s, b_oh.at(b, n))
                    for e in range(E0):
                        last = pe.matmul(PS[2][:, e * CT * 2:(e + 1) * CT * 2], oh[n][:, e, :], lists_rhs[:, n, b, e, :],
                                         start=False, stop=False, skip_group_check=True)
                    last.then_inc(b_ohu.s, 1)
            pe.matmul(PS[2][:, 0:E0 * CT * 2], zero16, zero16[:, 0:E0 * CT * 2], start=False, stop=True,
                      skip_group_check=True).then_inc(b_cnt, 1)

            def turn(e):
                pe.wait_ge(b_xs, e + 1)
                if e >= 2:
                    pe.wait_ge(b_xe, e - 1)
                for t in range(CT):
                    last = pe.transpose(PS[e % 2][:, t * 128:(t + 1) * 128], xs[e % 2][:, t, :], ident)
                last.then_inc(b_tr, 1)

            def down(e):
                pe.wait_ge(b_g, 2 * e + 2)
                if e >= 2:
                    pe.wait_ge(b_y, e - 1)
                for t in range(CT):
                    for c in range(2):
                        last = pe.matmul(PS[6 + e % 2][:, t * 128:(t + 1) * 128], hh[e % 2][:, c, t * 128:(t + 1) * 128],
                                         F["w2"][:, (2 * e + c) * D:(2 * e + c + 1) * D], start=(c == 0), stop=(c == 1))
                last.then_inc(b_dn, 1)

            pe.wait_ge(b_idx, 1)
            turn(0)
            for e in range(E0):
                if e + 1 < E0:
                    turn(e + 1)
                pe.wait_ge(b_xe, e + 1)
                for c in range(2):
                    u = 2 * e + c
                    if u >= 2:
                        pe.wait_ge(b_sa, u - 1)
                        pe.wait_ge(b_g, u - 1)
                    at = e * HID0 + c * 128
                    pe.matmul(PS[2 + c][:, :], F["w1"][:, at:at + 128], xeT[e % 2], start=True, stop=True)
                    pe.matmul(PS[4 + c][:, :], F["w3"][:, at:at + 128], xeT[e % 2], start=True, stop=True).then_inc(b_up, 1)
                if e >= 1:
                    down(e - 1)
            down(E0 - 1)

        if upto >= 3:
            pe_prog.append(pe_ffn0)
            act_prog.append(act_ffn0)
            dve_prog.append(dve_ffn0)
            pool_prog.append(pool_ffn0)
            sp_prog.append(sp_ffn0)

        NH = 2 * HEADS
        STEPS = NH + 6

        def attention(name, layer, a_t, mask, pack, qk, phase, last_layer):
            L = W[pack]
            moe = not last_layer
            top[0] = 0
            qk_raw = work[:, 0:width(qk)]
            raw = views(qk_raw, qk)
            xnc, st, mv, ve, rstd = carve(2, D), carve(2, 6), carve(2, 2), carve(2), carve(2)
            xnT = [carve(256) for _ in range(2)]
            v_sb = [carve(2, HEADS * HD) for _ in range(2)]
            qp = [carve(512) for _ in range(2)]
            pr = [carve(384) for _ in range(3)]
            pt = [carve(384) for _ in range(2)]
            ot = [carve(HEADS // 2, 256) for _ in range(2)]
            nmx, sm, rc = carve(3, 2), carve(3, 2), carve(3, 2)
            h1, h2 = [carve(512) for _ in range(2)], [carve(512) for _ in range(2)]
            ex, sg, bi, wt2 = carve(2, E1), carve(2, E1), carve(2, E1), [carve(2, E1) for _ in range(2)]
            cgt, ceq, rk = carve(2, E1 * E1), carve(2, E1 * E1), carve(2, E1)
            w_eff, brow = carve(128), carve(128)
            qmax, scl = carve(2), carve(4)
            F = lambda n: f"{name}_{n}"

            MISC = []
            for s in range(STEPS):
                if s % 2 == 0 and s < NH:
                    MISC.append((s, "q", s // 2))
                for p, at in ((1, 0), (0, HEADS)):
                    if s == at + 6:
                        MISC.append((s, "t", p))
                    if at + 8 <= s < at + 12:
                        MISC.append((s, "v", 4 * p + s - at - 8))
                if moe and s % HEADS == 1 and s < NH:
                    MISC.append((s, "g", s // HEADS))
                if s == HEADS + 5 or s == NH + 5:
                    MISC.append((s, "o", 0 if s < NH else 1))
            place = {m[1:]: k for k, m in enumerate(MISC)}
            AHEAD = 5
            m_f, m_e = sig(F("misc_full"), len(MISC), AHEAD), sig(F("misc_empty"), len(MISC), AHEAD)
            s_f, s_mx, s_ex, s_rc = sig(F("scores"), NH), sig(F("maxima"), NH), sig(F("exps"), NH), sig(F("sums"), NH)
            s_nm, s_t, s_te, s_pv = sig(F("weights"), NH), sig(F("turned"), NH), sig(F("turned_out"), NH), sig(F("values"), NH)
            s_ot = sig(F("heads_out"), HEADS)
            ln_v, ln_p, ln_x = sig(F("variance"), 2, 1), sig(F("rstd"), 2, 1), sig(F("normed"), 2, 1)
            dv = sig(F("dve_order"), 10 + (18 if moe else 0), 5)
            if moe:
                f_u, f_r, f_q, f_d, f_x = (sig(F("moe_" + n), 2 * E1) for n in ("up", "relu", "square", "down", "added"))
                g_w = sig(F("gates"), 2)
            else:
                ln_b, pre_q = sig(F("biased"), 2, 1), sem(F("pre_q"))
            a_made, a_kept, pre = sem(F("A_made")), sem(F("A_kept")), sem(F("pre"))

            def pe_(pe):
                pe.wait_ge(w_in[qk], 16)
                for h in range(HEADS):
                    if h >= 8 and h % 4 == 0:
                        pe.wait_ge(a_kept, h // 4 - 1)
                    mm = pe.matmul(PS[h // 4 % 2][:, h % 4 * 128:(h % 4 + 1) * 128], raw["wqT"][0:HD, h * 128:(h + 1) * 128],
                                   raw["wkT"][0:HD, h * 128:(h + 1) * 128], start=True, stop=True)
                    if h % 4 == 3:
                        mm.then_inc(a_made, 1)
                if last_layer:
                    pe.wait_ge(w_in[pack], 16)
                    pe.matmul(PS[2][:, 0:128], L["aT"][0:16, :], L["b"][0:16, :], start=True, stop=True).then_inc(a_made, 1)
                pe.wait_ge(w_in[pack], 16)

                def turn(p):
                    for t in range(2):
                        mm = pe.transpose(PS[4][:, t * 128:(t + 1) * 128], xnc[:, t, :], ident)
                    return mm

                def values(c):
                    p, t, half_ = c // 4, c // 2 % 2, c % 2
                    return pe.matmul(PS[4][:, :], xnT[p][:, t * 128:(t + 1) * 128], L["wv"][:, half_ * 512:(half_ + 1) * 512],
                                     start=True, stop=True)

                pe.wait_ge(ln_x.s, ln_x.before(0))
                turn(0).then_inc(m_f.s, 1)
                for c in range(4):
                    pe.wait_ge(m_e.s, m_e.before(c))
                    values(c).then_inc(m_f.s, 1)
                with pe.Fori(0, PASSES) as i:
                    def misc(s, kinds):
                        for at, kind, n in MISC:
                            if at != s or kind not in kinds:
                                continue
                            k = place[kind, n]
                            if kind == "t":
                                pe.wait_ge(ln_x.s, ln_x.at(i, 1 - n))
                            if kind == "o":
                                pe.wait_ge(s_ot.s, s_ot.at(i, 8 * n + 7))
                            pe.wait_ge(m_e.s, m_e.at(i, k - 1))
                            if kind == "q":
                                p = n // 8
                                for j in range(2):
                                    h = (2 * n + j) % HEADS
                                    mm = pe.matmul(PS[4][:, j * 256:(j + 1) * 256], a_t[:, h * 128:(h + 1) * 128], xnT[p], start=True, stop=True)
                            if kind == "t":
                                mm = turn(n)
                            if kind == "v":
                                mm = values(n)
                            if kind == "g":
                                for t in range(2):
                                    mm = pe.matmul(PS[4][:, t * E1:(t + 1) * E1], xnT[n][:, t * 128:(t + 1) * 128], L["gw"], start=True, stop=True)
                            if kind == "o":
                                for j in range(HEADS // 2):
                                    for t in range(2):
                                        mm = pe.matmul(PS[4][:, t * 128:(t + 1) * 128], ot[n][:, j, t * 128:(t + 1) * 128],
                                                       L["wout"][:, j * 128:(j + 1) * 128], start=(j == 0 and t == 0),
                                                       stop=(moe and j == HEADS // 2 - 1), skip_group_check=True)
                                if last_layer:
                                    for t in range(2):
                                        mm = pe.matmul(PS[4][:, t * 128:(t + 1) * 128], xnT[n][:, t * 128:(t + 1) * 128], w_eff,
                                                       start=False, stop=True, skip_group_check=True)
                            mm.then_inc(m_f.s, 1)

                    for s in range(STEPS):
                        misc(s, "q")
                        g = s - 1
                        if 0 <= g < NH:
                            pe.wait_ge(m_e.s, m_e.at(i, place["q", g // 2]))
                            pe.wait_ge(s_ex.s, s_ex.at(i, g - 2))
                            bk, q = PS[g % 2], qp[g // 2 % 2]
                            at = g % 2 * 256
                            pe.matmul(bk[:, 0:384], ident16[:, :], mask[:, :], start=True, stop=False, skip_group_check=True)
                            pe.matmul(bk[:, 0:128], q[:, at:at + 128], xnT[g // HEADS][:, 0:128], start=False, stop=True, skip_group_check=True)
                            pe.matmul(bk[:, 128:384], q[:, at + 128:at + 256], xnT[g // HEADS], start=False, stop=True,
                                      skip_group_check=True).then_inc(s_f.s, 1)
                        if moe:
                            for u in range(2 * E1):
                                at = 2 * u + 1 if u < E1 else 2 * u + 5
                                if at == s:
                                    p, e = u // E1, u % E1
                                    pe.wait_ge(f_r.s, f_r.at(i, u - 1))
                                    for c in range(2):
                                        mm = pe.matmul(PS[6][:, c * 256:(c + 1) * 256], L["up"][:, e * HID1 + c * 128:e * HID1 + (c + 1) * 128],
                                                       xnT[p], start=True, stop=True)
                                    mm.then_inc(f_u.s, 1)
                        g = s - 3
                        if 0 <= g < NH:
                            pe.wait_ge(s_nm.s, s_nm.at(i, g))
                            pe.wait_ge(s_te.s, s_te.at(i, g - 2))
                            for c, src in enumerate((0, 1, 2)):
                                mm = pe.transpose(PS[2 + g % 2][:, c * 128:(c + 1) * 128], pr[g % 3][:, src * 128:(src + 1) * 128], ident)
                            mm.then_inc(s_t.s, 1)
                        g = s - 4
                        if 0 <= g < NH:
                            pe.wait_ge(s_te.s, s_te.at(i, g))
                            if g % 2 == 0:
                                pe.wait_ge(s_ot.s, s_ot.at(i, g // 2 - 1))
                            rows_, h, v = slice(64 * (g % 2), 64 * (g % 2) + 64), g % HEADS, v_sb[g // HEADS]
                            pe.matmul(PS[5][rows_, 0:256], v[:, 0, h * HD:(h + 1) * HD], pt[g % 2][:, 0:256], start=True, stop=False, skip_group_check=True)
                            pe.matmul(PS[5][rows_, 128:256], v[:, 1, h * HD:(h + 1) * HD], pt[g % 2][:, 256:384], start=False, stop=True,
                                      skip_group_check=True).then_inc(s_pv.s, 1)
                        misc(s, "tvgo")
                        if moe:
                            for u in range(2 * E1):
                                at = 2 * u + 3 if u < E1 else 2 * u + 7
                                if at == s:
                                    e = u % E1
                                    pe.wait_ge(f_q.s, f_q.at(i, u))
                                    pe.wait_ge(f_x.s, f_x.at(i, u - 1))
                                    for t in range(2):
                                        for c in range(2):
                                            mm = pe.matmul(PS[7][:, t * 128:(t + 1) * 128], h2[u % 2][:, c * 256 + t * 128:c * 256 + (t + 1) * 128],
                                                           L["down"][:, (2 * e + c) * D:(2 * e + c + 1) * D], start=(c == 0), stop=(c == 1))
                                    mm.then_inc(f_d.s, 1)

            def act_(act):
                for n in range(4):
                    act.wait_ge(a_made, n + 1)
                    act.activation(a_t[:, n * 512:(n + 1) * 512], PS[n % 2][:, :], ACT.Copy).then_inc(a_kept, 1)
                act.wait_ge(w_in[qk], 16)
                act.activation(mask[:, :], raw["mask"], ACT.Copy).then_inc(a_kept, 1)
                act.wait_ge(a_kept, 5)
                act.sem_inc(pre, 1)
                act.wait_ge(pre, 2)
                act.wait_ge(m_f.s, m_f.before(0))
                act.activation(xnT[0], PS[4][:, 0:256], ACT.Copy).then_inc(m_e.s, 1)
                with act.Fori(0, PASSES) as i:
                    for s in range(STEPS):
                        for at, kind, n in MISC:
                            if at != s or kind not in "qtg":
                                continue
                            k = place[kind, n]
                            act.wait_ge(m_f.s, m_f.at(i, k))
                            if kind == "q":
                                act.wait_ge(s_f.s, s_f.at(i, 2 * n - 3))
                                act.activation(qp[n % 2], PS[4][:, :], ACT.Copy, scale=HD ** -0.5).then_inc(m_e.s, 1)
                            if kind == "t":
                                act.activation(xnT[n], PS[4][:, 0:256], ACT.Copy).then_inc(m_e.s, 1)
                            if kind == "g":
                                act.wait_ge(g_w.s, g_w.at(i, n - 1))
                                act.activation(ex, PS[4][:, 0:2 * E1].rearrange("p (t e) -> p t e", e=E1), ACT.Exp, scale=-1.0).then_inc(m_e.s, 1)
                        g = s - 1
                        if 0 <= g < NH:
                            act.wait_ge(s_mx.s, s_mx.at(i, g))
                            act.wait_ge(s_t.s, s_t.at(i, g - 3))
                            act.activation(pr[g % 3][:, 0:128], PS[g % 2][:, 0:128], ACT.Exp, bias=nmx[:, g % 3, 0:1], accum_out=sm[:, g % 3, 0:1])
                            act.activation(pr[g % 3][:, 128:384], PS[g % 2][:, 128:384], ACT.Exp, bias=nmx[:, g % 3, 1:2],
                                           accum_out=sm[:, g % 3, 1:2]).then_inc(s_ex.s, 1)
                        if moe:
                            for u in range(2 * E1):
                                at = 2 * u + 1 if u < E1 else 2 * u + 5
                                if at == s:
                                    act.wait_ge(f_u.s, f_u.at(i, u))
                                    act.wait_ge(f_q.s, f_q.at(i, u - 2))
                                    act.activation(h1[u % 2], PS[6][:, :], ACT.Relu).then_inc(f_r.s, 1)
                        g = s - 4
                        if 0 <= g < NH and g % 2 == 1:
                            p, j = g // HEADS, g // 2 % 8
                            act.wait_ge(s_pv.s, s_pv.at(i, g))
                            act.wait_ge(m_f.s, m_f.at(i, place["o", p] - len(MISC)))
                            act.activation(ot[p][:, j, :], PS[5][:, 0:256], ACT.Copy).then_inc(s_ot.s, 1)

            def dve_(dve):
                k = [0, 0]

                def mark(ins):
                    k[0] += 1
                    ins.then_inc(dv.s, 1)

                def settle(i):
                    dve.wait_ge(dv.s, dv.before(k[0] - 1) if i is None else dv.at(i, k[0] - 1))

                def stats(i, tile):
                    for t in range(2):
                        mark(dve.bn_stats(st[:, t, :], x_sb[:, tile + t, :]))

                def moments(i):
                    for t in range(2):
                        mark(dve.bn_aggr(mv[:, t, :], st[:, t, :]))

                def variance(i, p):
                    settle(i)
                    mark(dve.tensor_scalar(ve, mv[:, :, 1], EPS, None, ALU.add))
                    settle(i)
                    dve.sem_inc(ln_v.s, 1)

                def normed(i, tile):
                    for t in range(2):
                        ins = dve.tensor_scalar(xnc[:, t, :], x_sb[:, tile + t, :], mv[:, t, 0:1], rstd[:, t:t + 1], ALU.subtract, ALU.mult)
                    ins.then_inc(ln_x.s, 1)

                def values_out(c):
                    p, t, half_ = c // 4, c // 2 % 2, c % 2
                    return dve.tensor_copy(v_sb[p][:, t, half_ * 512:(half_ + 1) * 512], PS[4][:, :])

                if last_layer:
                    dve.wait_ge(w_in[pack], 16)
                    dve.tensor_reduce(qmax[:, 0:1], L["kernel"], AX, ALU.max, apply_absolute_value=True).then_inc(pre_q, 1)
                    dve.wait_ge(pre_q, 2)
                    dve.tensor_scalar(scl[:, 0:1], qmax[:, 1:2], 1.0 / 7.0, None, ALU.mult).then_inc(pre_q, 1)
                    dve.wait_ge(pre_q, 3)
                    dve.reciprocal(scl[:, 1:2], scl[:, 0:1]).then_inc(pre_q, 1)
                    dve.wait_ge(pre_q, 4)
                    dve.tensor_scalar(w_eff, L["kernel"], scl[:, 1:2], 1.5 * 2 ** 23, ALU.mult, ALU.add).then_inc(pre_q, 1)
                    dve.wait_ge(pre_q, 5)
                    dve.tensor_scalar(w_eff, w_eff, 1.5 * 2 ** 23, -8.0, ALU.subtract, ALU.max).then_inc(pre_q, 1)
                    dve.wait_ge(pre_q, 6)
                    dve.tensor_scalar(w_eff, w_eff, 7.0, scl[:, 0:1], ALU.min, ALU.mult).then_inc(pre_q, 1)
                    dve.wait_ge(pre_q, 7)
                    dve.wait_ge(a_made, 5)
                    dve.tensor_tensor(w_eff, w_eff, PS[2][:, 0:128], ALU.add).then_inc(pre_q, 1)
                    dve.tensor_tensor(brow, L["bias"], L["bo"], ALU.add).then_inc(pre_q, 1)
                    dve.wait_ge(pre_q, 9)
                dve.wait_ge(pre, 1)
                dve.sem_inc(pre, 1)
                stats(None, 0)
                settle(None)
                moments(None)
                variance(None, 0)
                assert k[0] == dv.ahead
                dve.wait_ge(ln_p.s, ln_p.before(0))
                normed(None, 0)
                for c in range(4):
                    dve.wait_ge(m_f.s, m_f.before(c + 1))
                    values_out(c).then_inc(m_e.s, 1)
                with dve.Fori(0, PASSES) as i:
                    k[0] = 0
                    for s in range(STEPS):
                        for p, at in ((1, 0), (0, HEADS)):
                            tile = 4 * i + (2 if p == 1 else 4)
                            if s == at + 2:
                                stats(i, tile)
                                settle(i)
                        g = s - 2
                        if 0 <= g < NH:
                            dve.wait_ge(s_ex.s, s_ex.at(i, g))
                            dve.reciprocal(rc[:, g % 3, :], sm[:, g % 3, :]).then_inc(s_rc.s, 1)
                        for p, at in ((1, 0), (0, HEADS)):
                            if s == at + 2:
                                moments(i)
                        g = s - 1
                        if 0 <= g < NH:
                            dve.wait_ge(s_f.s, s_f.at(i, g))
                            dve.wait_ge(s_ex.s, s_ex.at(i, g - 3))
                            dve.tensor_reduce(nmx[:, g % 3, 0:1], PS[g % 2][:, 0:128], AX, ALU.max, negate=True)
                            dve.tensor_reduce(nmx[:, g % 3, 1:2], PS[g % 2][:, 128:384], AX, ALU.max, negate=True).then_inc(s_mx.s, 1)
                        g = s - 3
                        if 0 <= g < NH:
                            dve.wait_ge(s_t.s, s_t.at(i, g))
                            dve.wait_ge(s_pv.s, s_pv.at(i, g - 2))
                            dve.tensor_copy(pt[g % 2], PS[2 + g % 2][:, 0:384]).then_inc(s_te.s, 1)
                        for p, at in ((1, 0), (0, HEADS)):
                            tile = 4 * i + (2 if p == 1 else 4)
                            if s == at + 3:
                                variance(i, 1 - p)
                            if s == at + 4:
                                dve.wait_ge(ln_p.s, ln_p.at(i, 1 - p))
                                dve.wait_ge(m_f.s, m_f.at(i, place["t", 1 - p] - (len(MISC) if p == 1 else 0)))
                                normed(i, tile)
                        for at, kind, n in MISC:
                            if at != s or kind not in "vgo":
                                continue
                            kk = place[kind, n]
                            if kind == "v":
                                dve.wait_ge(m_f.s, m_f.at(i, kk))
                                dve.wait_ge(s_pv.s, s_pv.at(i, 15 if n < 4 else -1))
                                values_out(n).then_inc(m_e.s, 1)
                            if kind == "g":
                                dve.wait_ge(m_e.s, m_e.at(i, kk))
                                mark(dve.tensor_scalar(sg, ex, 1.0, None, ALU.add)); settle(i)
                                mark(dve.reciprocal(sg, sg)); settle(i)
                                mark(dve.tensor_tensor(bi, sg, spread(L["eb"].unsqueeze(1), 2, E1), ALU.add)); settle(i)
                                other, own = spread(bi.unsqueeze(2), 2, E1, E1), spread(bi.unsqueeze(3), 2, E1, E1)
                                sq = lambda v: v.rearrange("p t (e j) -> p t e j", j=E1)
                                mark(dve.tensor_tensor(sq(cgt), other, own, ALU.is_gt))
                                mark(dve.tensor_tensor(sq(ceq), other, own, ALU.is_equal)); settle(i)
                                mark(dve.tensor_tensor(ceq, ceq, spread(C["tri8"].unsqueeze(1), 2, E1 * E1), ALU.mult)); settle(i)
                                mark(dve.tensor_tensor(cgt, cgt, ceq, ALU.add)); settle(i)
                                mark(dve.tensor_reduce(rk, sq(cgt), AX, ALU.add)); settle(i)
                                dve.wait_ge(f_x.s, f_x.at(i, E1 * n + E1 - 1 - 2 * E1))
                                mark(dve.scalar_tensor_tensor(wt2[n], rk, 1.5, sg, ALU.is_lt, ALU.mult)); settle(i)
                                dve.tensor_tensor(wt2[n], wt2[n], wt2[n], ALU.mult).then_inc(g_w.s, 1)
                            if kind == "o":
                                dve.wait_ge(m_f.s, m_f.at(i, kk))
                                if moe:
                                    dve.wait_ge(f_x.s, f_x.at(i, 7 if n == 0 else 14))
                                else:
                                    dve.wait_ge(ln_b.s, ln_b.at(i, n - 1))
                                tt = bass.ds(4 * i + 2 * n, 2)
                                dve.tensor_tensor(x_sb[:, tt, :], x_sb[:, tt, :], PS[4][:, 0:256].rearrange("p (t d) -> p t d", d=D),
                                                  ALU.add).then_inc(m_e.s, 1)
                        if moe:
                            for u in range(2 * E1):
                                at = 2 * u + 3 if u < E1 else 2 * u + 7
                                if at == s:
                                    p, e = u // E1, u % E1
                                    dve.wait_ge(f_d.s, f_d.at(i, u))
                                    dve.wait_ge(g_w.s, g_w.at(i, p))
                                    dve.wait_ge(f_x.s, f_x.at(i, u - 1))
                                    if u == 2 * E1 - 1:
                                        dve.wait_ge(m_e.s, m_e.at(i, place["o", 1]))
                                    for t in range(2):
                                        ins = dve.scalar_tensor_tensor(x_sb[:, 4 * i + 2 * p + t, :], PS[7][:, t * 128:(t + 1) * 128],
                                                                       wt2[p][:, t, e:e + 1], x_sb[:, 4 * i + 2 * p + t, :], ALU.mult, ALU.add)
                                    ins.then_inc(f_x.s, 1)
                    assert k[0] == dv.n, (k[0], dv.n)


            def pool_(pool):
                if last_layer:
                    pool.wait_ge(pre_q, 1)
                    pool.partition_all_reduce(qmax[:, 1:2], qmax[:, 0:1], 128, bass.bass_isa.ReduceOp.max).then_inc(pre_q, 1)
                    pool.wait_ge(pre_q, 9)

                def power():
                    return pool.tensor_tensor(rstd, ve, half[:, 0:2], ALU.pow)

                def bias(tile):
                    tt = bass.ds(tile, 2)
                    return pool.tensor_tensor(x_sb[:, tt, :], x_sb[:, tt, :], spread(brow.unsqueeze(1), 2, D), ALU.add)

                pool.wait_ge(ln_v.s, ln_v.before(0))
                power().then_inc(ln_p.s, 1)
                if last_layer:
                    pool.wait_ge(ln_x.s, ln_x.before(0))
                    bias(0).then_inc(ln_b.s, 1)
                with pool.Fori(0, PASSES) as i:
                    for s in range(STEPS):
                        g = s - 2
                        if 0 <= g < NH:
                            pool.wait_ge(s_rc.s, s_rc.at(i, g))
                            for q, (c0, c1) in enumerate(((0, 128), (128, 384))):
                                ins = pool.tensor_tensor(pr[g % 3][:, c0:c1], pr[g % 3][:, c0:c1], spread(rc[:, g % 3, q:q + 1], c1 - c0), ALU.mult)
                            ins.then_inc(s_nm.s, 1)
                        for p, at in ((1, 0), (0, HEADS)):
                            if s == at + 3:
                                pool.wait_ge(ln_v.s, ln_v.at(i, 1 - p))
                                power().then_inc(ln_p.s, 1)
                            if s == at + 5 and last_layer:
                                pool.wait_ge(ln_x.s, ln_x.at(i, 1 - p))
                                bias(4 * i + (2 if p == 1 else 4)).then_inc(ln_b.s, 1)
                        if moe:
                            for u in range(2 * E1):
                                at = 2 * u + 2 if u < E1 else 2 * u + 6
                                if at == s:
                                    pool.wait_ge(f_r.s, f_r.at(i, u))
                                    pool.wait_ge(f_d.s, f_d.at(i, u - 2))
                                    pool.tensor_tensor(h2[u % 2], h1[u % 2], h1[u % 2], ALU.mult).then_inc(f_q.s, 1)

            def sp_(sp):
                sp.wait_ge(phase_end, 4 * (phase - 1))
                sp.dma_start(qk_raw, ins[qk]).then_inc(w_in[qk], 16)
                if layer == 1:
                    sp.dma_start(regions["l2"][:, :], ins["l2"]).then_inc(w_in["l2"], 16)
                    sp.dma_start(regions["l3"][:, 0:width("l3")], ins["l3"]).then_inc(w_in["l3"], 16)

            def make16(act):
                if layer == 1:
                    act.activation(ident16[:, :], ident, ACT.Copy).then_inc(a_kept, 1)
                act_(act)

            pe_prog.append(pe_)
            act_prog.append(act_)
            dve_prog.append(dve_)
            pool_prog.append(pool_)
            sp_prog.append(sp_)

        if upto >= 4:
            attention("l1", 1, a1_t, mask1, "l1", "qk1", 4, False)

        def layer2():
            L = W["l2"]
            top[0] = 0
            xnc, st, mv, ve, rstd = carve(4, D), carve(4, 6), carve(4, 2), carve(4), carve(4)
            xnT, qin, rq, qT = carve(512), carve(512), carve(512), carve(512)
            kb = carve(G2, 512)
            v_sb = carve(4, 128)
            vcol, nb2, ed, thr = carve(1), carve(1), carve(4), carve(4, G2)
            mb0 = [carve(512).bitcast(BF16).rearrange("p (g k) -> p g k", k=256) for _ in range(2)]
            mb1 = [carve(256).bitcast(BF16).rearrange("p (g k) -> p g k", k=128) for _ in range(2)]
            pr0, pr1 = [carve(G2, 256) for _ in range(2)], [carve(G2, 128) for _ in range(2)]
            pt = carve(384)
            oT = carve(512)
            nmx, sm, rc = carve(2, 2, G2), carve(2, 2, G2), carve(2, 2, G2)
            sa = carve(512)
            h0, hA, hB = carve(C2, 512), carve(C2, 512), h0_late
            ORDER = ["in", "q", "k", "v", "d", "t", "o"]
            N = len(ORDER)
            place = {n: k for k, n in enumerate(ORDER)}
            m_f, m_e = sig("l2_misc_full", N, 1), sig("l2_misc_empty", N, 1)
            rq_s = sig("l2_relu_in", 1)
            f_ab, f_s, f_h = sig("l2_up", C2), sig("l2_silu", C2), sig("l2_gated", C2)
            f_i, f_ig, f_j, f_jg = sig("l2_mid1", C2), sig("l2_gelu1", C2), sig("l2_mid2", C2), sig("l2_gelu2", C2)
            mb_s, s_f, s_mx, s_ex, s_rc, s_nm = (sig("l2_" + n, 2) for n in ("masks", "scores", "maxima", "exps", "sums", "weights"))
            t_f, t_e, pv, ot = sig("l2_turned", 8), sig("l2_turned_out", 8), sig("l2_values", 8), sig("l2_heads_out", 2)
            ln_v, ln_p, ln_x = sig("l2_variance", 1, 1), sig("l2_rstd", 1, 1), sig("l2_normed", 1, 1)
            dv = sig("l2_dve_order", 4 + 4 + 1 + 3, 9)
            pre, pre_k = sem("l2_pre"), sem("l2_pre_k")

            def pe_(pe):
                pe.wait_ge(w_in["l2"], 16)
                pe.matmul(PS[0][:, 0:1], L["wop"][0:32, :], L["w2c"][0:32, :], start=True, stop=True).then_inc(pre, 1)

                def turn():
                    for t in range(4):
                        mm = pe.transpose(PS[4][:, t * 128:(t + 1) * 128], xnc[:, t, :], ident)
                    mm.then_inc(m_f.s, 1)

                pe.wait_ge(ln_x.s, ln_x.before(0))
                turn()
                pe.wait_ge(pre_k, 2)
                pe.wait_ge(pre, 4)
                with pe.Fori(0, PASSES) as i:
                    def free(n):
                        pe.wait_ge(m_e.s, m_e.at(i, place[n] - 1))

                    def up(c):
                        if c == 0:
                            pe.wait_ge(f_jg.s, f_jg.at(i, -1))
                        pe.wait_ge(f_h.s, f_h.at(i, c - 1))
                        pe.matmul(PS[6][:, :], L["w1"][:, c * 128:(c + 1) * 128], xnT, start=True, stop=True)
                        pe.matmul(PS[7][:, :], L["w2"][:, c * 128:(c + 1) * 128], xnT, start=True, stop=True).then_inc(f_ab.s, 1)

                    def mid(c, w, src, made, out_s, before):
                        pe.wait_ge(before.s, before.at(i, C2 - 1))
                        pe.wait_ge(out_s.s, out_s.at(i, c - 2))
                        for kk in range(C2):
                            mm = pe.matmul(PS[6 + c % 2][:, :], w[:, kk * HID2 + c * 128:kk * HID2 + (c + 1) * 128], src[:, kk, :],
                                           start=(kk == 0), stop=(kk == C2 - 1))
                        mm.then_inc(made.s, 1)

                    def scores(p):
                        pe.wait_ge(mb_s.s, mb_s.at(i, p))
                        pe.wait_ge(s_ex.s, s_ex.at(i, p - 1))
                        for j in range(2):
                            pe.matmul(PS[j][:, :], ident16[:, :], mb0[p][:, 2 * j:2 * j + 2, :].rearrange("p g k -> p (g k)"), start=True, stop=False)
                        pe.matmul(PS[2][:, :], ident16[:, :], mb1[p].rearrange("p g k -> p (g k)"), start=True, stop=False)
                        for j in range(2):
                            pe.matmul(PS[j][:, :], qT[:, p * 256:p * 256 + 128], kb[:, 2 * j:2 * j + 2, p * 256:(p + 1) * 256], start=False, stop=True)
                        pe.matmul(PS[2][:, :], qT[:, p * 256 + 128:(p + 1) * 256], kb[:, :, p * 256 + 128:(p + 1) * 256],
                                  start=False, stop=True).then_inc(s_f.s, 1)

                    def turned(p, g):
                        n = 4 * p + g
                        pe.wait_ge(s_nm.s, s_nm.at(i, p))
                        pe.wait_ge(t_e.s, t_e.at(i, n - 1))
                        for c, src in enumerate((pr0[p][:, g, 128:256], pr1[p][:, g, :], pr0[p][:, g, 0:128])):
                            mm = pe.transpose(PS[3][:, c * 128:(c + 1) * 128], src, ident)
                        mm.then_inc(t_f.s, 1)

                    def values(p, g):
                        n = 4 * p + g
                        pe.wait_ge(t_e.s, t_e.at(i, n))
                        if g == 0:
                            pe.wait_ge(ot.s, ot.at(i, p - 1))
                        r = slice(DH2 * g, DH2 * (g + 1))
                        pe.matmul(PS[5][r, 0:256], v_sb[:, 2 * p + 1, r], pt[:, 0:256], start=True, stop=False, skip_group_check=True)
                        pe.matmul(PS[5][r, 0:128], v_sb[:, 2 * p, r], pt[:, 256:384], start=False, stop=True,
                                  skip_group_check=True).then_inc(pv.s, 1)

                    free("in")
                    pe.matmul(PS[4][:, :], L["wq"], xnT, start=True, stop=True).then_inc(m_f.s, 1)
                    up(0)
                    up(1)
                    free("q")
                    pe.matmul(PS[4][:, :], L["wqkv"][:, 0:128], qin, start=True, stop=True).then_inc(m_f.s, 1)
                    up(2)
                    free("k")
                    pe.matmul(PS[4][:, :], L["wqkv"][:, 128:256], qin, start=True, stop=True).then_inc(m_f.s, 1)
                    up(3)
                    free("v")
                    for t in range(4):
                        mm = pe.matmul(PS[4][:, t * 128:(t + 1) * 128], qin[:, t * 128:(t + 1) * 128], L["wqkv"][:, 256:384], start=True, stop=True)
                    mm.then_inc(m_f.s, 1)
                    pe.wait_ge(rq_s.s, rq_s.at(i, 0))
                    free("d")
                    for t in range(4):
                        mm = pe.matmul(PS[4][:, t:t + 1], rq[:, t * 128:(t + 1) * 128], vcol, start=True, stop=True)
                    mm.then_inc(m_f.s, 1)
                    mid1 = lambda c: mid(c, L["h1"], h0, f_i, f_ig, f_h)
                    mid2 = lambda c: mid(c, L["h2"], hA, f_j, f_jg, f_ig)
                    mid1(0)
                    scores(0)
                    mid1(1)
                    scores(1)
                    fill = [lambda: mid1(2), lambda: mid1(3), lambda: mid2(0), lambda: mid2(1), lambda: mid2(2), lambda: mid2(3)]
                    for p in range(2):
                        for g in range(G2):
                            turned(p, g)
                            if fill:
                                fill.pop(0)()
                            values(p, g)
                    pe.wait_ge(ln_x.s, ln_x.at(i, 0))
                    free("t")
                    turn()
                    pe.wait_ge(f_jg.s, f_jg.at(i, C2 - 1))
                    pe.wait_ge(ot.s, ot.at(i, 1))
                    free("o")
                    for t in range(4):
                        cs = slice(t * 128, (t + 1) * 128)
                        for c in range(C2):
                            pe.matmul(PS[4][:, cs], hB[:, c, cs], L["w3"][:, c * 128:(c + 1) * 128], start=(t == 0 and c == 0), stop=False, skip_group_check=True)
                        mm = pe.matmul(PS[4][:, cs], oT[:, cs], ident, start=False, stop=True, skip_group_check=True)
                    mm.then_inc(m_f.s, 1)

            def act_(act):
                act.wait_ge(m_f.s, m_f.before(0))
                act.activation(xnT, PS[4][:, :], ACT.Copy).then_inc(m_e.s, 1)
                act.wait_ge(pre_k, 2)
                with act.Fori(0, PASSES) as i:
                    def silu(c):
                        act.wait_ge(f_ab.s, f_ab.at(i, c))
                        act.wait_ge(f_h.s, f_h.at(i, c - 1))
                        act.activation(sa, PS[6][:, :], ACT.Silu, scale=L["s1"][:, c:c + 1]).then_inc(f_s.s, 1)

                    act.wait_ge(m_f.s, m_f.at(i, place["in"]))
                    act.wait_ge(rq_s.s, rq_s.at(i, 0))
                    act.activation(qin, PS[4][:, :], ACT.Copy).then_inc(m_e.s, 1)
                    silu(0)
                    silu(1)
                    silu(2)
                    act.wait_ge(m_f.s, m_f.at(i, place["k"]))
                    for g in range(G2):
                        r = slice(DH2 * g, DH2 * (g + 1))
                        ins_ = act.activation(kb[r, g, :], PS[4][r, :], ACT.Identity, bias=L["bk"][r, :])
                    ins_.then_inc(m_e.s, 1)
                    silu(3)
                    act.wait_ge(m_f.s, m_f.at(i, place["v"]))
                    act.wait_ge(pv.s, pv.at(i, -1))
                    act.activation(v_sb.rearrange("p t d -> p (t d)"), PS[4][:, :], ACT.Copy).then_inc(m_e.s, 1)
                    act.wait_ge(m_f.s, m_f.at(i, place["d"]))
                    act.activation(ed, PS[4][:, 0:4], ACT.Exp, scale=-1.0, bias=nb2).then_inc(m_e.s, 1)
                    for p in range(2):
                        act.wait_ge(s_mx.s, s_mx.at(i, p))
                        act.wait_ge(t_f.s, t_f.at(i, 4 * p + 3 - 8))
                        for g in range(G2):
                            act.activation(pr0[p][:, g, :], PS[g // 2][:, g % 2 * 256:(g % 2 + 1) * 256], ACT.Exp, bias=nmx[:, p, 0, g:g + 1],
                                           accum_out=sm[:, p, 0, g:g + 1])
                        for g in range(G2):
                            ins_ = act.activation(pr1[p][:, g, :], PS[2][:, g * 128:(g + 1) * 128], ACT.Exp, bias=nmx[:, p, 1, g:g + 1],
                                                  accum_out=sm[:, p, 1, g:g + 1])
                        ins_.then_inc(s_ex.s, 1)

                    def gelu(c, dst, scale, made, out_s):
                        act.wait_ge(made.s, made.at(i, c))
                        act.activation(dst[:, c, :], PS[6 + c % 2][:, :], ACT.Gelu, scale=scale[:, c:c + 1]).then_inc(out_s.s, 1)

                    for c in range(C2):
                        if c == 0:
                            act.wait_ge(f_j.s, f_j.at(i, -1))
                        gelu(c, hA, L["hs1"], f_i, f_ig)
                    for c in range(C2):
                        if c == 0:
                            act.wait_ge(m_f.s, m_f.at(i, place["o"] - N))
                        if c == 2:
                            head_out(act, i, 0)
                        gelu(c, hB, L["hs2"], f_j, f_jg)
                    head_out(act, i, 1)
                    act.wait_ge(m_f.s, m_f.at(i, place["t"]))
                    act.activation(xnT, PS[4][:, :], ACT.Copy).then_inc(m_e.s, 1)

            def head_out(act, i, p):
                act.wait_ge(pv.s, pv.at(i, 4 * p + 3))
                act.activation(oT[:, p * 256:(p + 1) * 256], PS[5][:, 0:256], ACT.Identity, bias=L["bv"]).then_inc(ot.s, 1)

            def dve_(dve):
                k = [0]

                def mark(ins):
                    k[0] += 1
                    ins.then_inc(dv.s, 1)

                def settle(i):
                    dve.wait_ge(dv.s, dv.before(k[0] - 1) if i is None else dv.at(i, k[0] - 1))

                def stats(i, tile):
                    for t in range(4):
                        mark(dve.bn_stats(st[:, t, :], x_sb[:, tile + t, :]))
                    settle(i)

                def moments():
                    for t in range(4):
                        mark(dve.bn_aggr(mv[:, t, :], st[:, t, :]))

                def variance(i):
                    settle(i)
                    mark(dve.tensor_scalar(ve, mv[:, :, 1], EPS, None, ALU.add))
                    settle(i)
                    dve.sem_inc(ln_v.s, 1)

                def normed(tile):
                    for t in range(4):
                        ins_ = dve.tensor_scalar(xnc[:, t, :], x_sb[:, tile + t, :], mv[:, t, 0:1], rstd[:, t:t + 1], ALU.subtract, ALU.mult)
                    ins_.then_inc(ln_x.s, 1)

                stats(None, 0)
                moments()
                variance(None)
                assert k[0] == dv.ahead
                dve.wait_ge(ln_p.s, ln_p.before(0))
                normed(0)
                dve.wait_ge(w_in["l2"], 16)
                dve.wait_ge(pre, 1)
                dve.tensor_copy(vcol, PS[0][:, 0:1]).then_inc(pre, 1)
                dve.tensor_scalar(nb2, L["b2"], -1.0, None, ALU.mult).then_inc(pre, 1)
                w3 = L["w3"].rearrange("p (c d) -> p c d", d=D)
                dve.tensor_tensor(w3, w3, spread(L["s3"].unsqueeze(1), C2, D), ALU.mult).then_inc(pre, 1)
                dve.wait_ge(pre, 4)
                dve.sem_inc(pre_k, 1)
                with dve.Fori(0, PASSES) as i:
                    k[0] = 0

                    def gated(c):
                        dve.wait_ge(f_s.s, f_s.at(i, c))
                        if c == 0:
                            dve.wait_ge(f_i.s, f_i.at(i, -1))
                        dve.scalar_tensor_tensor(h0[:, c, :], PS[7][:, :], L["s2"][:, c:c + 1], sa, ALU.mult, ALU.mult).then_inc(f_h.s, 1)

                    dve.wait_ge(m_f.s, m_f.at(i, place["in"]))
                    dve.tensor_scalar(rq, PS[4][:, :], 0.0, None, ALU.max).then_inc(rq_s.s, 1)
                    gated(0)
                    gated(1)
                    dve.wait_ge(m_f.s, m_f.at(i, place["q"]))
                    dve.tensor_scalar(qT, PS[4][:, :], L["bq"], 2.0 / S ** 0.5, ALU.add, ALU.mult).then_inc(m_e.s, 1)
                    gated(2)
                    gated(3)
                    dve.wait_ge(m_e.s, m_e.at(i, place["d"]))
                    mark(dve.tensor_scalar(ed, ed, 1.0, None, ALU.add)); settle(i)
                    mark(dve.reciprocal(ed, ed)); settle(i)
                    mark(dve.scalar_tensor_tensor(thr, spread(ed.unsqueeze(2), 4, G2), float(S), spread(C["win"].unsqueeze(1), 4, G2), ALU.mult, ALU.add))
                    settle(i)
                    for p in range(2):
                        for g in range(G2):
                            dve.tensor_scalar(mb0[p][:, g, :], C["dist"], thr[:, 2 * p, g:g + 1], MASKED, ALU.is_gt, ALU.mult)
                            ins_ = dve.tensor_scalar(mb1[p][:, g, :], C["dist"][:, 0:128], thr[:, 2 * p + 1, g:g + 1], MASKED, ALU.is_gt, ALU.mult)
                        ins_.then_inc(mb_s.s, 1)
                    tile = 4 * i + 4
                    stats(i, tile)
                    for p in range(2):
                        dve.wait_ge(s_f.s, s_f.at(i, p))
                        for j in range(2):
                            dve.tensor_reduce(nmx[:, p, 0, 2 * j:2 * j + 2], PS[j][:, :].rearrange("p (g k) -> p g k", k=256), AX, ALU.max, negate=True)
                        dve.tensor_reduce(nmx[:, p, 1, :], PS[2][:, :].rearrange("p (g k) -> p g k", k=128), AX, ALU.max, negate=True).then_inc(s_mx.s, 1)
                        if p == 0:
                            moments()
                            variance(i)
                        dve.wait_ge(s_ex.s, s_ex.at(i, p))
                        dve.reciprocal(rc[:, p, :, :], sm[:, p, :, :]).then_inc(s_rc.s, 1)
                    dve.wait_ge(ln_p.s, ln_p.at(i, 0))
                    normed(tile)
                    for n in range(8):
                        dve.wait_ge(t_f.s, t_f.at(i, n))
                        dve.wait_ge(pv.s, pv.at(i, n - 1))
                        dve.tensor_copy(pt, PS[3][:, 0:384]).then_inc(t_e.s, 1)
                    dve.wait_ge(m_f.s, m_f.at(i, place["o"]))
                    tt = bass.ds(4 * i, 4)
                    dve.tensor_tensor(x_sb[:, tt, :], x_sb[:, tt, :], PS[4][:, :].rearrange("p (t d) -> p t d", d=D), ALU.add).then_inc(m_e.s, 1)
                    assert k[0] == dv.n, (k[0], dv.n)

            def pool_(pool):
                pool.memset(kb, 0.0).then_inc(pre_k, 1)
                pool.wait_ge(ln_v.s, ln_v.before(0))
                pool.tensor_tensor(rstd, ve, half[:, 0:4], ALU.pow).then_inc(ln_p.s, 1)
                with pool.Fori(0, PASSES) as i:
                    for p in range(2):
                        if p == 1:
                            pool.wait_ge(ln_v.s, ln_v.at(i, 0))
                            pool.tensor_tensor(rstd, ve, half[:, 0:4], ALU.pow).then_inc(ln_p.s, 1)
                        pool.wait_ge(s_rc.s, s_rc.at(i, p))
                        pool.tensor_tensor(pr0[p], pr0[p], spread(rc[:, p, 0, :].unsqueeze(2), G2, 256), ALU.mult)
                        pool.tensor_tensor(pr1[p], pr1[p], spread(rc[:, p, 1, :].unsqueeze(2), G2, 128), ALU.mult).then_inc(s_nm.s, 1)

            pe_prog.append(pe_)
            act_prog.append(act_)
            dve_prog.append(dve_)
            pool_prog.append(pool_)

        h0_late = regions["l1"][:, 0:C2 * 512].rearrange("p (c t) -> p c t", t=512)
        if upto >= 5:
            layer2()
        if upto >= 9:
            attention("l3", 3, a3_t, mask3, "l3", "qk3", 6, True)
        def sp_store(sp):
            sp.wait_ge(phase_end, 4 * (len(pe_prog)))
            sp.dma_start(out_v, x_sb[:, 0:TILES, :]).then_inc(stored, 16)
            sp.wait_ge(stored, 16)

        block = ctx.enter_context(nc.Block())

        def run(eng, prog):
            for n, phase in enumerate(prog):
                phase(eng)
                close(eng, n + 1)

        @block.sync
        def _(sp):
            for phase in sp_prog:
                phase(sp)
            sp_store(sp)

        @block.tensor
        def _(pe):
            run(pe, pe_prog)

        @block.scalar
        def _(act):
            run(act, act_prog)

        @block.vector
        def _(dve):
            run(dve, dve_prog)

        @block.gpsimd
        def _(pool):
            run(pool, pool_prog)


def lay_out(a):
    f = np.float32
    P = np.arange(128)

    def pad(m):
        z = np.zeros((128, m.shape[1]), f)
        z[:m.shape[0]] = m
        return z

    def col(v):
        return pad(v.reshape(-1, 1))

    def rows(v):
        return np.repeat(v.reshape(1, -1), 128, axis=0)

    def chunks(m):
        return m.reshape(-1, 128, m.shape[1]).transpose(1, 0, 2).reshape(128, -1)

    def cols(v):
        return v.reshape(-1, 128).T

    tok = np.arange(S)
    flat = np.arange(HCH * 128).reshape(HCH, 128)
    be = np.arange(128)
    c = {
        "ident": np.eye(128), "blockones": be[:, None] % E0 == be[None, :] % E0,
        "lowerblk": (be[:, None] % E0 == be[None, :] % E0) & (be[:, None] // E0 < be[None, :] // E0),
        "dist": np.where(tok[None, :] < P[:, None], FAR, tok[None, :] - P[:, None]),
        "iota": np.repeat(np.arange(128)[None], 128, axis=0), "pidx": P[:, None],
        "tileno": rows(np.repeat(2 * np.arange(B)[None, :] + np.arange(2)[:, None], E0, axis=1)),
        "tri": np.concatenate([tok[None, :] < (n * 128 + P)[:, None] for n in range(2)], axis=1),
        "headmask": P[:, None] // HD0 == np.arange(H0)[None, :],
        "vmask": (flat.T[:, :, None] // KPAD == P[None, None, :] // HD0).reshape(128, -1),
        "tri8": np.repeat((np.arange(8)[None, :] < np.arange(8)[:, None]).reshape(1, 64), 128, axis=0),
        "win": rows(np.array(WINDOWS)),
    }
    l0 = {k + "T": a["L0_attn_" + k].T for k in ("wq", "wk", "wv", "wo", "wi1")}
    l0 |= {"wi2rep": pad(np.repeat(a["L0_attn_wi2"].T, 128, axis=1)), "bi1": col(a["L0_attn_bi1"]),
           "bi2": rows(a["L0_attn_bi2"]), "bo": rows(a["L0_attn_bo"]), "wg": a["L0_ffn_wg"]}
    l0 |= {k: col(a["L0_attn_" + k]) for k in ("bq", "bk", "bv")}
    f0 = {k: a["L0_ffn_" + k].transpose(1, 0, 2).reshape(128, -1) for k in ("w1", "w3")}
    f0["w2"] = chunks(a["L0_ffn_w2"].reshape(-1, D))
    l1 = {"wv": a["L1_attn_w_qkv"][:, 2048:], "wout": chunks(a["L1_attn_w_out"]),
          "up": a["L1_ffn_w_up"].transpose(2, 0, 1).reshape(128, -1),
          "down": chunks(a["L1_ffn_w_down"].transpose(0, 2, 1).reshape(-1, D)),
          "gw": a["L1_ffn_gate_w"].T, "eb": rows(a["L1_ffn_expert_bias"])}

    def per_head(w):
        return pad(w.reshape(D, HEADS, HD).transpose(2, 1, 0).reshape(HD, -1))

    q, j = np.arange(S)[:, None], np.arange(S)[None, :]
    causal = j <= q
    near = (j >= q - 16) & (j <= q + 16)
    ok1 = (near | (j < 64) | (q < 64)) & causal

    def masks(ok):
        m = np.where(ok, 0.0, MASKED)
        return np.concatenate([m[:128, :128], m[128:, :]], axis=1)

    qk1 = {"wqT": per_head(a["L1_attn_w_qkv"][:, :1024]), "wkT": per_head(a["L1_attn_w_qkv"][:, 1024:2048]), "mask": masks(ok1)}
    qk3 = {"wqT": per_head(a["L3_attn_Wq"]), "wkT": per_head(a["L3_attn_Wk"]), "mask": masks(causal)}
    bqkv = a["L2_attn_bqkv"]
    l2 = {"wq": a["L2_attn_Wq"].T, "wqkv": a["L2_attn_Wqkv"].T, "wop": pad(a["L2_attn_Wop"]), "w2c": col(a["L2_attn_W2"]),
          "b2": rows(a["L2_attn_b2"]), "bq": col(bqkv[:128]), "bk": col(bqkv[128:256]), "bv": col(bqkv[256:]),
          "w1": a["L2_ffn_w1_w"].T, "w2": a["L2_ffn_w2_w"].T, "h1": chunks(a["L2_ffn_h1_w"].T), "h2": chunks(a["L2_ffn_h2_w"].T),
          "w3": chunks(a["L2_ffn_w3_w"].T), "s1": cols(a["L2_ffn_w1_s"]), "s2": cols(a["L2_ffn_w2_s"]),
          "hs1": cols(a["L2_ffn_h1_s"]), "hs2": cols(a["L2_ffn_h2_s"]), "s3": rows(a["L2_ffn_w3_s"])}
    l3 = {"wv": a["L3_attn_Wv"], "wout": chunks(a["L3_attn_Wo"]), "kernel": a["L3_ffn_kernel"], "bias": rows(a["L3_ffn_bias"]),
          "bo": rows(a["L3_attn_bo"]), "aT": pad(a["L3_ffn_a"].T), "b": pad(a["L3_ffn_b"])}
    all_ = {"const": c, "l0": l0, "f0": f0, "l1": l1, "l2": l2, "l3": l3, "qk1": qk1, "qk3": qk3}
    got = {"x": a["L0_attn_x"]}
    for p, parts in PACKS.items():
        got[p] = np.ascontiguousarray(np.concatenate([np.asarray(all_[p][n], f) for n, _ in parts], axis=1))
        assert got[p].shape == (128, width(p)), p
    return got


def kernel(**inputs):
    import concourse.bacc as _bacc
    from concourse.bass_utils import run_bass_kernel_spmd as _run

    arrays = lay_out({k: np.asarray(v) for k, v in inputs.items()})
    nc = _bacc.Bacc("TRN2", target_bir_lowering=False, num_devices=1)
    ins = {n: nc.dram_tensor(f"in_{n}", v.shape, mybir.dt.float32, kind="ExternalInput").ap() for n, v in arrays.items()}
    out = nc.dram_tensor("out_x", (B, S, D), mybir.dt.float32, kind="ExternalOutput").ap()
    program(nc, ins, out)
    r = _run(nc, [{f"in_{n}": v for n, v in arrays.items()}], core_ids=[0])
    return r.results[0]["out_x"]
```

```python
import numpy as np

import concourse.bass as bass
from concourse import mybir
from contextlib import ExitStack

B, S, D = 16, 256, 128
TILES = B * S // 128
PASSES = B // 2
H0, HD0 = 16, 8
KEEP = int(S * 0.3)
KPAD = 80
HCH = H0 * KPAD // 128
E0, CAP, HID0 = 8, 512, 256
ROW = D + E0
HEADS, HD = 16, 64
E1, HID1 = 8, 256
G2, DH2 = 4, 32
WINDOWS = (32.0, 64.0, 128.0, 256.0)
HID2 = 512
C2 = HID2 // 128
EPS = 1e-5
MASKED = -1e30
FAR = 1e18

PACKS = {
    "const": [("ident", 128), ("blockones", 128), ("lowerblk", 128), ("dist", 256), ("iota", 128),
              ("tileno", 256), ("pidx", 1), ("tri", 512), ("headmask", H0), ("vmask", HCH * 128), ("tri8", 64), ("win", G2)],
    "l0": [("wqT", 128), ("wkT", 128), ("wvT", 128), ("woT", 128), ("wi1T", 64), ("wi2rep", 128),
           ("bq", 1), ("bk", 1), ("bv", 1), ("bi1", 1), ("bi2", 1), ("bo", 128), ("wg", E0)],
    "f0": [("w1", E0 * HID0), ("w3", E0 * HID0), ("w2", E0 * HID0)],
    "l1": [("wv", 1024), ("wout", 1024), ("up", E1 * HID1), ("down", E1 * HID1), ("gw", E1), ("eb", E1)],
    "l2": [("wq", 128), ("wqkv", 384), ("wop", 128), ("w2c", 1), ("b2", 1), ("bq", 1), ("bk", 1), ("bv", 1),
           ("w1", HID2), ("w2", HID2), ("h1", C2 * HID2), ("h2", C2 * HID2), ("w3", HID2),
           ("s1", C2), ("s2", C2), ("hs1", C2), ("hs2", C2), ("s3", 128)],
    "l3": [("wv", 1024), ("wout", 1024), ("kernel", 128), ("bias", 128), ("bo", 128), ("aT", 128), ("b", 128)],
    "qk1": [("wqT", 1024), ("wkT", 1024), ("mask", 384)],
    "qk3": [("wqT", 1024), ("wkT", 1024), ("mask", 384)],
}
LOADS = (("const", "l0"), ("f0",), ("l1",), ("l2", "l3"), ("qk1", "qk3"))


def width(pack):
    return sum(n for _, n in PACKS[pack])


class Sig:

    def __init__(self, nc, ctx, name, n, ahead=0):
        self.s, self.n, self.ahead = ctx.enter_context(nc.semaphore(name)), n, ahead

    def at(self, i, k):
        return i * self.n + (self.n + self.ahead + k + 1)

    def before(self, k):
        return self.n + k + 1

    def end(self):
        return self.n + self.ahead + PASSES * self.n


def program(nc, ins, out, upto=9):
    F32, BF16, U32, I32 = mybir.dt.float32, mybir.dt.bfloat16, mybir.dt.uint32, mybir.dt.int32
    ALU, ACT, AX = mybir.AluOpType, mybir.ActivationFunctionType, mybir.AxisListType.X
    ctx = ExitStack()
    with ctx:
        address = {}

        def sb(name, cols, dt=F32):
            made = ctx.enter_context(nc.sbuf_tensor(name, [128, cols], dt))
            if dt == F32:
                address[name] = nc.sbuf_base - 4 * cols
            return made

        def rounded(name, array, start, *shape):
            n = int(np.prod(shape))
            v = nc.alloc_sbuf_tensor_at(name, [128, n], mybir.dt.float32r, offset=address[array] + 4 * start, align_bytes=4)[:, :]
            return v.rearrange("p (a b) -> p a b", b=shape[1]) if len(shape) == 2 else v

        sigs = []

        def sig(name, n, ahead=0):
            sigs.append(Sig(nc, ctx, name, n, ahead))
            return sigs[-1]

        def sem(name):
            return ctx.enter_context(nc.semaphore(name))

        def views(region, pack):
            got, at = {}, 0
            for name, n in PACKS[pack]:
                got[name] = region[:, at:at + n]
                at += n
            return got

        x_t = sb("x_sb", (TILES + 4) * D)
        x_sb = x_t[:, :].rearrange("p (t d) -> p t d", d=D)
        regions = {p: sb("w_" + p, width(p)) for p in ("const", "l0", "f0", "l1", "l2")}
        regions["l3"] = regions["f0"]
        W = {p: views(regions[p], p) for p in ("const", "l0", "f0", "l1", "l2", "l3")}
        qk_t = sb("qk", 2 * HEADS * 128)
        a1_t, a3_t = qk_t[:, 0:HEADS * 128], qk_t[:, HEADS * 128:]
        mask1, mask3 = sb("mask1", 384, BF16), sb("mask3", 384, BF16)
        ident16 = sb("ident16", 128, BF16)
        half, one = sb("minus_half", 32), sb("one", 1)
        work = sb("work", 17400)
        PS = [ctx.enter_context(nc.psum_tensor(f"bank{j}", [128, 512], F32)) for j in range(8)]
        C = W["const"]
        ident = C["ident"]
        top = [0]

        def carve(*shape):
            n = int(np.prod(shape))
            v = work[:, top[0]:top[0] + n]
            top[0] += n
            assert top[0] <= 17400, top[0]
            if len(shape) == 2:
                v = v.rearrange("p (a b) -> p a b", b=shape[1])
            if len(shape) == 3:
                v = v.rearrange("p (a b c) -> p a b c", b=shape[1], c=shape[2])
            return v

        def spread(ap, *shape):
            return ap.to_broadcast([128, *shape])

        def copy(pool, dst, src):
            return pool.tensor_tensor(dst, src, spread(one[:, :].unsqueeze(2), *src.shape[1:]), ALU.mult)

        x_in, w_in, w_all = sem("x_in"), {}, {}
        for packs in LOADS:
            for p in packs:
                w_in[p], w_all[p] = (sem("in_" + "_".join(packs)) if p == packs[0] else w_in[packs[0]]), 16 * len(packs)
        phase_end = sem("phase_end")
        stored = sem("stored")
        rows_d = nc.dram_tensor("normed_rows", (B * S, ROW), F32, kind="Internal").ap()
        res_d = nc.dram_tensor("residual", (B * S, D), F32, kind="Internal").ap()
        rows_v, res_v = (d.rearrange("(t p) c -> p t c", p=128) for d in (rows_d, res_d))
        rows_out = sem("rows_out")
        out_v = out.rearrange("b (i p) d -> p (b i) d", p=128)

        def close(eng, n):
            eng.drain().then_inc(phase_end, 1)
            eng.wait_ge(phase_end, 4 * n)

        pe_prog, act_prog, dve_prog, pool_prog, sp_prog = [], [], [], [], []

        top[0] = 0
        xn_all = carve(TILES + 6, D)
        sc_nat = carve(2, B, E0)
        keep_scores = top[0]
        scT = carve(2, 128)
        keep_work = top[0]
        st_all, mv_all = carve(TILES, 6), carve(TILES, 2)
        ve_all, rstd_all = carve(TILES), carve(TILES)
        xn4, xnT4 = [carve(4, D) for _ in range(2)], [carve(512) for _ in range(2)]
        lg_all, ex_all = carve(TILES, E0), carve(TILES, E0)
        mx_all, sm_all, rc_all = carve(TILES), carve(TILES), carve(TILES)
        g_set = sem("g_set")
        g_stat, g_var, g_pow = sem("g_stat"), sem("g_var"), sem("g_pow")
        g_xn, g_saved, g_tr, g_xnT, g_lg, g_lgs = (sig("g_" + n, 2) for n in (
            "normed", "saved", "turned", "turned_out", "logits", "logits_out"))
        G_LAST = TILES // 8 - 1
        g_sm, g_ex, g_sct = sem("g_sm"), sem("g_ex"), sem("g_sct")
        bo0 = W["l0"]["bo"]

        def sp_load(sp):
            for s in sigs:
                sp.sem_inc(s.s, s.n)
            xv = ins["x"].rearrange("b (i p) d -> p (b i) d", p=128)
            for c in range(4):
                sp.dma_start(x_sb[:, 8 * c:8 * c + 8, :], xv[:, 8 * c:8 * c + 8, :]).then_inc(x_in, 16)
            for p in ("const", "l0", "f0", "l1"):
                sp.dma_start(regions[p][:, :], ins[p]).then_inc(w_in[p], 16)

        def sp_rows(sp):
            sp.wait_ge(g_saved.s, g_saved.at(G_LAST, 1))
            sp.dma_start(rows_v[:, :, 0:D], xn_all[:, 0:TILES, :]).then_inc(rows_out, 16)
            sp.wait_ge(g_sm, 6)
            for n in range(2):
                sp.dma_start(rows_v.rearrange("p (b i) c -> p i b c", i=2)[:, n, :, D:ROW], sc_nat[:, n, :, :]).then_inc(rows_out, 16)
            sp.wait_ge(rows_out, 48)

        def pool_gates(pool):
            pool.memset(x_sb[:, TILES:, :], 0.0).then_inc(g_set, 1)
            pool.memset(half[:, :], -0.5).then_inc(g_set, 1)
            pool.memset(one[:, :], 1.0).then_inc(g_set, 1)
            pool.wait_ge(g_set, 3)
            pool.wait_ge(g_var, 1)
            pool.tensor_tensor(rstd_all, ve_all, half[:, :], ALU.pow).then_inc(g_pow, 1)
            with pool.Fori(0, TILES // 8) as i:
                for h in range(2):
                    pool.wait_ge(g_xn.s, g_xn.at(i, h))
                    copy(pool, xn_all[:, bass.ds(8 * i + 4 * h, 4), :], xn4[h]).then_inc(g_saved.s, 1)

        def dve_gates(dve):
            dve.wait_ge(x_in, 64)
            with dve.Fori(0, TILES // 8) as i:
                for t in range(8):
                    dve.bn_stats(st_all[:, 8 * i + t, :], x_sb[:, 8 * i + t, :]).then_inc(g_stat, 1)
            dve.wait_ge(g_stat, TILES)
            for t in range(TILES):
                dve.bn_aggr(mv_all[:, t, :], st_all[:, t, :]).then_inc(g_stat, 1)
            dve.wait_ge(g_stat, 2 * TILES)
            dve.tensor_scalar(ve_all, mv_all[:, :, 1], EPS, None, ALU.add).then_inc(g_var, 1)
            dve.wait_ge(g_pow, 1)
            with dve.Fori(0, TILES // 8) as i:
                for h in range(2):
                    dve.wait_ge(g_tr.s, g_tr.at(i, h - 2))
                    dve.wait_ge(g_saved.s, g_saved.at(i, h - 2))
                    for k in range(4):
                        t = 8 * i + 4 * h + k
                        last = dve.tensor_scalar(xn4[h][:, k, :], x_sb[:, t, :], mv_all[:, t, 0:1],
                                                 rstd_all[:, bass.ds(t, 1)], ALU.subtract, ALU.mult)
                    last.then_inc(g_xn.s, 1)
                for h in range(2):
                    dve.wait_ge(g_lg.s, g_lg.at(i, h))
                    dve.tensor_copy(lg_all[:, bass.ds(8 * i + 4 * h, 4), :],
                                    PS[2 + h][:, 0:4 * E0].rearrange("p (t e) -> p t e", e=E0)).then_inc(g_lgs.s, 1)
            dve.wait_ge(g_lgs.s, g_lgs.at(G_LAST, 1))
            dve.tensor_reduce(mx_all, lg_all, AX, ALU.max).then_inc(g_sm, 1)
            dve.wait_ge(g_sm, 1)
            dve.tensor_tensor(lg_all, lg_all, spread(mx_all.unsqueeze(2), TILES, E0), ALU.subtract).then_inc(g_sm, 1)
            dve.wait_ge(g_ex, 1)
            dve.tensor_reduce(sm_all, ex_all, AX, ALU.add).then_inc(g_sm, 1)
            dve.wait_ge(g_sm, 3)
            dve.reciprocal(rc_all, sm_all).then_inc(g_sm, 1)
            dve.wait_ge(g_sm, 4)
            for n in range(2):
                dve.tensor_tensor(sc_nat[:, n, :, :], ex_all.rearrange("p (b i) e -> p i b e", i=2)[:, n, :, :],
                                  spread(rc_all.rearrange("p (b i) -> p i b", i=2)[:, n, :].unsqueeze(2), B, E0),
                                  ALU.mult).then_inc(g_sm, 1)
            dve.wait_ge(g_sct, 1)
            dve.tensor_copy(scT, PS[0][:, 0:256].rearrange("p (i t) -> p i t", i=2)).then_inc(g_sm, 1)

        def act_gates(act):
            with act.Fori(0, TILES // 8) as i:
                for h in range(2):
                    act.wait_ge(g_tr.s, g_tr.at(i, h))
                    act.wait_ge(g_lg.s, g_lg.at(i, h - 2))
                    act.activation(xnT4[h], PS[h][:, :], ACT.Copy).then_inc(g_xnT.s, 1)
            act.wait_ge(g_sm, 2)
            act.activation(ex_all, lg_all, ACT.Exp).then_inc(g_ex, 1)
            act.activation(ident16[:, :], ident, ACT.Copy).then_inc(g_ex, 1)

        def pe_gates(pe):
            pe.wait_ge(w_in["const"], w_all["const"])
            pe.wait_ge(w_in["l0"], w_all["l0"])
            with pe.Fori(0, TILES // 8) as i:
                for h in range(2):
                    pe.wait_ge(g_xn.s, g_xn.at(i, h))
                    pe.wait_ge(g_xnT.s, g_xnT.at(i, h - 2))
                    for k in range(4):
                        last = pe.transpose(PS[h][:, k * 128:(k + 1) * 128], xn4[h][:, k, :], ident)
                    last.then_inc(g_tr.s, 1)
                for h in range(2):
                    pe.wait_ge(g_xnT.s, g_xnT.at(i, h))
                    pe.wait_ge(g_lgs.s, g_lgs.at(i, h - 2))
                    for k in range(4):
                        last = pe.matmul(PS[2 + h][:, k * E0:(k + 1) * E0], xnT4[h][:, k * 128:(k + 1) * 128], W["l0"]["wg"],
                                         start=True, stop=True)
                    last.then_inc(g_lg.s, 1)
            pe.wait_ge(g_sm, 6)
            pe.wait_ge(g_xnT.s, g_xnT.at(G_LAST, 1))
            for n in range(2):
                last = pe.transpose(PS[0][:, n * 128:(n + 1) * 128], sc_nat[:, n, :, :].rearrange("p b e -> p (b e)"), ident)
            last.then_inc(g_sct, 1)

        sp_prog.append(sp_load)
        sp_prog.append(sp_rows)
        pe_prog.append(pe_gates)
        act_prog.append(act_gates)
        dve_prog.append(dve_gates)
        pool_prog.append(pool_gates)

        SEARCH = 2
        top[0] = keep_work
        xnc = [carve(2, D) for _ in range(2)]
        xnT = [carve(256) for _ in range(2)]
        qT, hT = [carve(256) for _ in range(2)], [carve(256) for _ in range(2)]
        row = [carve(256) for _ in range(2)]
        junk, junk2 = carve(256), carve(256)
        impc, cnt, rank = carve(2, 2), carve(2, 4), carve(2, 2)
        sel = [carve(2, KEEP) for _ in range(2)]
        xselT, kselT = [carve(KEEP) for _ in range(2)], [carve(KEEP) for _ in range(2)]
        xselR = [carve(H0, KPAD) for _ in range(2)]
        kblk = [carve(H0, KEEP) for _ in range(2)]
        early = regions["l2"]
        vblk = [early[:, p * HCH * 128:(p + 1) * HCH * 128].rearrange("p (c d) -> p c d", d=128) for p in range(2)]
        p0_flat = [qk_t[:, n * H0 * KPAD:(n + 1) * H0 * KPAD].rearrange("p (h k) -> p h k", k=KPAD) for n in range(3)]
        P0 = [[p0_flat[0], p0_flat[1]], [p0_flat[2], carve(H0, KPAD)]]
        PT0 = early[:, 2 * HCH * 128:4 * HCH * 128].rearrange("p (c q) -> p c q", q=256)
        oT0 = [carve(256) for _ in range(2)]
        mx0, sm0, rc0 = carve(4, H0), carve(4, H0), carve(4, H0)
        t_bits, c_bits, bit, kept, cnt_e = carve(1), carve(1), carve(1), carve(1), carve(1)
        u32 = lambda ap: ap.bitcast(U32)
        SEL, SOFT, FIND = 10, 16, 5 * SEARCH
        per = {}

        def batch_sig(name, m):
            s = sig(name, 2 * m)
            per[s] = m
            return s

        def of(s, i, c, k=0):
            return s.s, s.at(i, c * per[s] + k)

        a_xnc, a_tr, a_xnT, a_q, a_qe, a_h, a_he, a_imp, a_row, a_sel, a_xs, a_xse, a_xr, a_ks, a_kse, a_kb, a_vb, a_vbe, a_o, a_oe, a_out, a_x, a_bias = (
            batch_sig("a_" + n, 1) for n in (
                "rows", "turned", "turned_out", "queries", "queries_out", "hidden", "hidden_out", "importance", "importance_out", "kept", "kept_rows",
                "kept_rows_out", "kept_spread", "keys", "keys_out", "key_blocks", "value_blocks", "value_blocks_out",
                "heads", "heads_out", "output", "added", "biased"))
        a_s, a_sub, a_exp, a_rc, a_nm = (batch_sig("a_" + n, 2) for n in ("scores", "shifted", "exps", "sums", "weights"))
        a_pt, a_pte = batch_sig("a_weights_turned", 5), batch_sig("a_weights_turned_out", 5)
        a_dsel, a_dsoft, a_dfind = batch_sig("a_sel_order", SEL), batch_sig("a_softmax_order", SOFT), batch_sig("a_search_order", FIND)
        a_find, a_found = batch_sig("a_find", SEARCH), batch_sig("a_found", SEARCH)
        a_set, a_bits = sem("a_set"), sem("a_bits")
        HGROUPS = ((0, 6), (6, 11), (11, 16))
        VGROUPS = ((0, 4, 7), (4, 8, 6), (8, 10, 4))

        def run_steps(eng, step, tail):
            for p in range(2):
                step(0, p, p > 0)
            with eng.Fori(1, PASSES) as i:
                for p in range(2):
                    step(i, p, True)
            tail(PASSES, -1)

        def pool_attn0(pool):
            for p in range(2):
                pool.memset(xselR[p][:, :, KEEP:], 0.0).then_inc(a_set, 1)
                for q in range(2):
                    pool.memset(P0[p][q][:, :, KEEP:], 0.0).then_inc(a_set, 1)
            pool.memset(xn_all[:, TILES:, :], 0.0).then_inc(a_set, 1)
            pool.wait_ge(a_set, 7)

            def rows_(i, c):
                pool.wait_ge(*of(a_xs, i, c - 2))
                copy(pool, xnc[c % 2], xn_all[:, bass.ds(4 * i + 2 * c, 2), :]).then_inc(a_xnc.s, 1)

            def spread_rows(i, c):
                pool.wait_ge(*of(a_xse, i, c))
                pool.wait_ge(*of(a_vb, i, c - 2))
                copy(pool, xselR[c % 2][:, :, 0:KEEP], spread(xselT[c % 2].unsqueeze(1), H0, KEEP)).then_inc(a_xr.s, 1)

            def key_blocks(i, c):
                pool.wait_ge(*of(a_kse, i, c))
                pool.wait_ge(*of(a_s, i, c - 2, 1))
                pool.tensor_tensor(kblk[c % 2], spread(kselT[c % 2].unsqueeze(1), H0, KEEP),
                                   spread(C["headmask"].unsqueeze(2), H0, KEEP), ALU.mult).then_inc(a_kb.s, 1)

            def weights(i, c, q):
                w = P0[c % 2][q][:, :, 0:KEEP]
                pool.wait_ge(*of(a_rc, i, c, q))
                pool.tensor_tensor(w, w, spread(rc0[:, 2 * q + c % 2, :].unsqueeze(2), H0, KEEP), ALU.mult).then_inc(a_nm.s, 1)

            def biased(i, c):
                tt = bass.ds(4 * i + 2 * c, 2)
                pool.tensor_tensor(x_sb[:, tt, :], x_sb[:, tt, :], spread(bo0.unsqueeze(1), 2, D), ALU.add).then_inc(a_bias.s, 1)

            def step(i, p, back):
                biased(i, p)
                spread_rows(i, p + 1)
                rows_(i, p + 3)
                key_blocks(i, p + 1)
                weights(i, p, 0)
                weights(i, p, 1)

            rows_(0, 0)
            rows_(0, 1)
            spread_rows(0, 0)
            key_blocks(0, 0)
            rows_(0, 2)
            run_steps(pool, step, lambda i, c: None)

        def act_attn0(act):
            L = W["l0"]

            def turned_out(i, c):
                act.wait_ge(*of(a_tr, i, c))
                act.wait_ge(*of(a_q, i, c - 2))
                act.activation(xnT[c % 2], PS[6][:, 0:256], ACT.Copy).then_inc(a_xnT.s, 1)

            def hidden_out(i, c):
                act.wait_ge(*of(a_h, i, c))
                act.wait_ge(*of(a_imp, i, c - 2))
                act.activation(hT[c % 2][0:64, :], PS[7][0:64, 256:512], ACT.Relu, bias=L["bi1"][0:64, :]).then_inc(a_he.s, 1)

            def queries_out(i, c):
                act.wait_ge(*of(a_q, i, c))
                act.wait_ge(*of(a_s, i, c - 2, 1))
                act.activation(qT[c % 2], PS[6][:, 256:512], ACT.Identity, bias=L["bq"]).then_inc(a_qe.s, 1)

            def kept_out(i, c):
                act.wait_ge(*of(a_xs, i, c))
                act.wait_ge(*of(a_xr, i, c - 2))
                act.activation(xselT[c % 2], PS[7][:, 0:KEEP], ACT.Copy).then_inc(a_xse.s, 1)

            def keys_out(i, c):
                act.wait_ge(*of(a_ks, i, c))
                act.wait_ge(*of(a_kb, i, c - 2))
                act.activation(kselT[c % 2], PS[7][:, 128:128 + KEEP], ACT.Identity, bias=L["bk"]).then_inc(a_kse.s, 1)

            def exps(i, c, q):
                w = P0[c % 2][q][:, :, 0:KEEP]
                act.wait_ge(*of(a_sub, i, c, q))
                act.activation(w, w, ACT.Exp, scale=float(1 / np.sqrt(HD0))).then_inc(a_exp.s, 1)

            def weights_out(i, c):
                for j in range(5):
                    act.wait_ge(*of(a_pt, i, c, j))
                    if j == 0:
                        act.wait_ge(*of(a_o, i, c - 1))
                    act.activation(PT0[:, 2 * j:2 * j + 2, :].rearrange("p c t -> p (c t)"), PS[3 + j % 2][:, :], ACT.Copy).then_inc(a_pte.s, 1)

            def heads_out(i, c):
                act.wait_ge(*of(a_o, i, c))
                act.wait_ge(*of(a_out, i, c - 2))
                act.activation(oT0[c % 2], PS[5][:, 0:256], ACT.Identity, bias=L["bv"]).then_inc(a_oe.s, 1)

            def step(i, p, back):
                turned_out(i, p + 2)
                kept_out(i, p + 1)
                queries_out(i, p + 1)
                hidden_out(i, p + 2)
                if back:
                    weights_out(i, p - 1)
                keys_out(i, p + 1)
                exps(i, p, 0)
                exps(i, p, 1)
                if back:
                    heads_out(i, p - 1)

            def tail(i, c):
                weights_out(i, c)
                heads_out(i, c)

            turned_out(0, 0)
            hidden_out(0, 0)
            turned_out(0, 1)
            kept_out(0, 0)
            queries_out(0, 0)
            hidden_out(0, 1)
            keys_out(0, 0)
            run_steps(act, step, tail)

        def dve_attn0(dve):
            L = W["l0"]

            def link(s, i, c, k, ins):
                ins.then_inc(s.s, 1)
                dve.wait_ge(*of(s, i, c, k))

            def count(i, c, n):
                lk = lambda k, ins: link(a_dfind, i, c, 5 * n + k, ins)
                lk(0, dve.tensor_tensor(u32(c_bits), u32(t_bits), u32(bit), ALU.bitwise_or))
                lk(1, dve.tensor_scalar(junk2, scT.rearrange("p i t -> p (i t)"), c_bits, 0.0, ALU.is_ge, ALU.add, accum_out=cnt_e))
                dve.sem_inc(a_find.s, 1)

            def decide(i, c, n):
                lk = lambda k, ins: link(a_dfind, i, c, 5 * n + k, ins)
                dve.wait_ge(*of(a_found, i, c, n))
                lk(2, dve.scalar_tensor_tensor(u32(kept), PS[3 + 2 * n][:, 511:512], CAP - 0.5, u32(bit), ALU.is_ge, ALU.mult))
                lk(3, dve.tensor_tensor(u32(t_bits), u32(t_bits), u32(kept), ALU.bitwise_or))
                lk(4, dve.tensor_scalar(u32(bit), u32(bit), 1, None, ALU.logical_shift_right))

            def importance_out(i, c):
                dve.wait_ge(*of(a_imp, i, c))
                dve.tensor_scalar(row[c % 2], PS[6][:, 0:256], L["bi2"], None, ALU.add).then_inc(a_row.s, 1)

            def keep(i, c):
                p = c % 2
                dve.wait_ge(*of(a_row, i, c))
                dve.wait_ge(*of(a_xs, i, c - 2))
                for n in range(2):
                    lk = lambda k, ins: link(a_dsel, i, c, 5 * n + k, ins)
                    own = impc[:, p, n:n + 1]
                    lk(0, dve.scalar_tensor_tensor(junk[:, 0:128], row[p][:, n * 128:(n + 1) * 128], 1.0, ident,
                                                   ALU.mult, ALU.mult, accum_out=own))
                    lk(1, dve.tensor_scalar(junk, row[p], own, 0.0, ALU.is_gt, ALU.add, accum_out=cnt[:, p, 2 * n:2 * n + 1]))
                    lk(2, dve.scalar_tensor_tensor(junk, row[p], own, C["tri"][:, n * 256:(n + 1) * 256],
                                                   ALU.is_equal, ALU.mult, accum_out=cnt[:, p, 2 * n + 1:2 * n + 2]))
                    lk(3, dve.tensor_tensor(rank[:, p, n:n + 1], cnt[:, p, 2 * n:2 * n + 1], cnt[:, p, 2 * n + 1:2 * n + 2], ALU.add))
                    lk(4, dve.tensor_scalar(sel[p][:, n, :], C["iota"][:, 0:KEEP], rank[:, p, n:n + 1], None, ALU.is_equal))
                dve.sem_inc(a_sel.s, 1)

            def value_blocks_out(i, c):
                dve.wait_ge(*of(a_vb, i, c))
                dve.wait_ge(*of(a_o, i, c - 2))
                for c0, c1, bk in VGROUPS:
                    last = dve.tensor_tensor(vblk[c % 2][:, c0:c1, :].rearrange("p c d -> p (c d)"),
                                             PS[bk][:, 0:(c1 - c0) * 128], C["vmask"][:, c0 * 128:c1 * 128], ALU.mult)
                last.then_inc(a_vbe.s, 1)

            def shifted(i, c, q):
                m = 2 * q + c % 2
                lk = lambda k, ins: link(a_dsoft, i, c, 8 * q + k, ins)
                dve.wait_ge(*of(a_s, i, c, q))
                dve.wait_ge(*of(a_pt, i, c - 2, 4))
                scores = [PS[j][:, 0:(h1 - h0) * KEEP].rearrange("p (h k) -> p h k", k=KEEP) for j, (h0, h1) in enumerate(HGROUPS)]
                for j, (h0, h1) in enumerate(HGROUPS):
                    dve.tensor_reduce(mx0[:, m, h0:h1], scores[j], AX, ALU.max).then_inc(a_dsoft.s, 1)
                for j, (h0, h1) in enumerate(HGROUPS):
                    dve.wait_ge(*of(a_dsoft, i, c, 8 * q + j))
                    last = dve.tensor_tensor(P0[c % 2][q][:, h0:h1, 0:KEEP], scores[j], spread(mx0[:, m, h0:h1].unsqueeze(2), h1 - h0, KEEP), ALU.subtract)
                    if j < 2:
                        last.then_inc(a_dsoft.s, 1)
                last.then_inc(a_sub.s, 1)
                dve.sem_inc(a_dsoft.s, 1)

            def sums(i, c, q):
                m = 2 * q + c % 2
                dve.wait_ge(*of(a_exp, i, c, q))
                link(a_dsoft, i, c, 8 * q + 6, dve.tensor_reduce(sm0[:, m, :], P0[c % 2][q][:, :, 0:KEEP], AX, ALU.add))
                dve.reciprocal(rc0[:, m, :], sm0[:, m, :]).then_inc(a_rc.s, 1)
                dve.sem_inc(a_dsoft.s, 1)

            def added(i, c):
                tt = bass.ds(4 * i + 2 * c, 2)
                dve.wait_ge(*of(a_out, i, c))
                dve.wait_ge(*of(a_bias, i, c))
                dve.tensor_tensor(x_sb[:, tt, :], x_sb[:, tt, :], PS[5][:, 256:512].rearrange("p (t d) -> p t d", d=D), ALU.add).then_inc(a_x.s, 1)

            def step(i, p, back):
                shifted(i, p, 0)
                if back:
                    decide(i, p - 1, 1)
                count(i, p, 0)
                importance_out(i, p + 2)
                sums(i, p, 0)
                shifted(i, p, 1)
                decide(i, p, 0)
                keep(i, p + 2)
                value_blocks_out(i, p + 1)
                sums(i, p, 1)
                count(i, p, 1)
                if back:
                    added(i, p - 1)

            def tail(i, c):
                decide(i, c, 1)
                added(i, c)

            dve.wait_ge(g_sm, 7)
            dve.memset(u32(t_bits), 0).then_inc(a_bits, 1)
            dve.memset(u32(bit), 1 << 29).then_inc(a_bits, 1)
            dve.wait_ge(a_bits, 2)
            for c in range(2):
                importance_out(0, c)
                keep(0, c)
            value_blocks_out(0, 0)
            run_steps(dve, step, tail)

        def pe_attn0(pe):
            L = W["l0"]

            def search(i, c, n):
                pe.wait_ge(*of(a_find, i, c, n))
                pe.wait_ge(*(of(a_x, i, c - 1) if n else of(a_pte, i, c - 1, 4)))
                pe.matmul(PS[3 + 2 * n][:, 511:512], C["blockones"], cnt_e, start=True, stop=True).then_inc(a_found.s, 1)

            def turn(i, c):
                pe.wait_ge(*of(a_xnc, i, c))
                pe.wait_ge(*of(a_vbe, i, c - 2))
                pe.wait_ge(*of(a_row, i, c - 1))
                for n in range(2):
                    last = pe.transpose(PS[6][:, n * 128:(n + 1) * 128], xnc[c % 2][:, n, :], ident)
                last.then_inc(a_tr.s, 1)

            def hidden(i, c):
                pe.wait_ge(*of(a_xnT, i, c))
                pe.wait_ge(*of(a_xse, i, c - 1))
                pe.matmul(PS[7][0:64, 256:512], L["wi1T"], xnT[c % 2], start=True, stop=True).then_inc(a_h.s, 1)

            def importance(i, c):
                pe.wait_ge(*of(a_he, i, c))
                pe.wait_ge(*of(a_qe, i, c - 1))
                pe.matmul(PS[6][:, 0:256], L["wi2rep"][0:64, :], hT[c % 2][0:64, :], start=True, stop=True).then_inc(a_imp.s, 1)

            def queries(i, c):
                pe.wait_ge(*of(a_xnT, i, c))
                pe.wait_ge(*of(a_xnT, i, c + 1))
                pe.matmul(PS[6][:, 256:512], L["wqT"], xnT[c % 2], start=True, stop=True).then_inc(a_q.s, 1)

            def kept_rows(i, c):
                pe.wait_ge(*of(a_sel, i, c))
                pe.wait_ge(*of(a_vbe, i, c - 1))
                for n in range(2):
                    last = pe.matmul(PS[7][:, 0:KEEP], xnc[c % 2][:, n, :], sel[c % 2][:, n, :], start=(n == 0), stop=(n == 1))
                last.then_inc(a_xs.s, 1)

            def keys(i, c):
                pe.wait_ge(*of(a_xse, i, c))
                pe.wait_ge(*of(a_he, i, c + 1))
                pe.matmul(PS[7][:, 128:128 + KEEP], L["wkT"], xselT[c % 2], start=True, stop=True).then_inc(a_ks.s, 1)

            def value_blocks(i, c):
                pe.wait_ge(*of(a_xr, i, c))
                pe.wait_ge(*of(a_kse, i, c))
                pe.wait_ge(*of(a_qe, i, c))
                pe.wait_ge(*of(a_he, i, c + 1))
                pe.wait_ge(*of(a_row, i, c + 1))
                pe.wait_ge(*of(a_pte, i, c - 2, 4))
                for c0, c1, bk in VGROUPS:
                    for j in range(c0, c1):
                        last = pe.matmul(PS[bk][:, (j - c0) * 128:(j - c0 + 1) * 128],
                                         xselR[c % 2].rearrange("p h k -> p (h k)")[:, j * 128:(j + 1) * 128], L["wvT"], start=True, stop=True)
                last.then_inc(a_vb.s, 1)

            def scores(i, c, q):
                if q == 0:
                    pe.wait_ge(*of(a_kb, i, c))
                    pe.wait_ge(*of(a_qe, i, c))
                    pe.wait_ge(*of(a_sub, i, c - 1, 1))
                else:
                    pe.wait_ge(*of(a_sub, i, c, 0))
                for j, (h0, h1) in enumerate(HGROUPS):
                    last = pe.matmul(PS[j][:, 0:(h1 - h0) * KEEP], qT[c % 2][:, q * 128:(q + 1) * 128],
                                     kblk[c % 2][:, h0:h1, :].rearrange("p h k -> p (h k)"), start=True, stop=True)
                last.then_inc(a_s.s, 1)

            def weights_turned(i, c):
                for q in range(2):
                    pe.wait_ge(*of(a_nm, i, c, q))
                pe.wait_ge(*of(a_vbe, i, c + 1))
                pe.wait_ge(*of(a_dfind, i, c, FIND // 2 - 1))
                for j in range(5):
                    pe.wait_ge(*of(a_pte, i, c, j - 2))
                    for k in range(2):
                        for q in range(2):
                            last = pe.transpose(PS[3 + j % 2][:, k * 256 + q * 128:k * 256 + (q + 1) * 128],
                                                P0[c % 2][q].rearrange("p h k -> p (h k)")[:, (2 * j + k) * 128:(2 * j + k + 1) * 128], ident)
                    last.then_inc(a_pt.s, 1)

            def heads(i, c):
                pe.wait_ge(*of(a_pte, i, c, 4))
                pe.wait_ge(*of(a_vbe, i, c))
                pe.wait_ge(*of(a_x, i, c - 1))
                pe.wait_ge(*of(a_dfind, i, c, FIND - 1))
                for j in range(HCH):
                    last = pe.matmul(PS[5][:, 0:256], vblk[c % 2][:, j, :], PT0[:, j, :], start=(j == 0), stop=(j == HCH - 1))
                last.then_inc(a_o.s, 1)

            def output(i, c):
                pe.wait_ge(*of(a_oe, i, c))
                for n in range(2):
                    last = pe.matmul(PS[5][:, 256 + n * 128:256 + (n + 1) * 128], oT0[c % 2][:, n * 128:(n + 1) * 128], L["woT"], start=True, stop=True)
                last.then_inc(a_out.s, 1)

            def step(i, p, back):
                scores(i, p, 0)
                turn(i, p + 2)
                if back:
                    search(i, p - 1, 1)
                kept_rows(i, p + 1)
                queries(i, p + 1)
                hidden(i, p + 2)
                if back:
                    weights_turned(i, p - 1)
                keys(i, p + 1)
                importance(i, p + 2)
                scores(i, p, 1)
                search(i, p, 0)
                value_blocks(i, p + 1)
                if back:
                    heads(i, p - 1)
                if back:
                    output(i, p - 1)

            def tail(i, c):
                search(i, c, 1)
                weights_turned(i, c)
                heads(i, c)
                output(i, c)

            pe.wait_ge(a_set, 7)
            turn(0, 0)
            hidden(0, 0)
            importance(0, 0)
            turn(0, 1)
            kept_rows(0, 0)
            queries(0, 0)
            hidden(0, 1)
            keys(0, 0)
            importance(0, 1)
            value_blocks(0, 0)
            run_steps(pe, step, tail)

        if upto >= 2:
            pe_prog.append(pe_attn0)
            act_prog.append(act_attn0)
            dve_prog.append(dve_attn0)
            pool_prog.append(pool_attn0)
        else:
            for prog in (pe_prog, act_prog, dve_prog, pool_prog):
                prog.append(lambda eng: None)

        top[0] = 0
        CT = CAP // 128
        xg = carve(E0 * CT, ROW)
        assert top[0] <= keep_scores, top[0]
        top[0] = keep_work
        ones256, eq, gt, cum = carve(256), carve(256), carve(256), carve(256)
        eqn, allow, offs, ngt, total, first = (carve(1) for _ in range(6))
        pos, hi = carve(256), carve(256)
        eq4 = carve(256, CT)
        lo16 = carve(128).bitcast(BF16).rearrange("p (i b e) -> p i b e", b=B, e=E0)
        lists16 = carve(128 * CT * 2).bitcast(BF16).rearrange("p (j k w) -> p j k w", k=CT, w=2)
        lists_rhs = lists16.rearrange("p (i b e) k w -> p i b e (k w)", b=B, e=E0)
        iota16, zero16 = carve(64).bitcast(BF16), carve(64).bitcast(BF16)
        oh = [carve(E0 * 64).bitcast(BF16).rearrange("p (e s) -> p e s", s=128) for _ in range(2)]
        idx = carve(E0 * CT).bitcast(U32)
        xs = [carve(CT, D) for _ in range(2)]
        xeT = [carve(512) for _ in range(2)]
        sa = [carve(512) for _ in range(2)]
        hh = [carve(2, 512) for _ in range(2)]
        y = [carve(CT, D) for _ in range(2)]
        b_set, b_dv, b_cnt, b_selT, b_idx = sem("b_set"), sem("b_dv"), sem("b_cnt"), sem("b_selT"), sem("b_idx")
        b_oh, b_ohu = sig("b_onehot", 2), sig("b_onehot_used", 2)
        b_got = [sem(f"b_got{e}") for e in range(3)]
        b_acc, b_added, x_back = sem("b_acc"), sem("b_added"), sem("x_back")
        b_xs, b_tr, b_xe, b_up, b_sa, b_g, b_dn, b_y = (sem("b_" + n) for n in ("scaled", "turned", "turned_out", "up", "silu", "gated", "down", "y"))
        qk_raw = {qk: regions["l2"][:, n * width(qk):(n + 1) * width(qk)] for n, qk in enumerate(("qk1", "qk3"))}
        qk_jobs = (("qk1", a1_t, mask1), ("qk3", a3_t, mask3))
        qk_made, qk_kept = sem("qk_made"), sem("qk_kept")
        scT_f = scT.rearrange("p i t -> p (i t)")

        def dve_ffn0(dve):
            k = [0]

            def link(ins):
                k[0] += 1
                ins.then_inc(b_dv, 1)
                dve.wait_ge(b_dv, k[0])

            link(dve.memset(ones256, 1.0))
            link(dve.memset(zero16, 0.0))
            link(dve.tensor_copy(iota16, C["iota"]))
            link(dve.tensor_scalar(gt, scT_f, t_bits, 0.0, ALU.is_gt, ALU.add, accum_out=ngt))
            link(dve.tensor_scalar(eq, scT_f, t_bits, None, ALU.is_equal))
            link(dve.tensor_tensor_scan(cum, ones256, eq, 0.0, ALU.mult, ALU.add))
            link(dve.tensor_copy(eqn, cum[:, 255:256]))
            dve.sem_inc(b_set, 1)
            dve.wait_ge(b_cnt, 2)
            link(dve.tensor_scalar(allow, PS[0][:, 0:1], -1.0, float(CAP), ALU.mult, ALU.add))
            link(dve.tensor_tensor(offs, allow, PS[1][:, 0:1], ALU.subtract))
            link(dve.scalar_tensor_tensor(eq, cum, offs, eq, ALU.is_le, ALU.mult))
            link(dve.tensor_tensor(gt, gt, eq, ALU.add))
            link(dve.tensor_tensor_scan(cum, ones256, gt, 0.0, ALU.mult, ALU.add))
            link(dve.tensor_copy(total, cum[:, 255:256]))
            dve.sem_inc(b_set, 1)
            dve.wait_ge(b_cnt, 3)
            link(dve.tensor_copy(first, PS[2][:, 0:1]))
            link(dve.scalar_tensor_tensor(cum, cum, first, gt, ALU.add, ALU.mult))
            link(dve.tensor_scalar(cum, cum, -1.0, None, ALU.add))
            dve.sem_inc(b_set, 1)
            dve.wait_ge(b_selT, 1)
            link(dve.tensor_copy(pos, PS[0][:, 0:256]))
            link(dve.tensor_scalar(hi, pos, 128.0, None, ALU.is_ge))
            for c in range(2, CT):
                link(dve.scalar_tensor_tensor(hi, pos, 128.0 * c, hi, ALU.is_ge, ALU.add))
            link(dve.scalar_tensor_tensor(lo16.rearrange("p i b e -> p (i b e)"), hi, -128.0, pos, ALU.mult, ALU.add))
            link(dve.tensor_tensor(eq4, spread(hi.unsqueeze(2), 256, CT), spread(C["iota"][:, 0:CT].unsqueeze(1), 256, CT), ALU.is_equal))
            link(dve.tensor_tensor(lists16[:, :, :, 0], eq4, spread(C["tileno"].unsqueeze(2), 256, CT), ALU.mult))
            link(dve.tensor_scalar(lists16[:, :, :, 1], eq4, C["pidx"], None, ALU.mult))
            dve.sem_inc(b_set, 1)
            with dve.Fori(0, B) as b:
                for n in range(2):
                    dve.wait_ge(b_ohu.s, b_ohu.at(b, n - 2))
                    dve.tensor_tensor(oh[n], spread(lo16[:, n, b, :].unsqueeze(2), E0, 128), spread(iota16.unsqueeze(1), E0, 128),
                                      ALU.is_equal).then_inc(b_oh.s, 1)
            dve.wait_ge(b_ohu.s, 2 * B + 2)
            dve.wait_ge(b_cnt, 4)
            sums = PS[2][:, 0:E0 * CT * 2].rearrange("p (j w) -> p j w", w=2)
            link(dve.tensor_copy(pos[:, 0:E0 * CT], sums[:, :, 0]))
            dve.scalar_tensor_tensor(idx, pos[:, 0:E0 * CT], 128.0, sums[:, :, 1], ALU.mult, ALU.add).then_inc(b_idx, 1)

            def scaled(e):
                dve.wait_ge(b_got[e % 3], 16 * CT * (e // 3 + 1))
                if e >= 2:
                    dve.wait_ge(b_tr, e - 1)
                for t in range(CT):
                    r = xg[:, CT * e + t, :]
                    last = dve.tensor_scalar(xs[e % 2][:, t, :], r[:, 0:D], r[:, D + e:D + e + 1], None, ALU.mult)
                last.then_inc(b_xs, 1)

            def out_(e):
                dve.wait_ge(b_dn, e + 1)
                if e >= 2:
                    dve.wait_ge(b_added, 16 * CT * (e - 1))
                dve.tensor_copy(y[e % 2].rearrange("p t d -> p (t d)"), PS[6 + e % 2][:, :]).then_inc(b_y, 1)

            scaled(0)
            for e in range(E0):
                if e + 1 < E0:
                    scaled(e + 1)
                for c in range(2):
                    u = 2 * e + c
                    dve.wait_ge(b_sa, u + 1)
                    dve.wait_ge(b_up, u + 1)
                    if e >= 2:
                        dve.wait_ge(b_dn, e - 1)
                    dve.tensor_tensor(hh[e % 2][:, c, :], sa[c], PS[4 + c][:, :], ALU.mult).then_inc(b_g, 1)
                if e >= 1:
                    out_(e - 1)
            out_(E0 - 1)
            dve.wait_ge(x_back, 64)

        def pool_ffn0(pool):
            pool.wait_ge(b_idx, 1)
            pool.wait_ge(rows_out, 48)
            slot = lambda e, t: bass.IndirectOffsetOnAxis(ap=idx[:, CT * e + t:CT * e + t + 1], axis=0)
            for e in range(E0):
                if e >= 3:
                    pool.wait_ge(b_got[e % 3], 16 * CT * (e // 3))
                for t in range(CT):
                    pool.indirect_dma_start(xg[:, CT * e + t, :], None, rows_d, slot(e, t)).then_inc(b_got[e % 3], 16)
            pool.wait_ge(b_acc, 16)
            for e in range(E0):
                pool.wait_ge(b_y, e + 1)
                if e:
                    pool.wait_ge(b_added, 16 * CT * e)
                for t in range(CT):
                    pool.indirect_dma_start(res_d, slot(e, t), y[e % 2][:, t, :], None, compute_op=ALU.add).then_inc(b_added, 16)

        def sp_ffn0(sp):
            sp.wait_ge(phase_end, 4 * 2)
            sp.dma_start(res_v, x_sb[:, 0:TILES, :]).then_inc(b_acc, 16)
            for qk, _, _ in qk_jobs:
                sp.dma_start(qk_raw[qk], ins[qk]).then_inc(w_in[qk], 16)
            sp.wait_ge(b_added, 16 * CT * E0)
            for c in range(4):
                sp.dma_start(x_sb[:, 8 * c:8 * c + 8, :], res_v[:, 8 * c:8 * c + 8, :]).then_inc(x_back, 16)

        def act_ffn0(act):
            def evac(e):
                act.wait_ge(b_tr, e + 1)
                if e >= 2:
                    act.wait_ge(b_up, 2 * e - 2)
                act.activation(xeT[e % 2], PS[e % 2][:, :], ACT.Copy).then_inc(b_xe, 1)

            def keep_a(n):
                qk, a_t, mask = qk_jobs[n]
                act.wait_ge(w_in[qk], w_all[qk])
                act.activation(mask[:, :], views(qk_raw[qk], qk)["mask"], ACT.Copy)
                for j in range(HEADS // 4):
                    act.wait_ge(qk_made, 4 * n + j + 1)
                    act.activation(a_t[:, j * 512:(j + 1) * 512], PS[4 + j % 2][:, :], ACT.Copy).then_inc(qk_kept, 1)

            keep_a(0)
            evac(0)
            for e in range(E0):
                if e + 1 < E0:
                    evac(e + 1)
                for c in range(2):
                    u = 2 * e + c
                    act.wait_ge(b_up, u + 1)
                    if u >= 2:
                        act.wait_ge(b_g, u - 1)
                    act.activation(sa[c], PS[2 + c][:, :], ACT.Silu).then_inc(b_sa, 1)
            keep_a(1)

        def pe_ffn0(pe):
            F = W["f0"]

            def make_a(n):
                qk = qk_jobs[n][0]
                raw = views(qk_raw[qk], qk)
                pe.wait_ge(w_in[qk], w_all[qk])
                for h in range(HEADS):
                    j = 4 * n + h // 4
                    if h % 4 == 0 and j >= 2:
                        pe.wait_ge(qk_kept, j - 1)
                    half_, at = slice(64 * (h // 8), 64 * (h // 8) + 64), h % 8 * 128
                    mm = pe.matmul(PS[4 + j % 2][:, h % 4 * 128:(h % 4 + 1) * 128], raw["wqT"][half_, at:at + 128],
                                   raw["wkT"][half_, at:at + 128], start=True, stop=True)
                    if h % 4 == 3:
                        mm.then_inc(qk_made, 1)

            pe.wait_ge(w_in["f0"], w_all["f0"])
            pe.wait_ge(b_set, 1)
            pe.matmul(PS[0][:, 0:1], C["blockones"], ngt, start=True, stop=True).then_inc(b_cnt, 1)
            pe.matmul(PS[1][:, 0:1], C["lowerblk"], eqn, start=True, stop=True).then_inc(b_cnt, 1)
            pe.wait_ge(b_set, 2)
            pe.matmul(PS[2][:, 0:1], C["lowerblk"], total, start=True, stop=True).then_inc(b_cnt, 1)
            pe.wait_ge(b_set, 3)
            for n in range(2):
                last = pe.transpose(PS[0][:, n * 128:(n + 1) * 128], cum[:, n * 128:(n + 1) * 128], ident)
            last.then_inc(b_selT, 1)
            pe.wait_ge(b_set, 4)
            pe.matmul(PS[2][:, 0:E0 * CT * 2], zero16, zero16[:, 0:E0 * CT * 2], start=True, stop=False, skip_group_check=True)
            with pe.Fori(0, B) as b:
                for n in range(2):
                    pe.wait_ge(b_oh.s, b_oh.at(b, n))
                    for e in range(E0):
                        last = pe.matmul(PS[2][:, e * CT * 2:(e + 1) * CT * 2], oh[n][:, e, :], lists_rhs[:, n, b, e, :],
                                         start=False, stop=False, skip_group_check=True)
                    last.then_inc(b_ohu.s, 1)
            pe.matmul(PS[2][:, 0:E0 * CT * 2], zero16, zero16[:, 0:E0 * CT * 2], start=False, stop=True,
                      skip_group_check=True).then_inc(b_cnt, 1)

            def turn(e):
                pe.wait_ge(b_xs, e + 1)
                if e >= 2:
                    pe.wait_ge(b_xe, e - 1)
                for t in range(CT):
                    last = pe.transpose(PS[e % 2][:, t * 128:(t + 1) * 128], xs[e % 2][:, t, :], ident)
                last.then_inc(b_tr, 1)

            def down(e):
                pe.wait_ge(b_g, 2 * e + 2)
                if e >= 2:
                    pe.wait_ge(b_y, e - 1)
                for t in range(CT):
                    for c in range(2):
                        last = pe.matmul(PS[6 + e % 2][:, t * 128:(t + 1) * 128], hh[e % 2][:, c, t * 128:(t + 1) * 128],
                                         F["w2"][:, (2 * e + c) * D:(2 * e + c + 1) * D], start=(c == 0), stop=(c == 1))
                last.then_inc(b_dn, 1)

            make_a(0)
            pe.wait_ge(qk_kept, HEADS // 4)
            pe.wait_ge(b_idx, 1)
            turn(0)
            for e in range(E0):
                if e + 1 < E0:
                    turn(e + 1)
                pe.wait_ge(b_xe, e + 1)
                for c in range(2):
                    u = 2 * e + c
                    if u >= 2:
                        pe.wait_ge(b_sa, u - 1)
                        pe.wait_ge(b_g, u - 1)
                    at = e * HID0 + c * 128
                    pe.matmul(PS[2 + c][:, :], F["w1"][:, at:at + 128], xeT[e % 2], start=True, stop=True)
                    pe.matmul(PS[4 + c][:, :], F["w3"][:, at:at + 128], xeT[e % 2], start=True, stop=True).then_inc(b_up, 1)
                if e >= 1:
                    down(e - 1)
            down(E0 - 1)
            pe.wait_ge(b_g, 2 * E0)
            make_a(1)

        if upto >= 3:
            pe_prog.append(pe_ffn0)
            act_prog.append(act_ffn0)
            dve_prog.append(dve_ffn0)
            pool_prog.append(pool_ffn0)
            sp_prog.append(sp_ffn0)

        NH = 2 * HEADS
        FIRST = 6
        STEPS = range(FIRST, NH + FIRST)

        def attention(name, layer, a_t, mask, pack, phase, last_layer):
            L = W[pack]
            moe = not last_layer
            F = lambda n: f"{name}_{n}"
            top[0] = 0
            xnc, st, mv, ve, rstd = carve(2, D), carve(2, 6), carve(2, 2), carve(2), carve(2)
            xnT = [carve(256) for _ in range(2)]
            xn_at = top[0]
            carve(4, 256)
            x_hi, x_lo = ([rounded(F(f"{part}_{p}"), "work", xn_at + (2 * n + p) * 256, 256) for p in range(2)]
                          for n, part in enumerate(("xn_hi", "xn_lo")))
            a_hi = rounded(F("a_hi"), *(("w_f0", width("l3")) if moe else ("w_l1", 0)), HEADS * 128)
            a_lo = rounded(F("a_lo"), "qk", 0 if moe else HEADS * 128, HEADS * 128)
            v_sb = [carve(2, HEADS * HD) for _ in range(2)]
            qp = [carve(512) for _ in range(2)]
            pr = [carve(384) for _ in range(4)]
            pt = [carve(384) for _ in range(2)]
            ot = [carve(HEADS // 2, 256) for _ in range(2)]
            nmx, sm, rc = carve(4, 2), carve(4, 2), carve(4, 2)
            h1, h2 = [carve(512) for _ in range(2)], [carve(512) for _ in range(2)]
            ex, sg, bi, wt2 = carve(2, E1), carve(2, E1), carve(2, E1), [carve(2, E1) for _ in range(2)]
            cgt, ceq, rk = carve(2, E1 * E1), carve(2, E1 * E1), carve(2, E1)
            w_eff, brow = carve(128), carve(128)
            qmax, scl = carve(2), carve(4)

            MISC = []
            for s in STEPS:
                if s % 2 == 0:
                    MISC.append((s, "q", s // 2))
                for p, at in ((1, 0), (0, HEADS)):
                    if s == at + 6:
                        MISC.append((s, "t", p))
                    if at + 8 <= s < at + 12:
                        MISC.append((s, "v", 4 * p + s - at - 8))
                if moe and s % HEADS == 1:
                    MISC.append((s, "g", s // HEADS))
                if s == HEADS + 5 or s == NH + 5:
                    MISC.append((s, "o", 0 if s < NH else 1))
            PER = {"q": HEADS, "t": 2, "v": 8, "g": 2, "o": 2}
            BANK = {"q": 4, "t": 4, "v": 4, "g": 4, "o": 4} if moe else {"q": 4, "v": 6, "t": 7, "o": 7}
            shared = {}
            for bk in sorted(set(BANK.values())):
                items = [m for m in MISC if BANK[m[1]] == bk]
                start = [("t", 0)] * (BANK["t"] == bk) + [("v", c) for c in range(4)] * (BANK["v"] == bk)
                ahead = len(start) + sum(m[0] >= NH for m in items)
                shared[bk] = (sig(F(f"full{bk}"), len(items), ahead), sig(F(f"empty{bk}"), len(items), ahead),
                              {m[1:]: k for k, m in enumerate(items)}, start)

            def misc_at(i, kind, n, full, back=0):
                f, e, place, _ = shared[BANK[kind]]
                N = len(place)
                while (kind, n) not in place:
                    n, back = (n + PER[kind], back - N) if n < min(m for k, m in place if k == kind) else (n - PER[kind], back + N)
                sm_ = f if full else e
                return sm_.s, sm_.at(i, place[kind, n] + back)

            def made(i, kind, n):
                return misc_at(i, kind, n, True)

            def read(i, kind, n):
                return misc_at(i, kind, n, False)

            def free(i, kind, n):
                return misc_at(i, kind, n, False, -1)

            def early(kind, n, full):
                f, e, _, start = shared[BANK[kind]]
                sm_ = f if full else e
                return sm_.s, sm_.before(start.index((kind, n)))

            full_ = lambda kind: shared[BANK[kind]][0].s
            empty_ = lambda kind: shared[BANK[kind]][1].s
            s_f, s_mx, s_ex, s_rc = sig(F("scores"), NH), sig(F("maxima"), NH), sig(F("exps"), NH), sig(F("sums"), NH)
            s_nm, s_t, s_te, s_pv = sig(F("weights"), NH), sig(F("turned"), NH), sig(F("turned_out"), NH), sig(F("values"), NH)
            s_ot = sig(F("heads_out"), HEADS)
            ln_v, ln_p, ln_x = (sig(F(n), 2, 2) for n in ("variance", "rstd", "normed"))
            x_s = sig(F("normed_split"), 2, 1)
            dv = sig(F("dve_order"), 10 + (18 if moe else 0), 12 + (9 if moe else 0))
            if moe:
                f_u, f_r, f_q, f_d, f_x = (sig(F("moe_" + n), 2 * E1) for n in ("up", "relu", "square", "down", "added"))
                g_w = sig(F("gates"), 2)
            else:
                ln_b, pre_q = sig(F("biased"), 2, 2), sem(F("pre_q"))

            def units(s, lag):
                return (s - 1 - lag) // 2 if moe and (s - 1 - lag) % 2 == 0 else None

            def pe_(pe):
                pe.wait_ge(w_in[pack], w_all[pack])
                if last_layer:
                    pe.matmul(PS[2][:, 0:128], L["aT"][0:16, :], L["b"][0:16, :], start=True, stop=True)

                def turn(bank):
                    for t in range(2):
                        mm = pe.transpose(bank[:, t * 128:(t + 1) * 128], xnc[:, t, :], ident)
                    return mm

                def values(bank, c):
                    p, t, half_ = c // 4, c // 2 % 2, c % 2
                    return pe.matmul(bank[:, :], xnT[p][:, t * 128:(t + 1) * 128], L["wv"][:, half_ * 512:(half_ + 1) * 512],
                                     start=True, stop=True)

                def misc(i, s, kinds):
                    for at, kind, n in MISC:
                        if at != s or kind not in kinds:
                            continue
                        bank = PS[BANK[kind]]
                        if kind == "t":
                            pe.wait_ge(ln_x.s, ln_x.at(i, -n))
                        if kind == "o":
                            pe.wait_ge(s_ot.s, s_ot.at(i, 8 * n + 7))
                        pe.wait_ge(*free(i, kind, n))
                        if kind == "q":
                            pe.wait_ge(x_s.s, x_s.at(i, n // 8 - 1))
                            for j in range(2):
                                h, p = (2 * n + j) % HEADS, n // 8 % 2
                                to, hs = bank[:, j * 256:(j + 1) * 256], slice(h * 128, (h + 1) * 128)
                                pe.matmul(to, a_hi[:, hs], x_hi[p], start=True, stop=False)
                                pe.matmul(to, a_hi[:, hs], x_lo[p], start=False, stop=False)
                                mm = pe.matmul(to, a_lo[:, hs], x_hi[p], start=False, stop=True)
                        if kind == "t":
                            mm = turn(bank)
                        if kind == "v":
                            mm = values(bank, n)
                        if kind == "g":
                            for t in range(2):
                                mm = pe.matmul(bank[:, t * E1:(t + 1) * E1], xnT[n % 2][:, t * 128:(t + 1) * 128], L["gw"], start=True, stop=True)
                        if kind == "o":
                            for j in range(HEADS // 2):
                                for t in range(2):
                                    mm = pe.matmul(bank[:, t * 128:(t + 1) * 128], ot[n][:, j, t * 128:(t + 1) * 128],
                                                   L["wout"][:, j * 128:(j + 1) * 128], start=(j == 0 and t == 0),
                                                   stop=(moe and j == HEADS // 2 - 1), skip_group_check=True)
                            if last_layer:
                                for t in range(2):
                                    mm = pe.matmul(bank[:, t * 128:(t + 1) * 128], xnT[n][:, t * 128:(t + 1) * 128], w_eff,
                                                   start=False, stop=True, skip_group_check=True)
                        mm.then_inc(full_(kind), 1)

                def step(i, s, least):
                    misc(i, s, "q")
                    g = s - 1
                    if g >= least:
                        pe.wait_ge(*read(i, "q", g // 2))
                        pe.wait_ge(s_ex.s, s_ex.at(i, g - 2))
                        bk, q, x = PS[g % 2], qp[g // 2 % 2], xnT[g // HEADS % 2]
                        at = g % 2 * 256
                        pe.matmul(bk[:, 0:384], ident16[:, :], mask[:, :], start=True, stop=False, skip_group_check=True)
                        pe.matmul(bk[:, 0:128], q[:, at:at + 128], x[:, 0:128], start=False, stop=True, skip_group_check=True)
                        pe.matmul(bk[:, 128:384], q[:, at + 128:at + 256], x, start=False, stop=True,
                                  skip_group_check=True).then_inc(s_f.s, 1)
                    u = units(s, 0)
                    if u is not None and 2 * u >= least:
                        e = u % E1
                        pe.wait_ge(f_r.s, f_r.at(i, u - 1))
                        for c in range(2):
                            mm = pe.matmul(PS[6][:, c * 256:(c + 1) * 256], L["up"][:, e * HID1 + c * 128:e * HID1 + (c + 1) * 128],
                                           xnT[u // E1 % 2], start=True, stop=True)
                        mm.then_inc(f_u.s, 1)
                    g = s - 3
                    if g >= least:
                        pe.wait_ge(s_nm.s, s_nm.at(i, g))
                        pe.wait_ge(s_te.s, s_te.at(i, g - 2))
                        for c in range(3):
                            mm = pe.transpose(PS[2 + g % 2][:, c * 128:(c + 1) * 128], pr[g % 4][:, c * 128:(c + 1) * 128], ident)
                        mm.then_inc(s_t.s, 1)
                    g = s - 4
                    if g >= least:
                        pe.wait_ge(s_te.s, s_te.at(i, g))
                        if g % 2 == 0:
                            pe.wait_ge(s_ot.s, s_ot.at(i, g // 2 - 1))
                        rows_, h, v = slice(64 * (g % 2), 64 * (g % 2) + 64), g % HEADS, v_sb[g // HEADS % 2]
                        pe.matmul(PS[5][rows_, 0:256], v[:, 0, h * HD:(h + 1) * HD], pt[g % 2][:, 0:256], start=True, stop=False, skip_group_check=True)
                        pe.matmul(PS[5][rows_, 128:256], v[:, 1, h * HD:(h + 1) * HD], pt[g % 2][:, 256:384], start=False, stop=True,
                                  skip_group_check=True).then_inc(s_pv.s, 1)
                    misc(i, s, "tvg" if least else "tvgo")
                    u = units(s, 2)
                    if u is not None and 2 * u >= least:
                        e = u % E1
                        pe.wait_ge(f_q.s, f_q.at(i, u))
                        pe.wait_ge(f_x.s, f_x.at(i, u - 1))
                        for t in range(2):
                            for c in range(2):
                                mm = pe.matmul(PS[7][:, t * 128:(t + 1) * 128], h2[u % 2][:, c * 256 + t * 128:c * 256 + (t + 1) * 128],
                                               L["down"][:, (2 * e + c) * D:(2 * e + c + 1) * D], start=(c == 0), stop=(c == 1))
                        mm.then_inc(f_d.s, 1)

                pe.wait_ge(ln_x.s, ln_x.before(0))
                turn(PS[BANK["t"]]).then_inc(full_("t"), 1)
                for c in range(4):
                    if c == 0:
                        pe.wait_ge(*early("t", 0, False))
                    else:
                        pe.wait_ge(*early("v", c - 1, False))
                    values(PS[BANK["v"]], c).then_inc(full_("v"), 1)
                pe.wait_ge(*early("v", 3, False))
                for s in range(NH, NH + FIRST):
                    step(-1, s, NH)
                pe.wait_ge(*free(-1, "o", 1))
                pe.sem_inc(full_("o"), 1)
                with pe.Fori(0, PASSES) as i:
                    for s in STEPS:
                        step(i, s, 0)

            def act_(act):
                act.wait_ge(*early("t", 0, True))
                act.activation(xnT[0], PS[BANK["t"]][:, 0:256], ACT.Copy)
                act.activation(x_hi[0], PS[BANK["t"]][:, 0:256], ACT.Copy).then_inc(empty_("t"), 1)

                def step(i, s, least):
                    for at, kind, n in MISC:
                        if at != s or kind not in "qtg":
                            continue
                        bank = PS[BANK[kind]]
                        act.wait_ge(*made(i, kind, n))
                        if kind == "q":
                            act.wait_ge(s_f.s, s_f.at(i, 2 * n - 3))
                            act.activation(qp[n % 2], bank[:, :], ACT.Copy, scale=HD ** -0.5).then_inc(empty_(kind), 1)
                        if kind == "t":
                            act.activation(xnT[n], bank[:, 0:256], ACT.Copy)
                            act.activation(x_hi[n], bank[:, 0:256], ACT.Copy).then_inc(empty_(kind), 1)
                        if kind == "g":
                            act.wait_ge(g_w.s, g_w.at(i, n - 1))
                            act.activation(ex, bank[:, 0:2 * E1].rearrange("p (t e) -> p t e", e=E1), ACT.Exp, scale=-1.0).then_inc(empty_(kind), 1)
                    g = s - 1
                    if g >= least:
                        act.wait_ge(s_mx.s, s_mx.at(i, g))
                        act.wait_ge(s_t.s, s_t.at(i, g - 4))
                        act.activation(pr[g % 4][:, 0:128], PS[g % 2][:, 0:128], ACT.Exp, bias=nmx[:, g % 4, 0:1], accum_out=sm[:, g % 4, 0:1])
                        act.activation(pr[g % 4][:, 128:384], PS[g % 2][:, 128:384], ACT.Exp, bias=nmx[:, g % 4, 1:2],
                                       accum_out=sm[:, g % 4, 1:2]).then_inc(s_ex.s, 1)
                    u = units(s, 0)
                    if u is not None and 2 * u >= least:
                        act.wait_ge(f_u.s, f_u.at(i, u))
                        act.wait_ge(f_q.s, f_q.at(i, u - 2))
                        act.activation(h1[u % 2], PS[6][:, :], ACT.Relu).then_inc(f_r.s, 1)
                    g = s - 4
                    if g >= least and g % 2 == 1:
                        act.wait_ge(s_pv.s, s_pv.at(i, g))
                        act.wait_ge(*made(i, "o", g // HEADS - 2))
                        act.activation(ot[g // HEADS % 2][:, g // 2 % 8, :], PS[5][:, 0:256], ACT.Copy).then_inc(s_ot.s, 1)

                for s in range(NH, NH + FIRST):
                    step(-1, s, NH)
                with act.Fori(0, PASSES) as i:
                    for s in STEPS:
                        step(i, s, 0)

            def dve_(dve):
                k = [0, 0]

                def mark(ins):
                    k[0] += 1
                    ins.then_inc(dv.s, 1)

                def settle(i):
                    dve.wait_ge(dv.s, dv.before(k[0] - 1) if i is None or isinstance(i, int) else dv.at(i, k[0] - 1))

                def stats(i, tile):
                    for t in range(2):
                        mark(dve.bn_stats(st[:, t, :], x_sb[:, tile + t, :]))

                def moments(i):
                    for t in range(2):
                        mark(dve.bn_aggr(mv[:, t, :], st[:, t, :]))

                def variance(i):
                    settle(i)
                    mark(dve.tensor_scalar(ve, mv[:, :, 1], EPS, None, ALU.add))
                    settle(i)
                    dve.sem_inc(ln_v.s, 1)

                def normed(i, tile):
                    for t in range(2):
                        ins = dve.tensor_scalar(xnc[:, t, :], x_sb[:, tile + t, :], mv[:, t, 0:1], rstd[:, t:t + 1], ALU.subtract, ALU.mult)
                    ins.then_inc(ln_x.s, 1)

                def rest(p):
                    dve.tensor_tensor(x_lo[p], xnT[p], x_hi[p].bitcast(F32), ALU.subtract).then_inc(x_s.s, 1)

                def values_out(c):
                    p, t, half_ = c // 4, c // 2 % 2, c % 2
                    return dve.tensor_copy(v_sb[p][:, t, half_ * 512:(half_ + 1) * 512], PS[BANK["v"]][:, :])

                if last_layer:
                    dve.wait_ge(w_in[pack], w_all[pack])
                    dve.tensor_reduce(qmax[:, 0:1], L["kernel"], AX, ALU.max, apply_absolute_value=True).then_inc(pre_q, 1)
                    dve.wait_ge(pre_q, 2)
                    dve.tensor_scalar(scl[:, 0:1], qmax[:, 1:2], 1.0 / 7.0, None, ALU.mult).then_inc(pre_q, 1)
                    dve.wait_ge(pre_q, 3)
                    dve.reciprocal(scl[:, 1:2], scl[:, 0:1]).then_inc(pre_q, 1)
                    dve.wait_ge(pre_q, 4)
                    dve.tensor_scalar(w_eff, L["kernel"], scl[:, 1:2], 1.5 * 2 ** 23, ALU.mult, ALU.add).then_inc(pre_q, 1)
                    dve.wait_ge(pre_q, 5)
                    dve.tensor_scalar(w_eff, w_eff, 1.5 * 2 ** 23, -8.0, ALU.subtract, ALU.max).then_inc(pre_q, 1)
                    dve.wait_ge(pre_q, 6)
                    dve.tensor_scalar(w_eff, w_eff, 7.0, scl[:, 0:1], ALU.min, ALU.mult).then_inc(pre_q, 1)
                    dve.tensor_tensor(brow, L["bias"], L["bo"], ALU.add).then_inc(pre_q, 1)
                    dve.wait_ge(pre_q, 8)
                mark(dve.tensor_copy(a_hi, a_t))
                settle(None)
                mark(dve.tensor_tensor(a_lo, a_t, a_hi.bitcast(F32), ALU.subtract))
                stats(None, 0)
                settle(None)
                moments(None)
                variance(None)
                dve.wait_ge(ln_p.s, ln_p.before(0))
                normed(None, 0)
                dve.wait_ge(*early("t", 0, False))
                rest(0)
                if last_layer:
                    dve.tensor_tensor(w_eff, w_eff, PS[2][:, 0:128], ALU.add).then_inc(pre_q, 1)
                    dve.wait_ge(pre_q, 9)
                for c in range(4):
                    dve.wait_ge(*early("v", c, True))
                    values_out(c).then_inc(empty_("v"), 1)

                def step(i, s, least):
                    for at, tile in ((NH, 4 * i + 6), (HEADS, 4 * i + 4)):
                        if s == at + 2:
                            stats(i, tile)
                            settle(i)
                    g = s - 2
                    if g >= least:
                        dve.wait_ge(s_ex.s, s_ex.at(i, g))
                        dve.reciprocal(rc[:, g % 4, :], sm[:, g % 4, :]).then_inc(s_rc.s, 1)
                    if s in (NH + 2, HEADS + 2):
                        moments(i)
                    g = s - 1
                    if g >= least:
                        dve.wait_ge(s_f.s, s_f.at(i, g))
                        dve.wait_ge(s_ex.s, s_ex.at(i, g - 4))
                        dve.tensor_reduce(nmx[:, g % 4, 0:1], PS[g % 2][:, 0:128], AX, ALU.max, negate=True)
                        dve.tensor_reduce(nmx[:, g % 4, 1:2], PS[g % 2][:, 128:384], AX, ALU.max, negate=True).then_inc(s_mx.s, 1)
                    g = s - 3
                    if g >= least:
                        dve.wait_ge(s_t.s, s_t.at(i, g))
                        dve.wait_ge(s_pv.s, s_pv.at(i, g - 2))
                        dve.tensor_copy(pt[g % 2], PS[2 + g % 2][:, 0:384]).then_inc(s_te.s, 1)
                    for p, at, tile in ((1, NH, 4 * i + 6), (0, HEADS, 4 * i + 4)):
                        if s == at + 3:
                            variance(i)
                        if s == at + 4:
                            dve.wait_ge(ln_p.s, ln_p.at(i, p))
                            if not least:
                                dve.wait_ge(*made(i, "t", 1 - p))
                            normed(i, tile)
                    for at, kind, n in MISC:
                        if at == s - 1 and kind == "t":
                            dve.wait_ge(*read(i, kind, n))
                            rest(n)
                        if at != s or kind not in "vgo" or (least and kind == "o"):
                            continue
                        bank = PS[BANK[kind]]
                        if kind == "v":
                            dve.wait_ge(*made(i, kind, n))
                            dve.wait_ge(s_pv.s, s_pv.at(i, 15 if n < 4 else -1))
                            values_out(n).then_inc(empty_(kind), 1)
                        if kind == "g":
                            w = wt2[n % 2]
                            dve.wait_ge(*read(i, kind, n))
                            mark(dve.tensor_scalar(sg, ex, 1.0, None, ALU.add)); settle(i)
                            mark(dve.reciprocal(sg, sg)); settle(i)
                            mark(dve.tensor_tensor(bi, sg, spread(L["eb"].unsqueeze(1), 2, E1), ALU.add)); settle(i)
                            other, own = spread(bi.unsqueeze(2), 2, E1, E1), spread(bi.unsqueeze(3), 2, E1, E1)
                            sq = lambda v: v.rearrange("p t (e j) -> p t e j", j=E1)
                            mark(dve.tensor_tensor(sq(cgt), other, own, ALU.is_gt))
                            mark(dve.tensor_tensor(sq(ceq), other, own, ALU.is_equal)); settle(i)
                            mark(dve.tensor_tensor(ceq, ceq, spread(C["tri8"].unsqueeze(1), 2, E1 * E1), ALU.mult)); settle(i)
                            mark(dve.tensor_tensor(cgt, cgt, ceq, ALU.add)); settle(i)
                            mark(dve.tensor_reduce(rk, sq(cgt), AX, ALU.add)); settle(i)
                            dve.wait_ge(f_x.s, f_x.at(i, E1 * (n - 1) - 1))
                            mark(dve.scalar_tensor_tensor(w, rk, 1.5, sg, ALU.is_lt, ALU.mult)); settle(i)
                            dve.tensor_tensor(w, w, w, ALU.mult).then_inc(g_w.s, 1)
                        if kind == "o":
                            dve.wait_ge(*made(i, kind, n))
                            if moe:
                                dve.wait_ge(f_x.s, f_x.at(i, E1 * n + E1 - 1))
                            else:
                                dve.wait_ge(ln_b.s, ln_b.at(i, n - 2))
                            tt = bass.ds(4 * i + 2 * n, 2)
                            dve.tensor_tensor(x_sb[:, tt, :], x_sb[:, tt, :], bank[:, 0:256].rearrange("p (t d) -> p t d", d=D),
                                              ALU.add).then_inc(empty_(kind), 1)
                    u = units(s, 2)
                    if u is not None and 2 * u >= least:
                        e, w = u % E1, wt2[u // E1 % 2]
                        dve.wait_ge(f_d.s, f_d.at(i, u))
                        dve.wait_ge(g_w.s, g_w.at(i, u // E1))
                        dve.wait_ge(f_x.s, f_x.at(i, u - 1))
                        for t in range(2):
                            row_ = x_sb[:, 4 * i + 2 * (u // E1) + t, :]
                            ins = dve.scalar_tensor_tensor(row_, PS[7][:, t * 128:(t + 1) * 128], w[:, t, e:e + 1], row_, ALU.mult, ALU.add)
                        ins.then_inc(f_x.s, 1)

                for s in range(NH, NH + FIRST):
                    step(-1, s, NH)
                assert k[0] == dv.ahead, k[0]
                dve.wait_ge(*free(-1, "o", 1))
                dve.sem_inc(empty_("o"), 1)
                with dve.Fori(0, PASSES) as i:
                    k[0] = 0
                    for s in STEPS:
                        step(i, s, 0)
                    assert k[0] == dv.n, (k[0], dv.n)

            def pool_(pool):
                if last_layer:
                    pool.wait_ge(pre_q, 1)
                    pool.partition_all_reduce(qmax[:, 1:2], qmax[:, 0:1], 128, bass.bass_isa.ReduceOp.max).then_inc(pre_q, 1)
                    pool.wait_ge(pre_q, 8)

                def power():
                    return pool.tensor_tensor(rstd, ve, half[:, 0:2], ALU.pow)

                def bias(tile):
                    tt = bass.ds(tile, 2)
                    return pool.tensor_tensor(x_sb[:, tt, :], x_sb[:, tt, :], spread(brow.unsqueeze(1), 2, D), ALU.add)

                pool.wait_ge(ln_v.s, ln_v.before(0))
                power().then_inc(ln_p.s, 1)
                if last_layer:
                    pool.wait_ge(ln_x.s, ln_x.before(0))
                    bias(0).then_inc(ln_b.s, 1)
                def step(i, s, least):
                    g = s - 2
                    if g >= least:
                        pool.wait_ge(s_rc.s, s_rc.at(i, g))
                        for q, (c0, c1) in enumerate(((0, 128), (128, 384))):
                            ins = pool.tensor_tensor(pr[g % 4][:, c0:c1], pr[g % 4][:, c0:c1], spread(rc[:, g % 4, q:q + 1], c1 - c0), ALU.mult)
                        ins.then_inc(s_nm.s, 1)
                    for p, at, tile in ((1, NH, 4 * i + 6), (0, HEADS, 4 * i + 4)):
                        if s == at + 3:
                            pool.wait_ge(ln_v.s, ln_v.at(i, p))
                            power().then_inc(ln_p.s, 1)
                        if s == at + 5 and last_layer:
                            pool.wait_ge(ln_x.s, ln_x.at(i, p))
                            bias(tile).then_inc(ln_b.s, 1)
                    u = units(s, 1)
                    if u is not None and 2 * u >= least:
                        pool.wait_ge(f_r.s, f_r.at(i, u))
                        pool.wait_ge(f_d.s, f_d.at(i, u - 2))
                        pool.tensor_tensor(h2[u % 2], h1[u % 2], h1[u % 2], ALU.mult).then_inc(f_q.s, 1)

                for s in range(NH, NH + FIRST):
                    step(-1, s, NH)
                with pool.Fori(0, PASSES) as i:
                    for s in STEPS:
                        step(i, s, 0)

            def sp_(sp):
                if layer == 1:
                    sp.wait_ge(phase_end, 4 * (phase - 1))
                    sp.dma_start(regions["l2"][:, :], ins["l2"]).then_inc(w_in["l2"], 16)
                    sp.dma_start(regions["l3"][:, 0:width("l3")], ins["l3"]).then_inc(w_in["l3"], 16)

            pe_prog.append(pe_)
            act_prog.append(act_)
            dve_prog.append(dve_)
            pool_prog.append(pool_)
            sp_prog.append(sp_)

        if upto >= 4:
            attention("l1", 1, a1_t, mask1, "l1", 4, False)

        def layer2():
            L = W["l2"]
            top[0] = 0
            xnc, st, mv, ve, rstd = carve(4, D), carve(4, 6), carve(4, 2), carve(4), carve(4)
            xnT, qin, rq, qT = carve(512), carve(512), carve(512), carve(512)
            kb = carve(G2, 512)
            v_sb = carve(4, 128)
            vcol, nb2, ed, thr = carve(1), carve(1), carve(4), carve(4, G2)
            mb0 = [carve(512).bitcast(BF16).rearrange("p (g k) -> p g k", k=256) for _ in range(2)]
            mb1 = [carve(256).bitcast(BF16).rearrange("p (g k) -> p g k", k=128) for _ in range(2)]
            pr0, pr1 = [carve(G2, 256) for _ in range(2)], [carve(G2, 128) for _ in range(2)]
            pt = [carve(384) for _ in range(2)]
            oT = carve(512)
            nmx, sm, rc = carve(2, 2, G2), carve(2, 2, G2), carve(2, 2, G2)
            sa = [carve(512) for _ in range(2)]
            h_start = top[0]
            h0, hA, hB = carve(C2, 512), carve(C2, 512), h0_late
            h_at = {w: sum(n for _, n in PACKS["l2"][:[m for m, _ in PACKS["l2"]].index(w)]) for w in ("h1", "h2")}
            hi_w = [rounded(f"hi_{w}", "w_l1", (1 + n) * C2 * HID2, C2 * HID2) for n, w in enumerate(h_at)]
            lo_w = [rounded(f"lo_{w}", "w_l2", h_at[w], C2 * HID2) for w in h_at]
            hi_0, lo_0 = rounded("hi_h0", "w_f0", width("l3"), C2, 512), rounded("lo_h0", "work", h_start, C2, 512)
            hi_A, lo_A = rounded("hi_hA", "qk", 0, C2, 512), rounded("lo_hA", "work", h_start + C2 * 512, C2, 512)
            PRE = 8
            ORDER = ["in", "q", "v", "k", "t"]
            N = len(ORDER)
            place = {n: k for k, n in enumerate(ORDER)}
            m_f, m_e = sig("l2_misc_full", N, 1), sig("l2_misc_empty", N, 1)
            rq_s = sig("l2_relu_in", 1)
            d_f, d_e, o_f, o_e = (sig("l2_" + n, 1) for n in ("reach", "reach_out", "output", "added"))
            UP_BANKS = ((6, 7), (0, 1))
            MID_BANKS = ((6, 7, 5, 3), (6, 7, 0, 1))
            f_ab, f_s, f_h = sig("l2_up", C2), sig("l2_silu", C2), sig("l2_gated", C2)
            f_i, f_ig, f_sp, f_j, f_jg = sig("l2_mid1", C2), sig("l2_gelu1", C2), sig("l2_split", C2), sig("l2_mid2", C2), sig("l2_gelu2", C2)
            mb_s, s_f, s_mx, s_ex, s_rc, s_nm = (sig("l2_" + n, 2) for n in ("masks", "scores", "maxima", "exps", "sums", "weights"))
            t_f, t_e, pv, ot = sig("l2_turned", 8), sig("l2_turned_out", 8), sig("l2_values", 8), sig("l2_heads_out", 2)
            ln_v, ln_p, ln_x = sig("l2_variance", 1, 1), sig("l2_rstd", 1, 1), sig("l2_normed", 1, 1)
            dv = sig("l2_dve_order", 4 + 4 + 1 + 3 + 3 * C2, 9)
            pre, pre_k = sem("l2_pre"), sem("l2_pre_k")

            def pe_(pe):
                pe.wait_ge(w_in["l2"], w_all["l2"])
                pe.matmul(PS[0][:, 0:1], L["wop"][0:32, :], L["w2c"][0:32, :], start=True, stop=True).then_inc(pre, 1)

                def turn():
                    for t in range(4):
                        mm = pe.transpose(PS[4][:, t * 128:(t + 1) * 128], xnc[:, t, :], ident)
                    mm.then_inc(m_f.s, 1)

                pe.wait_ge(ln_x.s, ln_x.before(0))
                turn()
                pe.wait_ge(pre_k, 2)
                pe.wait_ge(pre, 4)
                with pe.Fori(0, PASSES) as i:
                    def free(n):
                        pe.wait_ge(m_e.s, m_e.at(i, place[n] - 1))

                    def up(c, which=range(2)):
                        if c == 0 and which[0] == 0:
                            pe.wait_ge(f_jg.s, f_jg.at(i, -1))
                        if c >= 2:
                            pe.wait_ge(dv.s, dv.at(i, c - 2))
                        for n in which:
                            mm = pe.matmul(PS[UP_BANKS[c % 2][n]][:, :], L[("w1", "w2")[n]][:, c * 128:(c + 1) * 128], xnT, start=True, stop=True)
                        if which[-1] == 1:
                            mm.then_inc(f_ab.s, 1)

                    def mid(c, layer, parts=range(C2)):
                        hi, lo, made, before = ((hi_0, lo_0, f_i, f_h), (hi_A, lo_A, f_j, f_sp))[layer]
                        bank = PS[MID_BANKS[layer][c]]
                        if parts[0] == 0:
                            pe.wait_ge(pre, PRE)
                            if layer == 0 and c == 0:
                                pe.wait_ge(f_h.s, f_h.at(i, 1))
                            if layer == 0 and c == 2:
                                pe.wait_ge(ot.s, ot.at(i, -1))
                                pe.wait_ge(d_e.s, d_e.at(i, 0))
                            if layer == 0 and c == 3:
                                pe.wait_ge(t_e.s, t_e.at(i, -1))
                            if layer == 1 and c == 2:
                                pe.wait_ge(s_ex.s, s_ex.at(i, 1))
                        for kk in parts:
                            pe.wait_ge(before.s, before.at(i, kk))
                            at = slice(kk * HID2 + c * 128, kk * HID2 + (c + 1) * 128)
                            pe.matmul(bank[:, :], hi_w[layer][:, at], hi[:, kk, :], start=(kk == 0), stop=False)
                            pe.matmul(bank[:, :], hi_w[layer][:, at], lo[:, kk, :], start=False, stop=False)
                            mm = pe.matmul(bank[:, :], lo_w[layer][:, at], hi[:, kk, :], start=False, stop=(kk == C2 - 1))
                        if parts[-1] == C2 - 1:
                            mm.then_inc(made.s, 1)

                    def scores(p):
                        pe.wait_ge(mb_s.s, mb_s.at(i, p))
                        pe.wait_ge(s_ex.s, s_ex.at(i, p - 1))
                        pe.wait_ge(o_e.s, o_e.at(i, -1))
                        for j in range(2):
                            pe.matmul(PS[j][:, :], ident16[:, :], mb0[p][:, 2 * j:2 * j + 2, :].rearrange("p g k -> p (g k)"), start=True, stop=False)
                        pe.matmul(PS[2][:, :], ident16[:, :], mb1[p].rearrange("p g k -> p (g k)"), start=True, stop=False)
                        for j in range(2):
                            pe.matmul(PS[j][:, :], qT[:, p * 256:p * 256 + 128], kb[:, 2 * j:2 * j + 2, p * 256:(p + 1) * 256], start=False, stop=True)
                        pe.matmul(PS[2][:, :], qT[:, p * 256 + 128:(p + 1) * 256], kb[:, :, p * 256 + 128:(p + 1) * 256],
                                  start=False, stop=True).then_inc(s_f.s, 1)

                    def turned(p, g):
                        n = 4 * p + g
                        pe.wait_ge(s_nm.s, s_nm.at(i, p))
                        pe.wait_ge(t_e.s, t_e.at(i, n - 2))
                        if n == 0:
                            pe.wait_ge(f_ig.s, f_ig.at(i, C2 - 1))
                        if n == 1:
                            pe.wait_ge(m_e.s, m_e.at(i, place["t"]))
                        for c, src in enumerate((pr0[p][:, g, 128:256], pr1[p][:, g, :], pr0[p][:, g, 0:128])):
                            mm = pe.transpose(PS[(3, 4)[n % 2]][:, c * 128:(c + 1) * 128], src, ident)
                        mm.then_inc(t_f.s, 1)

                    def values(p, g):
                        n = 4 * p + g
                        pe.wait_ge(t_e.s, t_e.at(i, n))
                        if g == 0:
                            pe.wait_ge(ot.s, ot.at(i, p - 1))
                        r = slice(DH2 * g, DH2 * (g + 1))
                        pe.matmul(PS[5][r, 0:256], v_sb[:, 2 * p + 1, r], pt[n % 2][:, 0:256], start=True, stop=False, skip_group_check=True)
                        pe.matmul(PS[5][r, 0:128], v_sb[:, 2 * p, r], pt[n % 2][:, 256:384], start=False, stop=True,
                                  skip_group_check=True).then_inc(pv.s, 1)

                    def wide_out(t):
                        cs = slice(t * 128, (t + 1) * 128)
                        for c in range(C2):
                            pe.matmul(PS[2][:, cs], hB[:, c, cs], L["w3"][:, c * 128:(c + 1) * 128], start=(t == 0 and c == 0), stop=False, skip_group_check=True)

                    free("in")
                    pe.wait_ge(t_e.s, t_e.at(i, -1))
                    pe.matmul(PS[4][:, :], L["wq"], xnT, start=True, stop=True).then_inc(m_f.s, 1)
                    up(0, range(0, 1))
                    pe.wait_ge(rq_s.s, rq_s.at(i, 0))
                    pe.wait_ge(ot.s, ot.at(i, -1))
                    for t in range(4):
                        mm = pe.matmul(PS[5][:, t:t + 1], rq[:, t * 128:(t + 1) * 128], vcol, start=True, stop=True)
                    mm.then_inc(d_f.s, 1)
                    up(0, range(1, 2))
                    up(1)
                    free("q")
                    pe.matmul(PS[4][:, :], L["wqkv"][:, 0:128], qin, start=True, stop=True).then_inc(m_f.s, 1)
                    up(2)
                    free("v")
                    for t in range(4):
                        mm = pe.matmul(PS[4][:, t * 128:(t + 1) * 128], qin[:, t * 128:(t + 1) * 128], L["wqkv"][:, 256:384], start=True, stop=True)
                    mm.then_inc(m_f.s, 1)
                    up(3)
                    free("k")
                    pe.matmul(PS[4][:, :], L["wqkv"][:, 128:256], qin, start=True, stop=True).then_inc(m_f.s, 1)
                    mid(0, 0, range(0, 2))
                    mid(1, 0, range(0, 2))
                    pe.wait_ge(m_e.s, m_e.at(i, place["k"]))
                    scores(0)
                    mid(0, 0, range(2, C2))
                    mid(1, 0, range(2, C2))
                    mid(2, 0)
                    mid(3, 0)
                    pe.wait_ge(ln_x.s, ln_x.at(i, 0))
                    turn()
                    scores(1)
                    turned(0, 0)
                    turned(0, 1)
                    mid(0, 1, range(0, 2))
                    mid(1, 1, range(0, 2))
                    values(0, 0)
                    turned(0, 2)
                    values(0, 1)
                    turned(0, 3)
                    mid(0, 1, range(2, C2))
                    values(0, 2)
                    values(0, 3)
                    mid(1, 1, range(2, C2))
                    mid(2, 1)
                    turned(1, 0)
                    turned(1, 1)
                    mid(3, 1)
                    values(1, 0)
                    turned(1, 2)
                    values(1, 1)
                    turned(1, 3)
                    pe.wait_ge(f_jg.s, f_jg.at(i, C2 - 1))
                    wide_out(0)
                    wide_out(1)
                    values(1, 2)
                    wide_out(2)
                    values(1, 3)
                    wide_out(3)
                    pe.wait_ge(ot.s, ot.at(i, 1))
                    for t in range(4):
                        cs = slice(t * 128, (t + 1) * 128)
                        mm = pe.matmul(PS[2][:, cs], oT[:, cs], ident, start=False, stop=True, skip_group_check=True)
                    mm.then_inc(o_f.s, 1)

            def act_(act):
                act.wait_ge(m_f.s, m_f.before(0))
                act.activation(xnT, PS[4][:, :], ACT.Copy).then_inc(m_e.s, 1)
                act.wait_ge(pre_k, 2)
                with act.Fori(0, PASSES) as i:
                    def silu(c):
                        act.wait_ge(f_ab.s, f_ab.at(i, c))
                        act.wait_ge(*((dv.s, dv.at(i, c - 2)) if c >= 2 else (f_h.s, f_h.at(i, c - 2))))
                        act.activation(sa[c % 2], PS[UP_BANKS[c % 2][0]][:, :], ACT.Silu, scale=L["s1"][:, c:c + 1]).then_inc(f_s.s, 1)

                    act.wait_ge(m_f.s, m_f.at(i, place["in"]))
                    act.wait_ge(rq_s.s, rq_s.at(i, 0))
                    act.activation(qin, PS[4][:, :], ACT.Copy).then_inc(m_e.s, 1)
                    act.wait_ge(d_f.s, d_f.at(i, 0))
                    act.activation(ed, PS[5][:, 0:4], ACT.Exp, scale=-1.0, bias=nb2).then_inc(d_e.s, 1)
                    silu(0)
                    silu(1)
                    silu(2)
                    act.wait_ge(m_f.s, m_f.at(i, place["v"]))
                    act.wait_ge(pv.s, pv.at(i, -1))
                    act.activation(v_sb.rearrange("p t d -> p (t d)"), PS[4][:, :], ACT.Copy).then_inc(m_e.s, 1)
                    silu(3)
                    act.wait_ge(m_f.s, m_f.at(i, place["k"]))
                    for g in range(G2):
                        r = slice(DH2 * g, DH2 * (g + 1))
                        ins_ = act.activation(kb[r, g, :], PS[4][r, :], ACT.Identity, bias=L["bk"][r, :])
                    ins_.then_inc(m_e.s, 1)

                    def exps(p):
                        act.wait_ge(s_mx.s, s_mx.at(i, p))
                        act.wait_ge(t_f.s, t_f.at(i, 4 * p + 3 - 8))
                        for g in range(G2):
                            act.activation(pr0[p][:, g, :], PS[g // 2][:, g % 2 * 256:(g % 2 + 1) * 256], ACT.Exp, bias=nmx[:, p, 0, g:g + 1],
                                           accum_out=sm[:, p, 0, g:g + 1])
                        for g in range(G2):
                            ins_ = act.activation(pr1[p][:, g, :], PS[2][:, g * 128:(g + 1) * 128], ACT.Exp, bias=nmx[:, p, 1, g:g + 1],
                                                  accum_out=sm[:, p, 1, g:g + 1])
                        ins_.then_inc(s_ex.s, 1)

                    def gelu(c, layer, dst, scale, made, out_s):
                        act.wait_ge(made.s, made.at(i, c))
                        act.activation(dst[:, c, :], PS[MID_BANKS[layer][c]][:, :], ACT.Gelu, scale=scale[:, c:c + 1]).then_inc(out_s.s, 1)

                    exps(0)
                    for c in range(C2):
                        if c == 0:
                            act.wait_ge(f_j.s, f_j.at(i, -1))
                        gelu(c, 0, hA, L["hs1"], f_i, f_ig)
                    act.wait_ge(m_f.s, m_f.at(i, place["t"]))
                    act.activation(xnT, PS[4][:, :], ACT.Copy).then_inc(m_e.s, 1)
                    exps(1)
                    act.wait_ge(o_f.s, o_f.at(i, -1))
                    head_out(act, i, 0)
                    for c in range(C2):
                        gelu(c, 1, hB, L["hs2"], f_j, f_jg)
                    head_out(act, i, 1)

            def head_out(act, i, p):
                act.wait_ge(pv.s, pv.at(i, 4 * p + 3))
                act.activation(oT[:, p * 256:(p + 1) * 256], PS[5][:, 0:256], ACT.Identity, bias=L["bv"]).then_inc(ot.s, 1)

            def dve_(dve):
                k = [0]

                def mark(ins):
                    k[0] += 1
                    ins.then_inc(dv.s, 1)

                def settle(i):
                    dve.wait_ge(dv.s, dv.before(k[0] - 1) if i is None else dv.at(i, k[0] - 1))

                def stats(i, tile):
                    for t in range(4):
                        mark(dve.bn_stats(st[:, t, :], x_sb[:, tile + t, :]))
                    settle(i)

                def moments():
                    for t in range(4):
                        mark(dve.bn_aggr(mv[:, t, :], st[:, t, :]))

                def variance(i):
                    settle(i)
                    mark(dve.tensor_scalar(ve, mv[:, :, 1], EPS, None, ALU.add))
                    settle(i)
                    dve.sem_inc(ln_v.s, 1)

                def normed(tile):
                    for t in range(4):
                        ins_ = dve.tensor_scalar(xnc[:, t, :], x_sb[:, tile + t, :], mv[:, t, 0:1], rstd[:, t:t + 1], ALU.subtract, ALU.mult)
                    ins_.then_inc(ln_x.s, 1)

                stats(None, 0)
                moments()
                variance(None)
                assert k[0] == dv.ahead
                dve.wait_ge(ln_p.s, ln_p.before(0))
                normed(0)
                dve.wait_ge(w_in["l2"], w_all["l2"])
                dve.wait_ge(pre, 1)
                dve.tensor_copy(vcol, PS[0][:, 0:1]).then_inc(pre, 1)
                dve.tensor_scalar(nb2, L["b2"], -1.0, None, ALU.mult).then_inc(pre, 1)
                w3 = L["w3"].rearrange("p (c d) -> p c d", d=D)
                dve.tensor_tensor(w3, w3, spread(L["s3"].unsqueeze(1), C2, D), ALU.mult).then_inc(pre, 1)
                dve.wait_ge(pre, 4)
                for n, w in enumerate(("h1", "h2")):
                    dve.tensor_copy(hi_w[n], L[w]).then_inc(pre, 1)
                dve.sem_inc(pre_k, 1)
                with dve.Fori(0, PASSES) as i:
                    k[0] = 0

                    def split(full, hi, lo, c, done):
                        settle(i)
                        mark(dve.tensor_copy(hi[:, c, :], full[:, c, :]))
                        settle(i)
                        dve.tensor_tensor(lo[:, c, :], full[:, c, :], hi[:, c, :].bitcast(F32), ALU.subtract).then_inc(done.s, 1)

                    def gated(c):
                        dve.wait_ge(f_s.s, f_s.at(i, c))
                        if c == 0:
                            dve.wait_ge(f_i.s, f_i.at(i, -1))
                        dve.scalar_tensor_tensor(h0[:, c, :], PS[UP_BANKS[c % 2][1]][:, :], L["s2"][:, c:c + 1], sa[c % 2], ALU.mult, ALU.mult).then_inc(dv.s, 1)
                        k[0] += 1

                    def masks(p):
                        for g in range(G2):
                            dve.tensor_scalar(mb0[p][:, g, :], C["dist"], thr[:, 2 * p, g:g + 1], MASKED, ALU.is_gt, ALU.mult)
                            ins_ = dve.tensor_scalar(mb1[p][:, g, :], C["dist"][:, 0:128], thr[:, 2 * p + 1, g:g + 1], MASKED, ALU.is_gt, ALU.mult)
                        ins_.then_inc(mb_s.s, 1)

                    dve.wait_ge(m_f.s, m_f.at(i, place["in"]))
                    dve.tensor_scalar(rq, PS[4][:, :], 0.0, None, ALU.max).then_inc(rq_s.s, 1)
                    gated(0)
                    dve.wait_ge(m_f.s, m_f.at(i, place["q"]))
                    dve.tensor_scalar(qT, PS[4][:, :], L["bq"], 2.0 / S ** 0.5, ALU.add, ALU.mult).then_inc(m_e.s, 1)
                    gated(1)
                    dve.wait_ge(d_e.s, d_e.at(i, 0))
                    mark(dve.tensor_scalar(ed, ed, 1.0, None, ALU.add)); settle(i)
                    mark(dve.reciprocal(ed, ed)); settle(i)
                    mark(dve.scalar_tensor_tensor(thr, spread(ed.unsqueeze(2), 4, G2), float(S), spread(C["win"].unsqueeze(1), 4, G2), ALU.mult, ALU.add))
                    split(h0, hi_0, lo_0, 0, f_h)
                    gated(2)
                    split(h0, hi_0, lo_0, 1, f_h)
                    gated(3)
                    masks(0)
                    split(h0, hi_0, lo_0, 2, f_h)
                    split(h0, hi_0, lo_0, 3, f_h)
                    masks(1)
                    tile = 4 * i + 4
                    stats(i, tile)
                    def maxima(p):
                        dve.wait_ge(s_f.s, s_f.at(i, p))
                        for j in range(2):
                            dve.tensor_reduce(nmx[:, p, 0, 2 * j:2 * j + 2], PS[j][:, :].rearrange("p (g k) -> p g k", k=256), AX, ALU.max, negate=True)
                        dve.tensor_reduce(nmx[:, p, 1, :], PS[2][:, :].rearrange("p (g k) -> p g k", k=128), AX, ALU.max, negate=True).then_inc(s_mx.s, 1)

                    def sums(p):
                        dve.wait_ge(s_ex.s, s_ex.at(i, p))
                        dve.reciprocal(rc[:, p, :, :], sm[:, p, :, :]).then_inc(s_rc.s, 1)

                    def turned_out(*which):
                        for n in which:
                            dve.wait_ge(t_f.s, t_f.at(i, n))
                            dve.wait_ge(pv.s, pv.at(i, n - 2))
                            dve.tensor_copy(pt[n % 2], PS[(3, 4)[n % 2]][:, 0:384]).then_inc(t_e.s, 1)

                    maxima(0)
                    moments()
                    variance(i)
                    dve.wait_ge(ln_p.s, ln_p.at(i, 0))
                    normed(tile)
                    sums(0)
                    for c in range(C2):
                        if c == 2:
                            maxima(1)
                            turned_out(0, 1)
                        dve.wait_ge(f_ig.s, f_ig.at(i, c))
                        split(hA, hi_A, lo_A, c, f_sp)
                    turned_out(2, 3)
                    sums(1)
                    turned_out(*range(G2, 2 * G2))
                    dve.wait_ge(o_f.s, o_f.at(i, 0))
                    tt = bass.ds(4 * i, 4)
                    dve.tensor_tensor(x_sb[:, tt, :], x_sb[:, tt, :], PS[2][:, :].rearrange("p (t d) -> p t d", d=D), ALU.add).then_inc(o_e.s, 1)
                    assert k[0] == dv.n, (k[0], dv.n)

            def pool_(pool):
                pool.memset(kb, 0.0).then_inc(pre_k, 1)
                pool.wait_ge(ln_v.s, ln_v.before(0))
                pool.tensor_tensor(rstd, ve, half[:, 0:4], ALU.pow).then_inc(ln_p.s, 1)
                for n, w in enumerate(("h1", "h2")):
                    pool.wait_ge(pre, PRE - 2)
                    pool.tensor_tensor(lo_w[n], L[w], hi_w[n].bitcast(F32), ALU.subtract).then_inc(pre, 1)
                with pool.Fori(0, PASSES) as i:
                    for p in range(2):
                        if p == 0:
                            pool.wait_ge(ln_v.s, ln_v.at(i, 0))
                            pool.tensor_tensor(rstd, ve, half[:, 0:4], ALU.pow).then_inc(ln_p.s, 1)
                        pool.wait_ge(s_rc.s, s_rc.at(i, p))
                        pool.tensor_tensor(pr0[p], pr0[p], spread(rc[:, p, 0, :].unsqueeze(2), G2, 256), ALU.mult)
                        pool.tensor_tensor(pr1[p], pr1[p], spread(rc[:, p, 1, :].unsqueeze(2), G2, 128), ALU.mult).then_inc(s_nm.s, 1)

            pe_prog.append(pe_)
            act_prog.append(act_)
            dve_prog.append(dve_)
            pool_prog.append(pool_)

        h0_late = regions["l1"][:, 0:C2 * 512].rearrange("p (c t) -> p c t", t=512)
        if upto >= 5:
            layer2()
        if upto >= 9:
            attention("l3", 3, a3_t, mask3, "l3", 6, True)
        def sp_store(sp):
            sp.wait_ge(phase_end, 4 * (len(pe_prog)))
            sp.dma_start(out_v, x_sb[:, 0:TILES, :]).then_inc(stored, 16)
            sp.wait_ge(stored, 16)

        block = ctx.enter_context(nc.Block())

        def run(eng, prog):
            for n, phase in enumerate(prog):
                phase(eng)
                close(eng, n + 1)

        @block.sync
        def _(sp):
            for phase in sp_prog:
                phase(sp)
            sp_store(sp)

        @block.tensor
        def _(pe):
            run(pe, pe_prog)

        @block.scalar
        def _(act):
            run(act, act_prog)

        @block.vector
        def _(dve):
            run(dve, dve_prog)

        @block.gpsimd
        def _(pool):
            run(pool, pool_prog)


def lay_out(a):
    f = np.float32
    P = np.arange(128)

    def pad(m):
        z = np.zeros((128, m.shape[1]), f)
        z[:m.shape[0]] = m
        return z

    def col(v):
        return pad(v.reshape(-1, 1))

    def rows(v):
        return np.repeat(v.reshape(1, -1), 128, axis=0)

    def chunks(m):
        return m.reshape(-1, 128, m.shape[1]).transpose(1, 0, 2).reshape(128, -1)

    def cols(v):
        return v.reshape(-1, 128).T

    tok = np.arange(S)
    flat = np.arange(HCH * 128).reshape(HCH, 128)
    be = np.arange(128)
    c = {
        "ident": np.eye(128), "blockones": be[:, None] % E0 == be[None, :] % E0,
        "lowerblk": (be[:, None] % E0 == be[None, :] % E0) & (be[:, None] // E0 < be[None, :] // E0),
        "dist": np.where(tok[None, :] < P[:, None], FAR, tok[None, :] - P[:, None]),
        "iota": np.repeat(np.arange(128)[None], 128, axis=0), "pidx": P[:, None],
        "tileno": rows(np.repeat(2 * np.arange(B)[None, :] + np.arange(2)[:, None], E0, axis=1)),
        "tri": np.concatenate([tok[None, :] < (n * 128 + P)[:, None] for n in range(2)], axis=1),
        "headmask": P[:, None] // HD0 == np.arange(H0)[None, :],
        "vmask": (flat.T[:, :, None] // KPAD == P[None, None, :] // HD0).reshape(128, -1),
        "tri8": np.repeat((np.arange(8)[None, :] < np.arange(8)[:, None]).reshape(1, 64), 128, axis=0),
        "win": rows(np.array(WINDOWS)),
    }
    l0 = {k + "T": a["L0_attn_" + k].T for k in ("wq", "wk", "wv", "wo", "wi1")}
    l0 |= {"wi2rep": pad(np.repeat(a["L0_attn_wi2"].T, 128, axis=1)), "bi1": col(a["L0_attn_bi1"]),
           "bi2": rows(a["L0_attn_bi2"]), "bo": rows(a["L0_attn_bo"]), "wg": a["L0_ffn_wg"]}
    l0 |= {k: col(a["L0_attn_" + k]) for k in ("bq", "bk", "bv")}
    f0 = {k: a["L0_ffn_" + k].transpose(1, 0, 2).reshape(128, -1) for k in ("w1", "w3")}
    f0["w2"] = chunks(a["L0_ffn_w2"].reshape(-1, D))
    l1 = {"wv": a["L1_attn_w_qkv"][:, 2048:], "wout": chunks(a["L1_attn_w_out"]),
          "up": a["L1_ffn_w_up"].transpose(2, 0, 1).reshape(128, -1),
          "down": chunks(a["L1_ffn_w_down"].transpose(0, 2, 1).reshape(-1, D)),
          "gw": a["L1_ffn_gate_w"].T, "eb": rows(a["L1_ffn_expert_bias"])}

    def per_head(w):
        return w.reshape(D, 2, HEADS // 2, HD).transpose(1, 3, 2, 0).reshape(128, -1)

    q, j = np.arange(S)[:, None], np.arange(S)[None, :]
    causal = j <= q
    near = (j >= q - 16) & (j <= q + 16)
    ok1 = (near | (j < 64) | (q < 64)) & causal

    def masks(ok):
        m = np.where(ok, 0.0, MASKED)
        return np.concatenate([m[:128, :128], m[128:, :]], axis=1)

    qk1 = {"wqT": per_head(a["L1_attn_w_qkv"][:, :1024]), "wkT": per_head(a["L1_attn_w_qkv"][:, 1024:2048]), "mask": masks(ok1)}
    qk3 = {"wqT": per_head(a["L3_attn_Wq"]), "wkT": per_head(a["L3_attn_Wk"]), "mask": masks(causal)}
    bqkv = a["L2_attn_bqkv"]
    l2 = {"wq": a["L2_attn_Wq"].T, "wqkv": a["L2_attn_Wqkv"].T, "wop": pad(a["L2_attn_Wop"]), "w2c": col(a["L2_attn_W2"]),
          "b2": rows(a["L2_attn_b2"]), "bq": col(bqkv[:128]), "bk": col(bqkv[128:256]), "bv": col(bqkv[256:]),
          "w1": a["L2_ffn_w1_w"].T, "w2": a["L2_ffn_w2_w"].T, "h1": chunks(a["L2_ffn_h1_w"].T), "h2": chunks(a["L2_ffn_h2_w"].T),
          "w3": chunks(a["L2_ffn_w3_w"].T), "s1": cols(a["L2_ffn_w1_s"]), "s2": cols(a["L2_ffn_w2_s"]),
          "hs1": cols(a["L2_ffn_h1_s"]), "hs2": cols(a["L2_ffn_h2_s"]), "s3": rows(a["L2_ffn_w3_s"])}
    l3 = {"wv": a["L3_attn_Wv"], "wout": chunks(a["L3_attn_Wo"]), "kernel": a["L3_ffn_kernel"], "bias": rows(a["L3_ffn_bias"]),
          "bo": rows(a["L3_attn_bo"]), "aT": pad(a["L3_ffn_a"].T), "b": pad(a["L3_ffn_b"])}
    all_ = {"const": c, "l0": l0, "f0": f0, "l1": l1, "l2": l2, "l3": l3, "qk1": qk1, "qk3": qk3}
    got = {"x": a["L0_attn_x"]}
    for p, parts in PACKS.items():
        got[p] = np.ascontiguousarray(np.concatenate([np.asarray(all_[p][n], f) for n, _ in parts], axis=1))
        assert got[p].shape == (128, width(p)), p
    return got


def kernel(**inputs):
    import concourse.bacc as _bacc
    from concourse.bass_utils import run_bass_kernel_spmd as _run

    arrays = lay_out({k: np.asarray(v) for k, v in inputs.items()})
    nc = _bacc.Bacc("TRN2", target_bir_lowering=False, num_devices=1)
    ins = {n: nc.dram_tensor(f"in_{n}", v.shape, mybir.dt.float32, kind="ExternalInput").ap() for n, v in arrays.items()}
    out = nc.dram_tensor("out_x", (B, S, D), mybir.dt.float32, kind="ExternalOutput").ap()
    program(nc, ins, out)
    r = _run(nc, [{f"in_{n}": v for n, v in arrays.items()}], core_ids=[0])
    return r.results[0]["out_x"]
```
